# Optimizing a Trainium2 kernel written in Bass

```python
import numpy as np
import jax
import jax.numpy as jnp

def _softmax(x, axis=-1):
    return jax.nn.softmax(x, axis=axis)

def _gelu(x):
    return jax.nn.gelu(x, approximate=True)

def _silu(x):
    return jax.nn.silu(x)

def _sigmoid(x):
    return jax.nn.sigmoid(x)

def _layernorm(x, axis=-1, eps=1e-05):
    m = jnp.mean(x, axis=axis, keepdims=True)
    v = jnp.var(x, axis=axis, keepdims=True)
    return (x - m) / jnp.sqrt(v + eps)

def _scatter_add(tgt, idx, src, axis=0):
    return tgt.at[idx].add(src)

def _segment_sum(src, seg, n):
    return jax.ops.segment_sum(src, seg, n)
kernel_name = 'mk_gnn_preln_d4_gnn_r8_5cfd5c'

def setup_inputs(seed: int=0):
    np.random.seed(seed)
    _w = jnp.asarray

    def _rec_inputs():
        import jax
        import jax.numpy as jnp
        _gk = jax.random.key(seed)
        x = -0.0009044 + 1 * jax.random.normal(jax.random.fold_in(_gk, 1), (12500, 16), jnp.float32)
        src = jax.random.randint(jax.random.fold_in(_gk, 2), (400000,), 0, 12500, jnp.int32)
        dst = jnp.minimum((12500 * jax.random.uniform(jax.random.fold_in(_gk, 3), (400000,)) ** 2.0).astype(jnp.int32), 99999)
        _o = jnp.argsort(dst, stable=True)
        src = src[_o]
        dst = dst[_o]
        edge_attr_2 = 0.000411684 + 0.577418 * jax.random.normal(jax.random.fold_in(_gk, 11), (400000, 2), jnp.float32)
        edge_attr_8 = -0.00019784 + 0.999804 * jax.random.normal(jax.random.fold_in(_gk, 12), (400000, 8), jnp.float32)
        node_vec1 = -0.00472126 + 0.997171 * jax.random.normal(jax.random.fold_in(_gk, 15), (12500, 1), jnp.float32)
        return (x, src, dst, edge_attr_2, edge_attr_8, node_vec1)
    x, src, dst, edge_attr_2, edge_attr_8, node_vec1 = _rec_inputs()

    def _L0_gnn_setup():
        import jax, jax.numpy as jnp
        import numpy as np
        N_NODES = 12500
        N_EDGES = 200000
        F_IN = 16
        F_OUT = 16
        N_BASIS = 4

        def linear_basis(u, n):
            centers = jnp.linspace(-1.0, 1.0, n, dtype=u.dtype)
            dx = 2.0 / (n - 1)
            return jnp.maximum(0.0, 1.0 - jnp.abs(u[:, None] - centers[None, :]) / dx)
        key = jax.random.key(seed)
        k1, k2, k3, k4, k5 = jax.random.split(key, 5)
        x = jax.random.normal(k1, (N_NODES, F_IN), dtype=jnp.float32)
        edge_index = jax.random.randint(k2, (2, N_EDGES), 0, N_NODES, dtype=jnp.int64)
        edge_attr = jax.random.uniform(k3, (N_EDGES, 2), dtype=jnp.float32, minval=-1.0, maxval=1.0)
        weight = jax.random.uniform(k4, (N_BASIS, N_BASIS, F_IN, F_OUT), dtype=jnp.float32, minval=-0.05, maxval=0.05)
        return {'x': x, 'edge_index': edge_index, 'edge_attr': edge_attr, 'weight': weight}
    _L0_gnn_all = _L0_gnn_setup()
    _L0_gnn_in = {k: v for k, v in _L0_gnn_all.items() if k in ('weight',)}
    del _L0_gnn_all

    def _L1_gnn_setup():
        import jax, jax.numpy as jnp
        import numpy as np
        STALK_DIM = 16
        N_NODES = 6250
        N_EDGES = 50000
        HIDDEN = 64
        key = jax.random.key(seed)
        k1, k2, k3, k4 = jax.random.split(key, 4)
        d = STALK_DIM
        x = jax.random.normal(k1, (N_NODES, d), dtype=jnp.float32)
        edge_index = jax.random.randint(k2, (2, N_EDGES), 0, N_NODES, dtype=jnp.int64)
        W1 = jax.random.normal(k3, (HIDDEN, 2 * d), dtype=jnp.float32) * (1.0 / np.sqrt(2 * d))
        b1 = jnp.zeros((HIDDEN,), dtype=jnp.float32)
        W2 = jax.random.normal(k4, (d, HIDDEN), dtype=jnp.float32) * (1.0 / np.sqrt(HIDDEN))
        b2 = jnp.zeros((d,), dtype=jnp.float32)
        return {'x': x, 'edge_index': edge_index, 'W1': W1, 'b1': b1, 'W2': W2, 'b2': b2}
    _L1_gnn_all = _L1_gnn_setup()
    _L1_gnn_in = {k: v for k, v in _L1_gnn_all.items() if k in ('W1', 'b1', 'W2', 'b2')}
    del _L1_gnn_all

    def _L2_gnn_setup():
        import jax, jax.numpy as jnp
        import numpy as np
        N_NODES = 12500
        N_EDGES = 100000
        NFC = 16
        EFC = 8
        key = jax.random.key(seed)
        k1, k2, k3, k4 = jax.random.split(key, 4)
        node_features = jax.random.normal(k1, (N_NODES, NFC), dtype=jnp.float32)
        edge_features = jax.random.normal(k2, (N_EDGES, EFC), dtype=jnp.float32)
        pair_indices = jax.random.randint(k3, (N_EDGES, 2), 0, N_NODES, dtype=jnp.int32)
        kernel = jax.random.normal(k4, (EFC, NFC * NFC), dtype=jnp.float32) * (2.0 / (EFC + NFC * NFC)) ** 0.5
        bias = jnp.zeros((NFC * NFC,), dtype=jnp.float32)
        return {'node_features': node_features, 'edge_features': edge_features, 'pair_indices': pair_indices, 'kernel': kernel, 'bias': bias}
    _L2_gnn_all = _L2_gnn_setup()
    _L2_gnn_in = {k: v for k, v in _L2_gnn_all.items() if k in ('kernel', 'bias')}
    del _L2_gnn_all

    def _L3_gnn_setup():
        import jax, jax.numpy as jnp
        import numpy as np
        N_NODES = 12500
        N_EDGES = 400000
        D_NODE = 16
        D_EDGE = 8
        D_HIDDEN = 16
        key = jax.random.key(seed)
        ks = jax.random.split(key, 8)
        node_features = jax.random.normal(ks[0], (N_NODES, D_NODE), dtype=jnp.float32)
        edge_attr_e3nn = jax.random.normal(ks[1], (N_EDGES, D_EDGE), dtype=jnp.float32)
        node_attr_scalar_raw = jax.random.normal(ks[2], (N_NODES, 1), dtype=jnp.float32)
        W_msg_tp = jax.random.normal(ks[3], (D_NODE, D_EDGE, D_HIDDEN), dtype=jnp.float32)
        W_msg_lin = jax.random.normal(ks[4], (D_HIDDEN, D_HIDDEN), dtype=jnp.float32)
        W_upd_tp = jax.random.normal(ks[5], (D_NODE, D_HIDDEN, D_HIDDEN), dtype=jnp.float32)
        W_upd_lin = jax.random.normal(ks[6], (D_HIDDEN, D_NODE), dtype=jnp.float32)
        edge_index = jax.random.randint(ks[7], (2, N_EDGES), 0, N_NODES, dtype=jnp.int64)
        return {'node_features': node_features, 'edge_attr_e3nn': edge_attr_e3nn, 'node_attr_scalar_raw': node_attr_scalar_raw, 'W_msg_tp': W_msg_tp, 'W_msg_lin': W_msg_lin, 'W_upd_tp': W_upd_tp, 'W_upd_lin': W_upd_lin, 'edge_index': edge_index}
    _L3_gnn_all = _L3_gnn_setup()
    _L3_gnn_in = {k: v for k, v in _L3_gnn_all.items() if k in ('W_msg_tp', 'W_msg_lin', 'W_upd_tp', 'W_upd_lin')}
    del _L3_gnn_all
    return {'x': x, 'src': src, 'dst': dst, 'edge_attr_2': edge_attr_2, 'edge_attr_8': edge_attr_8, 'node_vec1': node_vec1, 'L0_gnn_weight': _L0_gnn_in['weight'], 'L1_gnn_W1': _L1_gnn_in['W1'], 'L1_gnn_b1': _L1_gnn_in['b1'], 'L1_gnn_W2': _L1_gnn_in['W2'], 'L1_gnn_b2': _L1_gnn_in['b2'], 'L2_gnn_kernel': _L2_gnn_in['kernel'], 'L2_gnn_bias': _L2_gnn_in['bias'], 'L3_gnn_W_msg_tp': _L3_gnn_in['W_msg_tp'], 'L3_gnn_W_msg_lin': _L3_gnn_in['W_msg_lin'], 'L3_gnn_W_upd_tp': _L3_gnn_in['W_upd_tp'], 'L3_gnn_W_upd_lin': _L3_gnn_in['W_upd_lin']}

def reference(x, src, dst, edge_attr_2, edge_attr_8, node_vec1, L0_gnn_weight, L1_gnn_W1, L1_gnn_b1, L1_gnn_W2, L1_gnn_b2, L2_gnn_kernel, L2_gnn_bias, L3_gnn_W_msg_tp, L3_gnn_W_msg_lin, L3_gnn_W_upd_tp, L3_gnn_W_upd_lin):
    import jax
    import jax.numpy as jnp

    def _L0_gnn_ref(x, edge_index, edge_attr, weight):
        import jax, jax.numpy as jnp
        import numpy as np
        N_NODES = 12500
        N_EDGES = 200000
        F_IN = 16
        F_OUT = 16
        N_BASIS = 4

        def linear_basis(u, n):
            centers = jnp.linspace(-1.0, 1.0, n, dtype=u.dtype)
            dx = 2.0 / (n - 1)
            return jnp.maximum(0.0, 1.0 - jnp.abs(u[:, None] - centers[None, :]) / dx)
        "BasisConvLayer forward, mode='conv', linear basis, no bias/activations.\n\n            For each edge e=(i<-j): msg_e = sum_{u,v} b_u(dx) b_v(dy) * (x_j @ W[u,v]);\n            out[i] = sum over incoming edges of msg_e.\n            "
        row, col = (edge_index[0], edge_index[1])
        x_j = x[col]
        bx = linear_basis(edge_attr[:, 0], N_BASIS)
        by = linear_basis(edge_attr[:, 1], N_BASIS)
        t = (bx[:, :, None] * by[:, None, :]).reshape(-1, N_BASIS * N_BASIS)
        w_flat = weight.reshape(N_BASIS * N_BASIS, F_IN, F_OUT)
        msg = jnp.zeros((x_j.shape[0], F_OUT), dtype=x.dtype)
        for k in range(N_BASIS * N_BASIS):
            msg = msg + t[:, k, None] * (x_j @ w_flat[k])
        out = jax.ops.segment_sum(msg, row, num_segments=N_NODES)
        return out

    def _L1_gnn_ref(x, edge_index, W1, b1, W2, b2):
        import jax, jax.numpy as jnp
        import numpy as np
        STALK_DIM = 16
        N_NODES = 6250
        N_EDGES = 50000
        HIDDEN = 64
        d = x.shape[1]
        n = x.shape[0]
        src, dst = (edge_index[0], edge_index[1])
        xs, xd = (x[src], x[dst])

        def reflection(a, b):
            h = jax.nn.relu(jnp.concatenate([a, b], axis=1) @ W1.T + b1)
            return h @ W2.T + b2

        def householder(v):
            vn = v / jnp.maximum(jnp.linalg.norm(v, axis=1, keepdims=True), 1e-12)
            return jnp.eye(d, dtype=v.dtype)[None] - 2.0 * vn[:, :, None] * vn[:, None, :]
        F_s = householder(reflection(xs, xd))
        F_d = householder(reflection(xd, xs))
        L_sd = -jnp.einsum('eki,ekj->eij', F_s, F_d)
        ones_e = jnp.ones(src.shape[0], dtype=x.dtype)
        deg = jnp.zeros(n, dtype=x.dtype).at[src].add(ones_e).at[dst].add(ones_e)
        deg_inv_sqrt = 1.0 / jnp.sqrt(jnp.maximum(deg, 1e-05))
        coef = deg_inv_sqrt[src] * deg_inv_sqrt[dst]
        msg_s = coef[:, None] * jnp.einsum('eij,ej->ei', L_sd, xd)
        msg_d = coef[:, None] * jnp.einsum('eji,ej->ei', L_sd, xs)
        out = x - jnp.zeros_like(x).at[src].add(msg_s) - jnp.zeros_like(x).at[dst].add(msg_d)
        return jax.nn.relu(out)

    def _L2_gnn_ref(node_features, edge_features, pair_indices, kernel, bias):
        import jax, jax.numpy as jnp
        import numpy as np
        N_NODES = 12500
        N_EDGES = 100000
        NFC = 16
        EFC = 8
        nfc = node_features.shape[-1]
        num_nodes = node_features.shape[0]
        edge_mats = (edge_features @ kernel + bias).reshape(-1, nfc, nfc)
        neighbors = node_features[pair_indices[:, 1]]
        transformed = jnp.einsum('eij,ej->ei', edge_mats, neighbors)
        aggregated = jax.ops.segment_sum(transformed, pair_indices[:, 0], num_segments=num_nodes)
        return aggregated

    def _L3_gnn_ref(node_features, edge_attr_e3nn, node_attr_scalar_raw, W_msg_tp, W_msg_lin, W_upd_tp, W_upd_lin, edge_index):
        import jax, jax.numpy as jnp
        import numpy as np
        N_NODES = 12500
        N_EDGES = 400000
        D_NODE = 16
        D_EDGE = 8
        D_HIDDEN = 16
        n_nodes = node_features.shape[0]
        row = edge_index[0]
        col = edge_index[1]
        norm_msg_tp = 1.0 / np.float32(np.sqrt(D_NODE * D_EDGE))
        norm_upd_tp = 1.0 / np.float32(np.sqrt(D_NODE * D_HIDDEN))
        norm_lin = 1.0 / np.float32(np.sqrt(D_HIDDEN))
        x_j = node_features[col]
        m = jnp.einsum('ei,ej,ijh->eh', x_j, edge_attr_e3nn, W_msg_tp) * norm_msg_tp
        m = jax.nn.silu(m)
        m = m @ W_msg_lin * norm_lin
        agg = jax.ops.segment_sum(m, row, num_segments=n_nodes)
        u = jnp.einsum('ni,nh,ihk->nk', node_features, agg, W_upd_tp) * norm_upd_tp
        u = jax.nn.silu(u)
        u = u @ W_upd_lin * norm_lin
        return node_features + u
    edge_index = jnp.stack([src, dst])
    edge_index_t = jnp.stack([src, dst], axis=1)
    h = jnp.maximum(_layernorm(x, axis=-1), 0.0)
    x = x + _L0_gnn_ref(h, edge_index, edge_attr_2, L0_gnn_weight)
    h = jnp.maximum(_layernorm(x, axis=-1), 0.0)
    x = x + _L1_gnn_ref(h, edge_index, L1_gnn_W1, L1_gnn_b1, L1_gnn_W2, L1_gnn_b2)
    h = jnp.maximum(_layernorm(x, axis=-1), 0.0)
    x = x + _L2_gnn_ref(h, edge_attr_8, edge_index_t, L2_gnn_kernel, L2_gnn_bias)
    h = jnp.maximum(_layernorm(x, axis=-1), 0.0)
    x = x + _L3_gnn_ref(h, edge_attr_8, node_vec1, L3_gnn_W_msg_tp, L3_gnn_W_msg_lin, L3_gnn_W_upd_tp, L3_gnn_W_upd_lin, edge_index)
    return x

_drawn_inputs = setup_inputs


def setup_inputs(seed=0):
    import zlib

    import numpy as np

    out = dict(_drawn_inputs(seed))
    spreads = {'L1_gnn_b1': (0.0, 0.1), 'L1_gnn_b2': (0.0, 0.1), 'L2_gnn_bias': (0.0, 0.1)}
    factors = {}
    for name, (base, spread) in spreads.items():
        noise = np.random.default_rng([zlib.crc32(name.encode()), seed]).standard_normal(out[name].shape)
        drawn = base * np.exp(spread * noise) if base else spread * noise
        out[name] = jnp.asarray(drawn.astype(out[name].dtype))
    for name, factor in factors.items():
        out[name] = (out[name] * factor).astype(out[name].dtype)
    return out
```

```python
import concourse.bass as bass
from concourse import mybir
from contextlib import ExitStack

FP = mybir.dt.float32
BF = mybir.dt.bfloat16
I32 = mybir.dt.int32
ALU = mybir.AluOpType
ACT = mybir.ActivationFunctionType
AX = mybir.AxisListType

P = 128
F = 16
GT = 104
CT = 4
HT = GT // 2
QN = GT // CT
HQ = QN // 2
PW = 16
DW = 20
KT = 25
KS = 5
MAGIC = 12582912.0
ONE = 1
OUTSIDE = 1 << 20

W_SLO, W_DLO, W_DST, W_DROW, W_SRC, W_DHI, W_A2, W_A8 = 0, 1, 2, 3, 4, 5, 6, 8


class Shapes:
    def __init__(self, n_nodes, n_edges):
        self.n = n_nodes
        self.e = n_edges
        self.nb = -(-n_nodes // P)
        self.npad = self.nb * P
        self.last = n_nodes - (self.nb - 1) * P
        self.j = n_edges // P
        self.g = -(-(self.j + self.nb) // GT)
        self.t = self.g * GT
        assert n_edges % P == 0 and self.j % (KT * KS) == 0 and self.nb <= P


def counter(eng, sem, base=0):
    n = [0]

    def step(ins):
        n[0] += 1
        ins.then_inc(sem, 1)
        eng.wait_ge(sem, base + n[0])
        return n[0]

    step.count = n
    return step


def start_at_one(eng, *sems):
    for s in sems:
        eng.sem_inc(s, ONE)


def bc(ap, axis, shape):
    return ap.unsqueeze(axis).to_broadcast(shape)


def setup_phase(nc, sh, io, dr, cst):
    J, NB, G = sh.j, sh.nb, sh.g
    n_it = J // (KT * KS)
    src_v = io["src"].rearrange("(p j) -> p j", p=P)
    dst_v = io["dst"].rearrange("(p j) -> p j", p=P)
    a2_v = io["edge_attr_2"].rearrange("(p j) c -> p (j c)", p=P)
    a8_v = io["edge_attr_8"].rearrange("(p j) c -> p (j c)", p=P)
    with nc.cleanup_on_exit(), ExitStack() as ctx:
        def sb(name, shape, dt):
            return ctx.enter_context(nc.sbuf_tensor(name, shape, dt))

        def sem(name):
            return nc.alloc_semaphore("su_" + name)

        key = [sb("key_src", [P, J], I32), sb("key_dst", [P, J], I32)]
        blk = [sb("blk_src", [P, J], FP), sb("blk_dst", [P, J], FP)]
        low = [sb("low_src", [P, J], FP), sb("low_dst", [P, J], FP)]
        pos = [sb("pos_src", [P, J], FP), sb("pos_dst", [P, J], FP)]
        mask = sb("mask", [P, J], FP)
        scan = sb("scan", [P, J], FP)
        row = [mask[:, :].bitcast(I32), scan[:, :].bitcast(I32)]
        cnt = sb("cnt", [P, 2 * NB], FP)
        tiles = sb("tiles", [P, 2 * NB], FP)
        base = sb("base", [P, 2 * NB], FP)
        before = sb("before", [P, 2, P + 1], FP)
        tri = sb("tri", [P, P], FP)
        ones = sb("ones", [P, P], FP)
        tno = sb("tile_no", [P, G], FP)
        fs = sb("fill_src", [P, GT * PW], FP)
        fd = sb("fill_dst", [P, HT * DW], FP)
        a2 = sb("a2_in", [P, KS, KT * 2], FP)
        a8 = sb("a8_in", [P, KS, KT * 8], FP)
        rows = sb("rows", [P, KS, KT, PW], FP)
        idx = sb("row_idx", [P, KS, KT], I32)
        ps_tot = ctx.enter_context(nc.psum_tensor("ps_tot", [P, 512], FP))
        ps_pre = ctx.enter_context(nc.psum_tensor("ps_pre", [P, 512], FP))

        s_key = [sem("key_src"), sem("key_dst")]
        s_fillc = sem("fill_const")
        s_filled = sem("filled")
        s_const = sem("const")
        s_sum = sem("sums")
        s_dve = sem("dve_chain")
        s_cl = sem("count_loop")
        s_rl = [sem("rank_loop_src"), sem("rank_loop_dst")]
        s_scan = [sem("scanned_src"), sem("scanned_dst")]
        s_begun, s_begun_d = sem("begun_pool"), sem("begun_dve")
        s_attr = [sem(f"attr{s}") for s in range(KS)]
        s_put = [sem(f"words_dve{s}") for s in range(KS)]
        s_puta = [sem(f"words_act{s}") for s in range(KS)]
        s_sent = [sem(f"rows_sent{s}") for s in range(KS)]
        s_free = [sem(f"rows_free{s}") for s in range(KS)]

        with nc.Block() as block:
            @block.sync
            def _(sp):
                sp.dma_start(key[0][:, :], src_v).then_inc(s_key[0], 16)
                sp.dma_start(key[1][:, :], dst_v).then_inc(s_key[1], 16)
                sp.wait_ge(s_fillc, 4)
                sp.dma_start(dr["S"].rearrange("(p g r) w -> p g (r w)", p=P, r=GT),
                             fs[:, :].unsqueeze(1).to_broadcast([P, G + 1, GT * PW])).then_inc(s_filled, 16)
                sp.dma_start(dr["D"].rearrange("(p g r) w -> p g (r w)", p=P, r=HT),
                             fd[:, :].unsqueeze(1).to_broadcast([P, 2 * (G + 1), HT * DW])).then_inc(s_filled, 16)
                with sp.Fori(0, n_it) as i:
                    for s in range(KS):
                        sp.wait_ge(s_puta[s], i * 2 + ONE)
                        at = i * (KS * KT) + s * KT
                        sp.dma_start(a2[:, s, :], a2_v[:, bass.ds(at * 2, KT * 2)]).then_inc(s_attr[s], 16)
                        sp.dma_start(a8[:, s, :], a8_v[:, bass.ds(at * 8, KT * 8)]).then_inc(s_attr[s], 16)

            @block.gpsimd
            def _(gp):
                gp.memset(fs[:, :], 0.0).then_inc(s_fillc, 1)
                gp.memset(fd[:, :], 0.0).then_inc(s_fillc, 1)
                gp.wait_ge(s_fillc, 2)
                fs_w = fs[:, :].rearrange("p (r w) -> p r w", w=PW)
                gp.memset(fs_w[:, :, W_SLO:W_DLO + 1], -1.0)
                gp.memset(fs_w.bitcast(I32)[:, :, W_DROW:W_DROW + 1], OUTSIDE).then_inc(s_fillc, 1)
                gp.memset(fd[:, :].rearrange("p (r w) -> p r w", w=DW)[:, :, F:F + 1], -1.0).then_inc(s_fillc, 1)
                gp.iota(cst["iota"][:, :], pattern=[[1, P]], base=0, channel_multiplier=0,
                        allow_small_or_imprecise_dtypes=True)
                gp.iota(tno[:, :], pattern=[[GT, G]], base=0, channel_multiplier=1,
                        allow_small_or_imprecise_dtypes=True)
                gp.memset(ones[:, :], 1.0)
                gp.memset(cst["ident"][:, :], 0.0)
                gp.memset(before[:, :, :], 0.0).then_inc(s_const, 1)
                gp.wait_ge(s_const, 1)
                gp.affine_select(out=cst["ident"][:, :], in_=cst["ident"][:, :], compare_op=ALU.not_equal, fill=1.0,
                                 base=0, pattern=[[-1, P]], channel_multiplier=1)
                gp.affine_select(out=tri[:, :], in_=ones[:, :], compare_op=ALU.is_gt, fill=0.0,
                                 base=0, pattern=[[1, P]], channel_multiplier=-1).then_inc(s_const, 1)
                gp.wait_ge(s_filled, 32)
                start_at_one(gp, *s_free)
                with gp.Fori(0, n_it) as i:
                    for s in range(KS):
                        gp.wait_ge(s_put[s], i + 1)
                        gp.wait_ge(s_puta[s], i * 2 + 2 + ONE)
                        gp.sem_inc(s_begun, 1)
                        for k in range(KT):
                            gp.indirect_dma_start(
                                out=dr["S"], out_offset=bass.IndirectOffsetOnAxis(ap=idx[:, s, k:k + 1], axis=0),
                                in_=rows[:, s, k, :], in_offset=None).then_inc(s_sent[s], 16)
                        for done in ([s - 1] if s else []) + ([s] if s == KS - 1 else []):
                            gp.wait_ge(s_sent[done], (i + 1) * (16 * KT))
                            gp.sem_inc(s_free[done], 1)

            @block.tensor
            def _(pe):
                pe.wait_ge(s_const, 2)
                pe.wait_ge(s_cl, 2 * NB)
                nc.tensor.matmul(ps_tot[:, 0:2 * NB], ones[:, :], cnt[:, :], start=True, stop=True)
                nc.tensor.matmul(ps_pre[:, 0:2 * NB], tri[:, :], cnt[:, :], start=True, stop=True).then_inc(s_sum, 1)

            @block.scalar
            def _(act):
                start_at_one(act, *s_puta)
                with act.Fori(0, n_it) as i:
                    for s in range(KS):
                        act.wait_ge(s_attr[s], i * 32 + 32)
                        act.wait_ge(s_free[s], i + ONE)
                        act.activation(rows[:, s, :, W_A2:W_A2 + 2],
                                       a2[:, s, :].rearrange("p (k c) -> p k c", c=2), ACT.Copy).then_inc(s_puta[s], 1)
                        act.activation(rows[:, s, :, W_A8:W_A8 + 8],
                                       a8[:, s, :].rearrange("p (k c) -> p k c", c=8), ACT.Copy).then_inc(s_puta[s], 1)

            @block.vector
            def _(dve):
                step = counter(dve, s_dve)
                tmp = mask[:, :].bitcast(I32)
                for o in range(2):
                    dve.wait_ge(s_key[o], 16)
                    step(nc.vector.tensor_scalar(tmp, key[o][:, :], 7, None, ALU.arith_shift_right))
                    step(nc.vector.tensor_copy(blk[o][:, :], tmp))
                    step(nc.vector.tensor_scalar(tmp, key[o][:, :], P - 1, None, ALU.bitwise_and))
                    step(nc.vector.tensor_copy(low[o][:, :], tmp))
                dve.wait_ge(s_const, 2)
                with dve.Fori(0, NB) as b:
                    loop = counter(dve, s_cl, b * 2)
                    for o in range(2):
                        loop(nc.vector.tensor_scalar(mask[:, :], blk[o][:, :], cst["iota"][:, bass.ds(b, 1)], 0.0,
                                                     ALU.is_equal, ALU.add,
                                                     accum_out=cnt[:, bass.ds(b + o * NB, 1)]))
                dve.wait_ge(s_sum, 1)
                step(nc.vector.tensor_scalar(tiles[:, :], ps_tot[:, 0:2 * NB], (P - 1) / 2, 1.0 / P, ALU.add, ALU.mult))
                step(nc.vector.tensor_scalar(tiles[:, :], tiles[:, :], MAGIC, -MAGIC, ALU.add, ALU.add))
                for o in range(2):
                    part = tiles[:, o * NB:(o + 1) * NB]
                    step(nc.vector.tensor_tensor_scan(before[:, o, 1:NB + 1], part, part, 0.0, ALU.add, ALU.max))
                    step(nc.vector.scalar_tensor_tensor(out=base[:, o * NB:(o + 1) * NB], in0=before[:, o, 0:NB],
                                                        scalar=float(P), in1=ps_pre[:, o * NB:(o + 1) * NB],
                                                        op0=ALU.mult, op1=ALU.add))
                for o in range(2):
                    step(nc.vector.memset(pos[o][:, :], 0.0))
                    with dve.Fori(0, NB) as b:
                        loop = counter(dve, s_rl[o], b * 2)
                        loop(nc.vector.tensor_scalar(mask[:, :], blk[o][:, :], cst["iota"][:, bass.ds(b, 1)], None,
                                                     ALU.is_equal))
                        nc.vector.tensor_tensor_scan(scan[:, :], mask[:, :], mask[:, :],
                                                     base[:, bass.ds(b + o * NB, 1)], ALU.add, ALU.max
                                                     ).then_inc(s_scan[o], 1)
                        dve.wait_ge(s_scan[o], b + 1)
                        dve.sem_inc(s_begun_d, 1)
                        loop(nc.vector.copy_predicated(pos[o][:, :], mask[:, :].bitcast(I32), scan[:, :]))
                t = blk[0][:, :]
                for o in range(2):
                    step(nc.vector.tensor_scalar(t, pos[o][:, :], -(P + 1) / 2, 1.0 / P, ALU.add, ALU.mult))
                    step(nc.vector.tensor_scalar(t, t, MAGIC, -MAGIC, ALU.add, ALU.add))
                    step(nc.vector.scalar_tensor_tensor(out=pos[o][:, :], in0=t, scalar=-float(P), in1=pos[o][:, :],
                                                        op0=ALU.mult, op1=ALU.add))
                    step(nc.vector.scalar_tensor_tensor(out=pos[o][:, :], in0=pos[o][:, :], scalar=float(GT), in1=t,
                                                        op0=ALU.mult, op1=ALU.add))
                    step(nc.vector.tensor_scalar(t, t, -(GT - 1) / 2, 1.0 / GT, ALU.add, ALU.mult))
                    step(nc.vector.tensor_scalar(t, t, MAGIC, -MAGIC, ALU.add, ALU.add))
                    step(nc.vector.scalar_tensor_tensor(out=pos[o][:, :], in0=t, scalar=float((P - 1) * GT),
                                                        in1=pos[o][:, :], op0=ALU.mult, op1=ALU.add))
                    step(nc.vector.tensor_scalar(row[o], pos[o][:, :], -float(GT), None, ALU.add))
                for o, name in enumerate(("own_src", "own_dst")):
                    own = cst[name][0:GT, :].rearrange("p (g b) -> p g b", b=NB)
                    tn = tno[0:GT, :].unsqueeze(2).to_broadcast([GT, G, NB])
                    sh3 = [GT, G, NB]
                    past = pos[0][0:GT, 0:G * NB].rearrange("p (g b) -> p g b", b=NB)
                    step(nc.vector.tensor_tensor(own, tn, bc(before[0:GT, o, 0:NB], 1, sh3), ALU.is_ge))
                    step(nc.vector.tensor_tensor(past, tn, bc(before[0:GT, o, 1:NB + 1], 1, sh3), ALU.is_ge))
                    step(nc.vector.tensor_tensor(own, own, past, ALU.subtract))
                with dve.Fori(0, n_it) as i:
                    for s in range(KS):
                        dve.wait_ge(s_free[s], i + ONE)
                        at = i * (KS * KT) + s * KT
                        r = rows[:, s, :, :]
                        ri = r.bitcast(I32)

                        def col(x):
                            return x[:, bass.ds(at, KT)].unsqueeze(2)
                        nc.vector.tensor_copy(r[:, :, W_SLO:W_SLO + 1], col(low[0][:, :]))
                        nc.vector.tensor_copy(r[:, :, W_DLO:W_DLO + 1], col(low[1][:, :]))
                        nc.vector.tensor_copy(ri[:, :, W_DST:W_DST + 1], col(key[1][:, :]))
                        nc.vector.tensor_copy(ri[:, :, W_DROW:W_DROW + 1], col(row[1]))
                        nc.vector.tensor_copy(ri[:, :, W_SRC:W_SRC + 1], col(key[0][:, :]))
                        nc.vector.tensor_copy(r[:, :, W_DHI:W_DHI + 1], col(blk[1][:, :]))
                        nc.vector.tensor_copy(idx[:, s, :], row[0][:, bass.ds(at, KT)]).then_inc(s_put[s], 1)


def norm_phase(nc, sh, tag, x, h, io=None, tail=None):
    NB = sh.nb
    with nc.cleanup_on_exit(), ExitStack() as ctx:
        xc = ctx.enter_context(nc.sbuf_tensor("xc" + tag, [P, P * F], FP))
        sq = ctx.enter_context(nc.sbuf_tensor("sq" + tag, [P, P * F], FP))
        st = ctx.enter_context(nc.sbuf_tensor("st" + tag, [P, 4, P], FP))
        s_x = nc.alloc_semaphore("nx" + tag)
        s_c = nc.alloc_semaphore("nc" + tag)
        s_v = nc.alloc_semaphore("nv" + tag)
        s_r = nc.alloc_semaphore("nr" + tag)
        s_z = nc.alloc_semaphore("nz" + tag)
        x3, c3, q3, h3 = (v[0:NB, :].rearrange("p (l f) -> p l f", f=F) for v in (x, xc, sq, h))
        with nc.Block() as block:
            if io is not None:
                @block.gpsimd
                def _(gp):
                    gp.memset(x[:, :], 0.0).then_inc(s_z, 1)

                @block.sync
                def _(sp):
                    sp.wait_ge(s_z, 1)
                    full = sh.nb - 1
                    sp.dma_start(x[0:full, :], io["x"][0:full * P, :].rearrange("(b l) f -> b (l f)", l=P)).then_inc(s_x, 16)
                    sp.dma_start(x[full:NB, 0:sh.last * F],
                                 io["x"][full * P:sh.n, :].rearrange("(b l) f -> b (l f)", b=1)).then_inc(s_x, 16)

            @block.vector
            def _(dve):
                if io is not None:
                    dve.wait_ge(s_x, 32)
                step = counter(dve, s_c)
                full = [NB, P, F]
                step(nc.vector.tensor_reduce(st[0:NB, 0, :], x3, AX.X, ALU.add))
                step(nc.vector.tensor_scalar(st[0:NB, 0, :], st[0:NB, 0, :], 1.0 / F, None, ALU.mult))
                step(nc.vector.tensor_tensor(c3, x3, bc(st[0:NB, 0, :], 2, full), ALU.subtract))
                step(nc.vector.tensor_tensor(q3, c3, c3, ALU.mult))
                step(nc.vector.tensor_reduce(st[0:NB, 1, :], q3, AX.X, ALU.add))
                nc.vector.tensor_scalar(st[0:NB, 1, :], st[0:NB, 1, :], 1.0 / F, 1e-5, ALU.mult, ALU.add).then_inc(s_v, 1)
                dve.wait_ge(s_r, 1)
                step(nc.vector.reciprocal(st[0:NB, 3, :], st[0:NB, 2, :]))
                step(nc.vector.tensor_tensor(c3, c3, bc(st[0:NB, 3, :], 2, full), ALU.mult))
                step(nc.vector.tensor_scalar(h3, c3, 0.0, None, ALU.max))

            @block.scalar
            def _(act):
                act.wait_ge(s_v, 1)
                act.activation(st[0:NB, 2, :], st[0:NB, 1, :], ACT.Sqrt).then_inc(s_r, 1)


def node_matmul(nc, sh, tag, src, weights, C, cst, mode, out, extra=None):
    NB = sh.nb
    L = 8
    n_pc = 1 if C * L <= 512 else 4
    lp = L // n_pc
    wid = lp * C
    CW = out.shape[1] if mode == "table" else C
    with nc.cleanup_on_exit(), ExitStack() as ctx:
        def sb(name, shape, dt=FP):
            return ctx.enter_context(nc.sbuf_tensor(name + tag, shape, dt))

        def sem(name):
            return nc.alloc_semaphore(f"nm_{name}{tag}")
        wbd = sb("wbd", [P, L * C])
        hs = sb("hs", [P, 2, P])
        hT = sb("hT", [P, 2, P])
        stage = sb("stage", [P, 2, L, CW])
        tp = [ctx.enter_context(nc.psum_tensor(f"tp{q}{tag}", [P, 512], FP)) for q in range(2)]
        pp = [ctx.enter_context(nc.psum_tensor(f"pp{k}{tag}", [P, 512], FP)) for k in range(n_pc)]
        s_z, s_w = sem("zero"), sem("weights")
        s_hs, s_tp, s_hT = ([sem(f"{n}{q}") for q in range(2)] for n in ("slice", "transposed", "features_first"))
        s_pp, s_begun = sem("product"), sem("begun")
        s_out = [sem(f"out{k}") for k in range(n_pc)]
        s_st = [sem(f"stored{q}") for q in range(2)]
        s_ch, s_pad, s_ex = sem("chain"), sem("pad"), sem("extra_cols")
        on_act = mode == "table" and extra is None

        with nc.Block() as block:
            @block.gpsimd
            def _(gp):
                gp.memset(wbd[:, :], 0.0).then_inc(s_z, 1)
                gp.memset(stage[:, :, :, :], 0.0).then_inc(s_pad, 1)

            @block.sync
            def _(sp):
                sp.wait_ge(s_z, 1)
                for k in range(L):
                    at = 0
                    for w in weights:
                        c = w.shape[1]
                        sp.dma_start(wbd[F * k:F * k + F, k * C + at:k * C + at + c], w).then_inc(s_w, 16)
                        at += c
                if mode == "table":
                    start_at_one(sp, *s_st)
                    y = out.rearrange("(b l) c -> b (l c)", l=P)
                    with sp.Fori(0, P // L // 2) as i:
                        for q in range(2):
                            for k in range(n_pc):
                                sp.wait_ge(s_out[k], i * 2 + (q + 1) + ONE)
                            sp.sem_inc(s_begun, 1)
                            if extra is not None:
                                sp.wait_ge(s_ex, i * 4 + (2 * q + 2))
                            sp.dma_start(y[:, bass.ds((i * 2 + q) * (L * CW), L * CW)],
                                         stage[0:NB, q, :, :].rearrange("p l c -> p (l c)")).then_inc(s_st[q], 16)
                    for q in range(2):
                        sp.wait_ge(s_st[q], 16 * (P // L // 2) + ONE)

            @block.tensor
            def _(pe):
                pe.wait_ge(s_w, 16 * L * len(weights))
                start_at_one(pe, *s_tp)
                with pe.Fori(0, P // L // 2) as i:
                    for q in range(2):
                        pe.wait_ge(s_hs[q], i + 1)
                        nc.tensor.transpose(tp[q][:, 0:NB], hs[0:NB, q, :], cst["ident"][0:NB, 0:NB]).then_inc(s_tp[q], 1)
                        pe.wait_ge(s_hT[q], i + 1)
                        for k in range(n_pc):
                            pe.wait_ge(s_out[k], i * 2 + q + ONE)
                            nc.tensor.matmul(pp[k][0:NB, 0:wid], hT[:, q, 0:NB], wbd[:, k * wid:(k + 1) * wid],
                                             start=True, stop=True).then_inc(s_pp, 1)

            @block.scalar
            def _(act):
                if on_act:
                    act.wait_ge(s_pad, 1)
                    start_at_one(act, *s_out[0::2])
                with act.Fori(0, P // L // 2) as i:
                    for q in range(2):
                        act.wait_ge(s_tp[q], i + ONE)
                        act.activation(hs[0:NB, q, :], src[0:NB, bass.ds((i * 2 + q) * (L * F), L * F)],
                                       ACT.Copy).then_inc(s_hs[q], 1)
                        act.wait_ge(s_tp[q], i + 1 + ONE)
                        act.activation(hT[:, q, 0:NB], tp[q][:, 0:NB], ACT.Copy).then_inc(s_hT[q], 1)
                        if on_act:
                            act.wait_ge(s_st[q], i * 16 + ONE)
                            for k in range(0, n_pc, 2):
                                act.wait_ge(s_pp, (i * 2 + q) * n_pc + (k + 1))
                                act.activation(stage[0:NB, q, k * lp:(k + 1) * lp, 0:C],
                                               pp[k][0:NB, 0:wid].rearrange("p (l c) -> p l c", c=C),
                                               ACT.Copy).then_inc(s_out[k], 1)

            @block.vector
            def _(dve):
                dve.wait_ge(s_pad, 1)
                start_at_one(dve, *s_out[1::2], *([] if on_act else s_out[0::2]))
                with dve.Fori(0, P // L // 2) as i:
                    for q in range(2):
                        n = i * 2 + q
                        if mode == "table":
                            dve.wait_ge(s_st[q], i * 16 + ONE)
                        for k in range(1 if on_act else 0, n_pc, 2 if on_act else 1):
                            dve.wait_ge(s_pp, n * n_pc + (k + 1))
                            prod = pp[k][0:NB, 0:wid].rearrange("p (l c) -> p l c", c=C)
                            lo = n * L + k * lp
                            part = (slice(0, NB), q, slice(k * lp, (k + 1) * lp))
                            if mode == "table" and extra is None:
                                nc.vector.tensor_copy(stage[0:NB, q, k * lp:(k + 1) * lp, 0:C], prod).then_inc(s_out[k], 1)
                            elif mode == "table":
                                nc.vector.tensor_tensor(stage[0:NB, q, k * lp:(k + 1) * lp, 0:C], prod,
                                                        bc(extra["bias"][0:NB, :], 1, [NB, lp, C]), ALU.add).then_inc(s_out[k], 1)
                            elif mode == "copy":
                                nc.vector.tensor_scalar(out[0:NB, bass.ds(lo * F, lp * F)], pp[k][0:NB, 0:wid], extra, None,
                                                        ALU.mult).then_inc(s_out[k], 1)
                            elif mode == "final":
                                nc.vector.scalar_tensor_tensor(out=out[0:NB, bass.ds(lo * F, lp * F)], in0=pp[k][0:NB, 0:wid],
                                                               scalar=extra, in1=out[0:NB, bass.ds(lo * F, lp * F)],
                                                               op0=ALU.mult, op1=ALU.add).then_inc(s_out[k], 1)
                            else:
                                ag = extra[0:NB, bass.ds(lo * F, lp * F)].rearrange("p (l c) -> p l c", c=F)
                                st4 = stage[0:NB, q, k * lp:(k + 1) * lp, :].rearrange("p l (c o) -> p l c o", o=F)
                                nc.vector.tensor_tensor(st4, pp[k][0:NB, 0:wid].rearrange("p (l c o) -> p l c o", c=F, o=F),
                                                        bc(ag, 3, [NB, lp, F, F]), ALU.mult).then_inc(s_ch, 1)
                                dve.wait_ge(s_ch, n * n_pc + (k + 1))
                                nc.vector.tensor_reduce(
                                    out[0:NB, bass.ds(lo * F, lp * F)].rearrange("p (l c) -> p l c", c=F),
                                    stage[0:NB, q, k * lp:(k + 1) * lp, :].rearrange("p l (c o) -> p l o c", o=F),
                                    AX.X, ALU.add).then_inc(s_out[k], 1)
                        if mode == "table" and extra is not None:
                            nc.vector.tensor_copy(stage[0:NB, q, :, C:C + F],
                                                  src[0:NB, bass.ds(n * (L * F), L * F)].rearrange("p (l f) -> p l f", f=F)
                                                  ).then_inc(s_ex, 1)
                            nc.vector.tensor_copy(stage[0:NB, q, :, C + F:C + F + 1],
                                                  extra["dinv"][0:NB, bass.ds(n * L, L)].unsqueeze(2)).then_inc(s_ex, 1)


def edge_phase(nc, sh, layer, io, dr, cst, table, hist=None):
    G, NB = sh.g, sh.nb
    C = table.shape[1]
    M = F + 1 if layer == 0 else F
    tag = f"_L{layer}"
    sides = 2 if layer == 1 else 1
    with nc.cleanup_on_exit(), ExitStack() as ctx:
        def sb(name, shape, dt=FP):
            return ctx.enter_context(nc.sbuf_tensor(name + tag, shape, dt))

        def pb(name):
            return ctx.enter_context(nc.psum_tensor(name + tag, [P, 512], FP))

        def sem(name):
            return nc.alloc_semaphore(f"{name}{tag}")

        def two(name):
            return [sem(f"{name}{s}") for s in range(2)]
        pay = sb("pay", [P, 2, HT, PW])
        payi = pay[:, :, :, :].bitcast(I32)
        rows = sb("rows", [P, sides, 2, CT, C])
        msg = sb("msg", [P, 2, CT, M])
        hot = sb("hot", [P, 2, CT, P])
        stg = sb("stg", [F + 1, 2, CT * P])
        ps = [pb(f"ps{s}") for s in range(2)]
        s_pay, s_gat, s_hot, s_msg, s_taken, s_sc, s_ev, s_st = (
            two(n) for n in ("payload", "gathered", "onehot", "message", "rows_used", "scattered", "evacuated", "stored"))
        s_ch = sem("chain")
        s_one = sem("ones")
        s_basis_ch = sem("basis_chain")
        if layer == 0:
            hat = sb("hat", [P, HT, 2, 4])
            basis = sb("basis", [P, 2, HT, F])
            cen = sb("centers", [P, 4])
            prod = sb("prod", [P, CT, 256])
            hlo = sb("hlo", [P, 2, CT, P], BF)
            hhi = sb("hhi", [P, 2, CT, NB], BF)
            zb = sb("zeros_bf", [P, P], BF)
            ps_h = pb("ps_hist")
            s_hh = two("hist_onehot")
            s_hd = two("hist_done")
            s_hf = sem("hist_final")
        if layer in (2, 3):
            prod = sb("prod", [P, CT, 128])
            pre = sb("pre", [P, 2, CT, F])
            s_pre = two("presilu")
        if layer == 1:
            hid = sb("hid", [P, 2, CT, P])
            hidT = sb("hidT", [P, 2, CT * P])
            w2 = sb("w2", [P, 2 * F])
            b2 = sb("b2", [P, 2, F])
            v = sb("v", [P, CT, 2, F])
            tv = sb("tv", [P, CT, 2, F])
            cur = sb("cur", [P, CT, 2, F])
            sc = sb("sc", [P, 3, CT * 2])
            dst = sb("dmsg", [P, 2, CT, DW])
            ps_t = [pb(f"ps_t{s}") for s in range(2)]
            ps_v = [pb(f"ps_v{s}") for s in range(2)]
            s_w2, s_w2z, s_dz = sem("w2"), sem("w2_zero"), sem("dmsg_zero")
            s_hid, s_tr, s_hT, s_v, s_dm, s_dsent, s_dfree, s_vread = (two(n) for n in ("hidden", "transposed", "hidden_T", "vectors", "dst_message", "dst_sent", "dst_free", "vectors_read"))

        s_taken = {0: s_taken, 1: s_taken, 2: s_msg, 3: s_pre if layer == 3 else None}[layer]
        s_begun = sem("begun")

        def half(i, hf):
            return dr["S"][bass.ds(i * (GT * P), GT * P), :].rearrange("(p t) w -> p t w", t=GT)[:, hf * HT:(hf + 1) * HT, :]

        with nc.Block() as block:
            @block.scalar
            def _(act):
                for hf in range(2):
                    act.dma_start(pay[:, hf, :, :], half(0, hf)).then_inc(s_pay[hf], 16)
                start_at_one(act, *s_ev)
                if layer == 1:
                    start_at_one(act, *s_hT)
                if layer == 3:
                    start_at_one(act, *s_msg)
                with act.Fori(0, G) as i:
                    for q in range(QN):
                        s, m = q % 2, q // 2
                        if layer == 1:
                            act.wait_ge(s_tr[s], i * HQ + (m + 1))
                            act.activation(hidT[:, s, :], ps_t[s][:, :], ACT.Relu).then_inc(s_hT[s], 1)
                        if layer == 3:
                            act.wait_ge(s_pre[s], i * HQ + (m + 1) + ONE)
                            act.wait_ge(s_sc[s], i * HQ + m + ONE)
                            act.activation(msg[:, s, :, :], pre[:, s, :, :], ACT.Silu,
                                           scale=float(1.0 / (F * 8) ** 0.5)).then_inc(s_msg[s], 1)
                        act.wait_ge(s_sc[s], i * HQ + (m + 1) + ONE)
                        act.wait_ge(s_st[s], (i * HQ + m) * 16 + ONE)
                        act.activation(stg[0:M, s, :], ps[s][0:M, :], ACT.Copy).then_inc(s_ev[s], 1)
                        if q in (HQ, QN - 1):
                            hf = 0 if q == HQ else 1
                            lq = (HQ if hf == 0 else QN) - 1
                            if layer == 1:
                                act.wait_ge(s_dsent[lq % 2], (i * HQ + (lq // 2 + 1)) * (16 * CT))
                            if layer == 0:
                                act.wait_ge(s_hh[lq % 2], (i * HQ + (lq // 2 + 1)) * 2)
                            act.dma_start(pay[:, hf, :, :], half(i + 1, hf)).then_inc(s_pay[hf], 16)
                for hf in range(2):
                    act.wait_ge(s_pay[hf], 16 * (G + 1))

            @block.gpsimd
            def _(gp):
                def gather(i, q):
                    s, m = q % 2, q // 2
                    if q == 0 or q == HQ:
                        gp.wait_ge(s_pay[q // HQ], i * 16 + 16)
                    gp.wait_ge(s_taken[s], i * HQ + m + ONE)
                    gp.sem_inc(s_begun, 1)
                    hf, t0 = q // HQ, (q % HQ) * CT
                    for k in range(CT):
                        for side, word in enumerate((W_DST, W_SRC)[:sides]):
                            gp.indirect_dma_start(
                                out=rows[:, side, s, k, :], out_offset=None, in_=table,
                                in_offset=bass.IndirectOffsetOnAxis(ap=payi[:, hf, t0 + k, word:word + 1], axis=0)
                            ).then_inc(s_gat[s], 16)

                if layer == 1:
                    start_at_one(gp, *s_dfree)
                    gp.memset(dst[:, :, :, :], 0.0).then_inc(s_dz, 1)
                if layer == 0:
                    gp.memset(msg[:, :, :, F:F + 1], 1.0).then_inc(s_one, 1)
                    for c in range(4):
                        gp.memset(cen[:, c:c + 1], -1.0 + c * 2.0 / 3.0)
                    gp.memset(zb[:, :], 0.0).then_inc(s_one, 1)
                if layer != 1:
                    with gp.Fori(0, G) as i:
                        for q in range(QN):
                            gather(i, q)
                else:
                    gather(0, 0)
                    with gp.Fori(0, G) as i:
                        for q in range(QN):
                            if q + 1 < QN:
                                gather(i, q + 1)
                            else:
                                gather(i + 1, 0)
                            s, m = q % 2, q // 2
                            hf, t0 = q // HQ, (q % HQ) * CT
                            gp.wait_ge(s_dm[s], i * HQ + (m + 1))
                            gp.sem_inc(s_begun, 1)
                            for k in range(CT):
                                gp.indirect_dma_start(
                                    out=dr["D"], out_offset=bass.IndirectOffsetOnAxis(
                                        ap=payi[:, hf, t0 + k, W_DROW:W_DROW + 1], axis=0),
                                    in_=dst[:, s, k, :], in_offset=None, bounds_check=sh.t * P - 1,
                                    oob_is_err=False).then_inc(s_dsent[s], 16)
                            for d in ([q - 1] if q else []) + ([q] if q == QN - 1 else []):
                                gp.wait_ge(s_dsent[d % 2], (i * HQ + (d // 2 + 1)) * (16 * CT))
                                gp.sem_inc(s_dfree[d % 2], 1)
                for s in range(2):
                    gp.wait_ge(s_gat[s], 16 * CT * sides * (HQ * G + (1 if layer == 1 and s == 0 else 0)))

            @block.sync
            def _(sp):
                if layer == 1:
                    sp.wait_ge(s_w2z, 1)
                    for k in range(2):
                        sp.dma_start(w2[64 * k:64 * k + 64, F * k:F * k + F], io["w2t"]).then_inc(s_w2, 16)
                        sp.dma_start(b2[:, k, :], io["b2"].partition_broadcast(P)).then_inc(s_w2, 16)
                start_at_one(sp, *s_st)
                with sp.Fori(0, G) as i:
                    for q in range(QN):
                        s, m = q % 2, q // 2
                        sp.wait_ge(s_ev[s], i * HQ + (m + 1) + ONE)
                        sums = dr["P"][bass.ds(i * GT + q * CT, CT), 0:M * P].rearrange("t (f l) -> f t l", l=P)
                        sp.dma_start(sums, stg[0:M, s, :].rearrange("f (t l) -> f t l", l=P)).then_inc(s_st[s], 16)
                for s in range(2):
                    sp.wait_ge(s_st[s], 16 * HQ * G + ONE)

            @block.tensor
            def _(pe):
                start_at_one(pe, *s_sc, *(s_hd if layer == 0 else []))
                if layer == 0:
                    pe.wait_ge(s_one, 2)
                    nc.tensor.matmul(ps_h[0:NB, 0:P], zb[:, 0:NB], zb[:, :], start=True, stop=False)
                if layer == 1:
                    pe.wait_ge(s_w2, 64)
                with pe.Fori(0, G) as i:
                    for q in range(QN):
                        s, m = q % 2, q // 2
                        if layer == 1:
                            pe.wait_ge(s_hid[s], i * HQ + (m + 1))
                            pe.wait_ge(s_hT[s], i * HQ + m + ONE)
                            for k in range(CT):
                                last = nc.tensor.transpose(ps_t[s][:, k * P:(k + 1) * P], hid[:, s, k, :], cst["ident"][:, :])
                            last.then_inc(s_tr[s], 1)
                            pe.wait_ge(s_hT[s], i * HQ + (m + 1) + ONE)
                            pe.wait_ge(s_vread[s], i * HQ + m + ONE)
                            for k in range(CT):
                                last = nc.tensor.matmul(ps_v[s][:, k * 2 * F:(k + 1) * 2 * F], hidT[:, s, k * P:(k + 1) * P],
                                                        w2[:, :], start=True, stop=True)
                            last.then_inc(s_v[s], 1)
                        pe.wait_ge(s_hot[s], i * HQ + (m + 1))
                        pe.wait_ge(s_msg[s], i * HQ + (m + 1) + ONE)
                        pe.wait_ge(s_ev[s], i * HQ + m + ONE)
                        for k in range(CT):
                            last = nc.tensor.matmul(ps[s][0:M, k * P:(k + 1) * P], msg[:, s, k, :], hot[:, s, k, :],
                                                    start=True, stop=True)
                        last.then_inc(s_sc[s], 1)
                        if layer == 0:
                            pe.wait_ge(s_hh[s], (i * HQ + m) * 2 + 2)
                            for k in range(CT):
                                last = nc.tensor.matmul(ps_h[0:NB, 0:P], hhi[:, s, k, :], hlo[:, s, k, :],
                                                        start=False, stop=False)
                            last.then_inc(s_hd[s], 1)
                if layer == 0:
                    nc.tensor.matmul(ps_h[0:NB, 0:P], zb[:, 0:NB], zb[:, :], start=False, stop=True).then_inc(s_hf, 1)

            @block.vector
            def _(dve):
                start_at_one(dve, *{0: s_taken + s_msg, 1: s_taken + s_msg, 2: s_msg, 3: s_taken}[layer],
                             *(s_vread if layer == 1 else []))
                if layer == 0:
                    dve.wait_ge(s_one, 2)
                if layer == 1:
                    nc.vector.memset(w2[:, :], 0.0).then_inc(s_w2z, 1)
                    dve.wait_ge(s_dz, 1)
                    dve.wait_ge(s_w2, 64)
                per_chunk = {0: 1, 1: 13, 2: 2, 3: 1}[layer]
                iota = cst["iota"]
                with dve.Fori(0, G) as i:
                    step = counter(dve, s_ch, i * (QN * per_chunk))
                    bstep = counter(dve, s_basis_ch, i * 10)
                    for q in range(QN):
                        s, m = q % 2, q // 2
                        hf, t0 = q // HQ, (q % HQ) * CT
                        turn = i * HQ + m
                        if q % HQ == 0:
                            dve.wait_ge(s_pay[hf], i * 16 + 16)
                            if layer == 0:
                                ph = pay[:, hf, :, W_A2:W_A2 + 2]
                                sh4 = [P, HT, 2, 4]
                                bstep(nc.vector.tensor_tensor(hat[:, :, :, :], bc(ph, 3, sh4),
                                                              cen[:, :].unsqueeze(1).unsqueeze(1).to_broadcast(sh4), ALU.subtract))
                                flat = hat[:, :, :, :].rearrange("p t a u -> p (t a u)")
                                bstep(nc.vector.scalar_tensor_tensor(out=flat, in0=flat, scalar=-1.0, in1=flat,
                                                                     op0=ALU.mult, op1=ALU.max))
                                bstep(nc.vector.tensor_scalar(flat, flat, -1.5, 1.0, ALU.mult, ALU.add))
                                bstep(nc.vector.tensor_scalar(hat[:, :, :, :], hat[:, :, :, :], 0.0, None, ALU.max))
                                bstep(nc.vector.tensor_tensor(
                                    basis[:, hf, :, :].rearrange("p t (u v) -> p t u v", v=4),
                                    bc(hat[:, :, 0, :], 3, [P, HT, 4, 4]), bc(hat[:, :, 1, :], 2, [P, HT, 4, 4]), ALU.mult))
                        dve.wait_ge(s_sc[s], turn + ONE)
                        here = pay[:, hf, t0:t0 + CT, :]
                        nc.vector.tensor_tensor(hot[:, s, :, :], bc(iota[:, :], 1, [P, CT, P]),
                                                here[:, :, W_SLO:W_SLO + 1].to_broadcast([P, CT, P]),
                                                ALU.is_equal).then_inc(s_hot[s], 1)
                        if layer == 0:
                            dve.wait_ge(s_hd[s], turn + ONE)
                            nc.vector.tensor_tensor(hlo[:, s, :, :], bc(iota[:, :], 1, [P, CT, P]),
                                                    here[:, :, W_DLO:W_DLO + 1].to_broadcast([P, CT, P]),
                                                    ALU.is_equal).then_inc(s_hh[s], 1)
                            nc.vector.tensor_tensor(hhi[:, s, :, :], bc(iota[:, 0:NB], 1, [P, CT, NB]),
                                                    here[:, :, W_DHI:W_DHI + 1].to_broadcast([P, CT, NB]),
                                                    ALU.is_equal).then_inc(s_hh[s], 1)
                        if layer != 1:
                            dve.wait_ge(s_gat[s], (turn + 1) * (16 * CT))
                        else:
                            dve.wait_ge(s_gat[s], (turn + 1) * (32 * CT))
                        got = rows[:, 0, s, :, :]
                        if layer == 0:
                            ba = basis[:, hf, t0:t0 + CT, :]
                            ins = nc.vector.tensor_tensor(
                                prod[:, :, :].rearrange("p t (k o) -> p t k o", o=F),
                                got.rearrange("p t (k o) -> p t k o", o=F), bc(ba, 3, [P, CT, F, F]), ALU.mult)
                            ins.then_inc(s_taken[s], 1)
                            dve.wait_ge(s_taken[s], turn + 1 + ONE)
                            nc.vector.tensor_reduce(msg[:, s, :, 0:F], prod[:, :, :].rearrange("p t (k o) -> p t o k", o=F),
                                                    AX.X, ALU.add).then_inc(s_msg[s], 1)
                            dve.wait_ge(s_msg[s], turn + 1 + ONE)
                        elif layer in (2, 3):
                            a8 = here[:, :, W_A8:W_A8 + 8]
                            step(nc.vector.tensor_tensor(
                                prod[:, :, :].rearrange("p t (k o) -> p t k o", o=F),
                                got[:, :, 0:128].rearrange("p t (k o) -> p t k o", o=F), bc(a8, 3, [P, CT, 8, F]), ALU.mult))
                            red = prod[:, :, :].rearrange("p t (k o) -> p t o k", o=F)
                            if layer == 2:
                                step(nc.vector.tensor_reduce(pre[:, s, :, :], red, AX.X, ALU.add))
                                nc.vector.tensor_tensor(msg[:, s, :, :], pre[:, s, :, :], got[:, :, 128:144],
                                                        ALU.add).then_inc(s_msg[s], 1)
                                dve.wait_ge(s_msg[s], turn + 1 + ONE)
                            else:
                                dve.wait_ge(s_msg[s], turn + ONE)
                                nc.vector.tensor_reduce(pre[:, s, :, :], red, AX.X, ALU.add).then_inc(s_pre[s], 1)
                                dve.wait_ge(s_pre[s], turn + 1 + ONE)
                        else:
                            D, S = got, rows[:, 1, s, :, :]
                            nc.vector.tensor_tensor(hid[:, s, :, 0:64], S[:, :, 0:64], D[:, :, 64:128], ALU.add)
                            nc.vector.tensor_tensor(hid[:, s, :, 64:128], D[:, :, 0:64], S[:, :, 64:128],
                                                    ALU.add).then_inc(s_hid[s], 1)
                            sh4 = [P, CT, 2, F]
                            dve.wait_ge(s_v[s], turn + 1)
                            nc.vector.tensor_tensor(v[:, :, :, :], ps_v[s][:, 0:CT * 2 * F].rearrange("p (t a f) -> p t a f", a=2, f=F),
                                                    bc(b2[:, :, :], 1, sh4), ALU.add).then_inc(s_vread[s], 1)
                            dve.wait_ge(s_vread[s], turn + 1 + ONE)
                            step(nc.vector.tensor_tensor(tv[:, :, :, :], v[:, :, :, :], v[:, :, :, :], ALU.mult))
                            w = [sc[:, k, :].rearrange("p (t a) -> p t a", a=2) for k in range(3)]
                            step(nc.vector.tensor_reduce(w[0], tv[:, :, :, :], AX.X, ALU.add))
                            step(nc.vector.tensor_scalar(sc[:, 0, :], sc[:, 0, :], 1e-24, 0.5, ALU.max, ALU.mult))
                            step(nc.vector.reciprocal(sc[:, 1, :], sc[:, 0, :]))
                            nc.vector.tensor_tensor(cur[:, :, 0, :], D[:, :, 128:144], D[:, :, 144:145].to_broadcast([P, CT, F]), ALU.mult)
                            nc.vector.tensor_tensor(cur[:, :, 1, :], S[:, :, 128:144], S[:, :, 144:145].to_broadcast([P, CT, F]),
                                                    ALU.mult).then_inc(s_taken[s], 1)
                            dve.wait_ge(s_taken[s], turn + 1 + ONE)
                            dve.wait_ge(s_sc[s], turn + ONE)
                            dve.wait_ge(s_dfree[s], turn + ONE)
                            for near in range(2):
                                vv = [v[:, :, a, :] for a in range(2)]
                                cc = [w[1][:, :, a] for a in range(2)]
                                order = (0, 1) if near else (1, 0)
                                for a in range(2):
                                    ins = nc.vector.tensor_tensor(tv[:, :, a, :], vv[order[a]], cur[:, :, a, :], ALU.mult)
                                step(ins)
                                step(nc.vector.tensor_reduce(w[2], tv[:, :, :, :], AX.X, ALU.add))
                                for a in range(2):
                                    ins = nc.vector.tensor_tensor(w[0][:, :, a], w[2][:, :, a], cc[order[a]], ALU.mult)
                                step(ins)
                                for a in range(2):
                                    ins = nc.vector.tensor_tensor(tv[:, :, a, :], vv[order[a]], bc(w[0][:, :, a], 2, [P, CT, F]), ALU.mult)
                                step(ins)
                                if not near:
                                    step(nc.vector.tensor_tensor(cur[:, :, :, :], cur[:, :, :, :], tv[:, :, :, :], ALU.subtract))
                            nc.vector.tensor_tensor(msg[:, s, :, :], cur[:, :, 0, :], tv[:, :, 0, :], ALU.subtract).then_inc(s_msg[s], 1)
                            nc.vector.tensor_copy(dst[:, s, :, F:F + 1], here[:, :, W_DLO:W_DLO + 1])
                            nc.vector.tensor_tensor(dst[:, s, :, 0:F], cur[:, :, 1, :], tv[:, :, 1, :], ALU.subtract).then_inc(s_dm[s], 1)
                            dve.wait_ge(s_dm[s], turn + 1)
                    if layer != 0:
                        assert step.count[0] == QN * per_chunk, step.count
                if layer == 0:
                    dve.wait_ge(s_hf, 1)
                    nc.vector.tensor_copy(hist[0:NB, :], ps_h[0:NB, 0:P])


def dst_phase(nc, sh, dr, cst):
    G = sh.g
    tag = "_D"
    with nc.cleanup_on_exit(), ExitStack() as ctx:
        def sb(name, shape, dt=FP):
            return ctx.enter_context(nc.sbuf_tensor(name + tag, shape, dt))

        def two(name):
            return [nc.alloc_semaphore(f"{name}{s}{tag}") for s in range(2)]
        pay = sb("pay", [P, 2, HT, DW])
        hot = sb("hot", [P, 2, CT, P])
        stg = sb("stg", [F, 2, CT * P])
        ps = [ctx.enter_context(nc.psum_tensor(f"ps{s}{tag}", [P, 512], FP)) for s in range(2)]
        s_pay, s_hot, s_sc, s_ev, s_st = (two(n) for n in ("payload", "onehot", "scattered", "evacuated", "stored"))

        def half(i, hf):
            return dr["D"][bass.ds(i * (GT * P), GT * P), :].rearrange("(p t) w -> p t w", t=GT)[:, hf * HT:(hf + 1) * HT, :]

        with nc.Block() as block:
            @block.scalar
            def _(act):
                for hf in range(2):
                    act.dma_start(pay[:, hf, :, :], half(0, hf)).then_inc(s_pay[hf], 16)
                start_at_one(act, *s_ev)
                with act.Fori(0, G) as i:
                    for q in range(QN):
                        s, m = q % 2, q // 2
                        act.wait_ge(s_sc[s], i * HQ + (m + 1) + ONE)
                        act.wait_ge(s_st[s], (i * HQ + m) * 16 + ONE)
                        act.activation(stg[:, s, :], ps[s][0:F, :], ACT.Copy).then_inc(s_ev[s], 1)
                        if q in (HQ - 1, QN - 1):
                            act.dma_start(pay[:, q // HQ, :, :], half(i + 1, q // HQ)).then_inc(s_pay[q // HQ], 16)
                for hf in range(2):
                    act.wait_ge(s_pay[hf], 16 * (G + 1))

            @block.sync
            def _(sp):
                start_at_one(sp, *s_st)
                with sp.Fori(0, G) as i:
                    for q in range(QN):
                        s, m = q % 2, q // 2
                        sp.wait_ge(s_ev[s], i * HQ + (m + 1) + ONE)
                        sums = dr["P"][bass.ds(i * GT + q * CT, CT), 0:F * P].rearrange("t (f l) -> f t l", l=P)
                        sp.dma_start(sums, stg[:, s, :].rearrange("f (t l) -> f t l", l=P)).then_inc(s_st[s], 16)
                for s in range(2):
                    sp.wait_ge(s_st[s], 16 * HQ * G + ONE)

            @block.tensor
            def _(pe):
                start_at_one(pe, *s_sc)
                with pe.Fori(0, G) as i:
                    for q in range(QN):
                        s, m = q % 2, q // 2
                        hf, t0 = q // HQ, (q % HQ) * CT
                        pe.wait_ge(s_hot[s], i * HQ + (m + 1))
                        pe.wait_ge(s_ev[s], i * HQ + m + ONE)
                        for k in range(CT):
                            last = nc.tensor.matmul(ps[s][0:F, k * P:(k + 1) * P], pay[:, hf, t0 + k, 0:F], hot[:, s, k, :],
                                                    start=True, stop=True)
                        last.then_inc(s_sc[s], 1)

            @block.vector
            def _(dve):
                with dve.Fori(0, G) as i:
                    for q in range(QN):
                        s, m = q % 2, q // 2
                        hf, t0 = q // HQ, (q % HQ) * CT
                        if q % HQ == 0:
                            dve.wait_ge(s_pay[hf], i * 16 + 16)
                        dve.wait_ge(s_sc[s], i * HQ + m + ONE)
                        nc.vector.tensor_tensor(hot[:, s, :, :], bc(cst["iota"][:, :], 1, [P, CT, P]),
                                                pay[:, hf, t0:t0 + CT, F:F + 1].to_broadcast([P, CT, P]),
                                                ALU.is_equal).then_inc(s_hot[s], 1)


def combine_phase(nc, sh, tag, own, dr, cst, M, finish):
    G, NB = sh.g, sh.nb
    n_bank = -(-M * P // 512)
    with nc.cleanup_on_exit(), ExitStack() as ctx:
        part = ctx.enter_context(nc.sbuf_tensor("part" + tag, [P, 2, M * P], FP))
        who = ctx.enter_context(nc.sbuf_tensor("who" + tag, [P, NB], FP))
        zero = ctx.enter_context(nc.sbuf_tensor("zero" + tag, [P, 512], FP))
        bank = [ctx.enter_context(nc.psum_tensor(f"bank{k}{tag}", [P, 512], FP)) for k in range(n_bank)]
        s_ld = [nc.alloc_semaphore(f"cb_load{s}{tag}") for s in range(2)]
        s_z, s_who, s_mm, s_fin, s_ch, s_cp = (nc.alloc_semaphore(f"cb_{n}{tag}")
                                         for n in ("zero", "who", "product", "final", "chain", "aux"))
        MH = 8 * P

        def halves(s):
            return (0, MH) if s == 0 else (MH, M * P)
        with nc.Block() as block:
            @block.sync
            def _(sp):
                with sp.Fori(0, G) as i:
                    for s in range(2):
                        lo, hi = halves(s)
                        sp.wait_ge(s_mm, i * 2 + ONE)
                        sp.dma_start(part[0:GT, s, lo:hi], dr["P"][bass.ds(i * GT, GT), lo:hi]).then_inc(s_ld[s], 16)

            @block.gpsimd
            def _(gp):
                gp.memset(zero[:, :], 0.0).then_inc(s_z, 1)

            @block.tensor
            def _(pe):
                pe.wait_ge(s_z, 1)
                start_at_one(pe, s_mm)
                for k in range(n_bank):
                    nc.tensor.matmul(bank[k][0:NB, :], zero[0:GT, 0:NB], zero[0:GT, :], start=True, stop=False)
                with pe.Fori(0, G) as i:
                    pe.wait_ge(s_who, i + 1)
                    for s in range(2):
                        pe.wait_ge(s_ld[s], i * 16 + 16)
                        lo, hi = halves(s)
                        for c in range(lo, hi, 512):
                            n = min(512, hi - c)
                            last = nc.tensor.matmul(bank[c // 512][0:NB, 0:n], who[0:GT, :], part[0:GT, s, c:c + n],
                                                    start=False, stop=False)
                        last.then_inc(s_mm, 1)
                for k in range(n_bank):
                    last = nc.tensor.matmul(bank[k][0:NB, :], zero[0:GT, 0:NB], zero[0:GT, :], start=False, stop=True)
                last.then_inc(s_fin, 1)

            @block.vector
            def _(dve):
                with dve.Fori(0, G) as i:
                    dve.wait_ge(s_mm, i * 2 + ONE)
                    nc.vector.tensor_copy(who[0:GT, :], own[0:GT, bass.ds(i * NB, NB)]).then_inc(s_who, 1)
                dve.wait_ge(s_fin, 1)
                step = counter(dve, s_ch)
                finish(dve, bank, step, s_cp)

            @block.scalar
            def _(act):
                if finish.root is not None:
                    finish.root(act, s_cp)


def bank_view(bank, NB, k):
    return bank[k][0:NB, :].rearrange("p (f l) -> p l f", l=P)


def four(buf, NB, k):
    return buf[0:NB, :].rearrange("p (l f) -> p l f", f=F)[:, :, 4 * k:4 * k + 4]


def gnn(nc, sh, io, out):
    NB, G = sh.nb, sh.g

    def dram(name, shape):
        return nc.dram_tensor(name, shape, FP, kind="Internal").ap()
    dr = {
        "S": dram("edges_src_order", [(sh.t + GT) * P, PW]),
        "D": dram("messages_dst_order", [(sh.t + GT) * P, DW]),
        "P": dram("tile_sums", [sh.t, (F + 1) * P]),
    }
    table = [dram(f"table{l}", [sh.npad, c]) for l, c in enumerate((256, 148, 144, 128))]
    with ExitStack() as ctx:
        def sb(name, shape, dt=FP):
            return ctx.enter_context(nc.sbuf_tensor(name, shape, dt))
        cst = {
            "iota": sb("iota", [P, P]), "ident": sb("ident", [P, P]),
            "own_src": sb("own_src", [P, G * NB]), "own_dst": sb("own_dst", [P, G * NB]),
        }
        setup_phase(nc, sh, io, dr, cst)

        x, h, agg = (sb(n, [P, P * F]) for n in ("x", "h", "agg"))
        hist, deg, dinv = (sb(n, [P, P]) for n in ("hist", "deg", "dinv"))
        bias = sb("bias1", [P, P])

        norm_phase(nc, sh, "0", x, h, io=io)
        node_matmul(nc, sh, "_t0", h, [io["w0"]], 256, cst, "table", table[0])
        edge_phase(nc, sh, 0, io, dr, cst, table[0], hist=hist)

        def finish0(dve, bank, step, s_cp):
            for k in range(4):
                step(nc.vector.tensor_tensor(four(x, NB, k), four(x, NB, k), bank_view(bank, NB, k), ALU.add))
            step(nc.vector.tensor_tensor(deg[0:NB, :], hist[0:NB, :], bank[4][0:NB, 0:P], ALU.add))
            nc.vector.tensor_scalar(deg[0:NB, :], deg[0:NB, :], 1e-5, None, ALU.max).then_inc(s_cp, 1)
            dve.wait_ge(s_cp, 2)
            step(nc.vector.reciprocal(dinv[0:NB, :], deg[0:NB, :]))

        def root0(act, s_cp):
            act.wait_ge(s_cp, 1)
            act.activation(deg[0:NB, :], deg[0:NB, :], ACT.Sqrt).then_inc(s_cp, 1)
        finish0.root = root0
        combine_phase(nc, sh, "_c0", cst["own_src"], dr, cst, F + 1, finish0)

        norm_phase(nc, sh, "1", x, h)
        s_bz, s_bl = nc.alloc_semaphore("bias_zero"), nc.alloc_semaphore("bias_load")
        with nc.Block() as block:
            @block.vector
            def _(dve):
                nc.vector.memset(bias[:, :], 0.0).then_inc(s_bz, 1)

            @block.sync
            def _(sp):
                sp.wait_ge(s_bz, 1)
                sp.dma_start(bias[:, 0:64], io["b1"].partition_broadcast(P)).then_inc(s_bl, 16)
                sp.wait_ge(s_bl, 16)
        node_matmul(nc, sh, "_t1", h, [io["w1a"], io["w1b"]], 128, cst, "table", table[1],
                    extra={"bias": bias, "dinv": dinv})
        edge_phase(nc, sh, 1, io, dr, cst, table[1])

        def finish1s(dve, bank, step, s_cp):
            for k in range(4):
                step(nc.vector.tensor_copy(four(agg, NB, k), bank_view(bank, NB, k)))
        finish1s.root = None
        combine_phase(nc, sh, "_c1s", cst["own_src"], dr, cst, F, finish1s)
        dst_phase(nc, sh, dr, cst)

        def finish1d(dve, bank, step, s_cp):
            for k in range(4):
                step(nc.vector.tensor_tensor(four(agg, NB, k), four(agg, NB, k), bank_view(bank, NB, k), ALU.add))
            a3 = agg[0:NB, :].rearrange("p (l f) -> p l f", f=F)
            step(nc.vector.tensor_tensor(a3, a3, bc(dinv[0:NB, :], 2, [NB, P, F]), ALU.mult))
            step(nc.vector.tensor_tensor(agg[0:NB, :], agg[0:NB, :], h[0:NB, :], ALU.add))
            step(nc.vector.scalar_tensor_tensor(out=x[0:NB, :], in0=agg[0:NB, :], scalar=0.0, in1=x[0:NB, :],
                                                op0=ALU.max, op1=ALU.add))
        finish1d.root = None
        combine_phase(nc, sh, "_c1d", cst["own_dst"], dr, cst, F, finish1d)

        norm_phase(nc, sh, "2", x, h)
        node_matmul(nc, sh, "_t2", h, [io["w2k"], io["w2b"]], 144, cst, "table", table[2])
        edge_phase(nc, sh, 2, io, dr, cst, table[2])

        def finish2(dve, bank, step, s_cp):
            for k in range(4):
                step(nc.vector.tensor_tensor(four(x, NB, k), four(x, NB, k), bank_view(bank, NB, k), ALU.add))
        finish2.root = None
        combine_phase(nc, sh, "_c2", cst["own_src"], dr, cst, F, finish2)

        norm_phase(nc, sh, "3", x, h)
        node_matmul(nc, sh, "_t3", h, [io["w3"]], 128, cst, "table", table[3])
        edge_phase(nc, sh, 3, io, dr, cst, table[3])
        combine_phase(nc, sh, "_c3", cst["own_src"], dr, cst, F, finish1s)
        u = sb("u", [P, P * F])
        su = sb("silu_u", [P, P * F])
        agg2 = sb("agg2", [P, P * F])
        node_matmul(nc, sh, "_lin", agg, [io["wml"]], F, cst, "copy", agg2, extra=0.25)
        node_matmul(nc, sh, "_upd", h, [io["wupd"]], 256, cst, "upd", u, extra=agg2)
        with nc.Block() as block:
            @block.scalar
            def _(act):
                act.activation(su[0:NB, :], u[0:NB, :], ACT.Silu, scale=1.0 / 16)

            @block.vector
            def _(dve):
                nc.vector.tensor_tensor(x[0:NB, :], x[0:NB, :], h[0:NB, :], ALU.add)
        node_matmul(nc, sh, "_fin", su, [io["wul"]], F, cst, "final", x, extra=0.25)
        s_o = nc.alloc_semaphore("stored_out")
        with nc.Block() as block:
            @block.sync
            def _(sp):
                full = NB - 1
                sp.dma_start(out[0:full * P, :].rearrange("(b l) f -> b (l f)", l=P), x[0:full, :]).then_inc(s_o, 16)
                sp.dma_start(out[full * P:sh.n, :].rearrange("(b l) f -> b (l f)", b=1), x[full:NB, 0:sh.last * F]).then_inc(s_o, 16)
                sp.wait_ge(s_o, 32)


def laid_out(inputs):
    import numpy as np
    c = np.ascontiguousarray
    a = {k: np.asarray(v) for k, v in inputs.items()}
    w1 = a["L1_gnn_W1"]
    return {
        "x": c(a["x"]), "src": c(a["src"]), "dst": c(a["dst"]),
        "edge_attr_2": c(a["edge_attr_2"]), "edge_attr_8": c(a["edge_attr_8"]),
        "w0": c(a["L0_gnn_weight"].reshape(16, 16, 16).transpose(1, 0, 2).reshape(16, 256)),
        "w1a": c(w1[:, 0:16].T), "w1b": c(w1[:, 16:32].T), "b1": c(a["L1_gnn_b1"]),
        "w2t": c(a["L1_gnn_W2"].T), "b2": c(a["L1_gnn_b2"]),
        "w2k": c(a["L2_gnn_kernel"].reshape(8, 16, 16).transpose(2, 0, 1).reshape(16, 128)),
        "w2b": c(a["L2_gnn_bias"].reshape(16, 16).T),
        "w3": c(a["L3_gnn_W_msg_tp"].reshape(16, 128)), "wml": c(a["L3_gnn_W_msg_lin"]),
        "wupd": c(a["L3_gnn_W_upd_tp"].reshape(16, 256)), "wul": c(a["L3_gnn_W_upd_lin"]),
    }


def kernel(**inputs):
    import concourse.bacc as _bacc
    from concourse.bass_utils import run_bass_kernel_spmd as _run

    arrays = laid_out(inputs)
    nc = _bacc.Bacc("TRN2", target_bir_lowering=False, num_devices=1)
    io = {k: nc.dram_tensor(f"in_{k}", v.shape, mybir.dt.from_np(v.dtype), kind="ExternalInput").ap()
          for k, v in arrays.items()}
    n = arrays["x"].shape[0]
    out = nc.dram_tensor("out_nodes", [n, F], FP, kind="ExternalOutput").ap()
    gnn(nc, Shapes(n, arrays["src"].shape[0]), io, out)
    r = _run(nc, [{f"in_{k}": v for k, v in arrays.items()}], core_ids=[0])
    return r.results[0]["out_nodes"]
```

```python
import concourse.bass as bass
from concourse import mybir
from contextlib import ExitStack

FP = mybir.dt.float32
BF = mybir.dt.bfloat16
I32 = mybir.dt.int32
I16 = mybir.dt.int16
ALU = mybir.AluOpType
ACT = mybir.ActivationFunctionType
AX = mybir.AxisListType

P = 128
F = 16
GT = 104
CT = 4
HT = GT // 2
QN = GT // CT
HQ = QN // 2
PW = 16
DW = 20
KT = 25
KS = 5
C1 = 148
MAGIC = 12582912.0
ONE = 1
OUTSIDE = 1 << 20

W_SLO, W_DLO, W_DST, W_DROW, W_SRC, W_DHI, W_A2, W_A8 = 0, 1, 2, 3, 4, 5, 6, 8


class Shapes:
    def __init__(self, n_nodes, n_edges):
        self.n = n_nodes
        self.e = n_edges
        self.nb = -(-n_nodes // P)
        self.npad = self.nb * P
        self.last = n_nodes - (self.nb - 1) * P
        self.j = n_edges // P
        self.g = -(-(self.j + self.nb) // GT)
        self.t = self.g * GT
        assert n_edges % P == 0 and self.j % (KT * KS) == 0 and self.nb <= P


def counter(eng, sem, base=0):
    n = [0]

    def step(ins):
        n[0] += 1
        ins.then_inc(sem, 1)
        eng.wait_ge(sem, base + n[0])
        return n[0]

    step.count = n
    return step


def start_at_one(eng, *sems):
    for s in sems:
        eng.sem_inc(s, ONE)


def bc(ap, axis, shape):
    return ap.unsqueeze(axis).to_broadcast(shape)


def setup_phase(nc, sh, io, dr, cst):
    J, NB, G = sh.j, sh.nb, sh.g
    n_it = J // (KT * KS)
    src_v = io["src"].rearrange("(p j) -> p j", p=P)
    dst_v = io["dst"].rearrange("(p j) -> p j", p=P)
    a2_v = io["edge_attr_2"].rearrange("(p j) c -> p (j c)", p=P)
    a8_v = io["edge_attr_8"].rearrange("(p j) c -> p (j c)", p=P)
    with nc.cleanup_on_exit(), ExitStack() as ctx:
        def sb(name, shape, dt):
            return ctx.enter_context(nc.sbuf_tensor(name, shape, dt))

        def sem(name):
            return nc.alloc_semaphore("su_" + name)

        key = [sb("key_src", [P, J], I32), sb("key_dst", [P, J], I32)]
        blk = [sb("blk_src", [P, J], FP), sb("blk_dst", [P, J], FP)]
        low = [sb("low_src", [P, J], FP), sb("low_dst", [P, J], FP)]
        pos = [sb("pos_src", [P, J], FP), sb("pos_dst", [P, J], FP)]
        mask = sb("mask", [P, J], FP)
        scan = sb("scan", [P, J], FP)
        row = [mask[:, :].bitcast(I32), scan[:, :].bitcast(I32)]
        slot = [mask[:, :].bitcast(BF)[:, k * J:(k + 1) * J] for k in range(2)]
        NE = NB + NB % 2
        cnt = sb("cnt", [P, 2 * NE], FP)
        tiles = sb("tiles", [P, 2 * NE], FP)
        base = sb("base", [P, 2 * NE], FP)
        before = sb("before", [P, 2, P + 1], FP)
        tri = sb("tri", [P, P], FP)
        ones = sb("ones", [P, P], FP)
        tno = sb("tile_no", [P, G], FP)
        nblk = sb("blocks_before_tile", [P, G], FP)
        tcol = sb("tile_col", [P, G], I32)
        fs = sb("fill_src", [P, GT * PW], FP)
        fd = sb("fill_dst", [P, HT * DW], FP)
        a2 = sb("a2_in", [P, KS, KT * 2], FP)
        a8 = sb("a8_in", [P, KS, KT * 8], FP)
        rows = sb("rows", [P, KS, KT, PW], FP)
        idx = sb("row_idx", [P, KS, KT], I32)
        ps_tot = ctx.enter_context(nc.psum_tensor("ps_tot", [P, 512], FP))
        ps_pre = ctx.enter_context(nc.psum_tensor("ps_pre", [P, 512], FP))

        s_key = [sem("key_src"), sem("key_dst")]
        s_fillc = sem("fill_const")
        s_tcol, s_tcolst = sem("tile_col"), sem("tile_col_stored")
        s_filled = sem("filled")
        s_const = sem("const")
        s_sum = sem("sums")
        s_dve = sem("dve_chain")
        s_cl = sem("count_loop")
        s_cla = sem("count_loop_act")
        s_prep = sem("keys_split")
        s_cp, s_mask = ([[sem(f"{n}_{o}{k}") for k in range(2)] for o in range(2)] for n in ("placed", "masked"))
        s_abs = [sem("distance_src"), sem("distance_dst")]
        s_scan = [sem("scanned_src"), sem("scanned_dst")]
        s_begun, s_begun_d, s_begun_a = sem("begun_pool"), sem("begun_dve"), sem("begun_act")
        s_attr = [sem(f"attr{s}") for s in range(KS)]
        s_put = [sem(f"words_dve{s}") for s in range(KS)]
        s_puta = [sem(f"words_act{s}") for s in range(KS)]
        s_sent = [sem(f"rows_sent{s}") for s in range(KS)]
        s_free = [sem(f"rows_free{s}") for s in range(KS)]

        with nc.Block() as block:
            @block.sync
            def _(sp):
                sp.dma_start(key[0][:, :], src_v).then_inc(s_key[0], 16)
                sp.dma_start(key[1][:, :], dst_v).then_inc(s_key[1], 16)
                sp.wait_ge(s_fillc, 4)
                sp.dma_start(dr["S"].rearrange("(p g r) w -> p g (r w)", p=P, r=GT),
                             fs[:, :].unsqueeze(1).to_broadcast([P, G + 1, GT * PW])).then_inc(s_filled, 16)
                sp.dma_start(dr["D"].rearrange("(p g r) w -> p g (r w)", p=P, r=HT),
                             fd[:, :].unsqueeze(1).to_broadcast([P, 2 * (G + 1), HT * DW])).then_inc(s_filled, 16)
                sp.wait_ge(s_tcol, 1)
                sp.dma_start(dr["cols"].rearrange("a (g t) -> (a t) g", t=GT), tcol[0:GT, :],
                             allow_slow_non_contiguous=True).then_inc(s_tcolst, 16)
                sp.wait_ge(s_tcolst, 16)
                with sp.Fori(0, n_it) as i:
                    for s in range(KS):
                        sp.wait_ge(s_puta[s], i * 2 + ONE)
                        at = i * (KS * KT) + s * KT
                        sp.dma_start(a2[:, s, :], a2_v[:, bass.ds(at * 2, KT * 2)]).then_inc(s_attr[s], 16)
                        sp.dma_start(a8[:, s, :], a8_v[:, bass.ds(at * 8, KT * 8)]).then_inc(s_attr[s], 16)

            @block.gpsimd
            def _(gp):
                gp.memset(fs[:, :], 0.0).then_inc(s_fillc, 1)
                gp.memset(fd[:, :], 0.0).then_inc(s_fillc, 1)
                gp.wait_ge(s_fillc, 2)
                fs_w = fs[:, :].rearrange("p (r w) -> p r w", w=PW)
                gp.memset(fs_w[:, :, W_SLO:W_DLO + 1], -1.0)
                gp.memset(fs_w.bitcast(I32)[:, :, W_DROW:W_DROW + 1], OUTSIDE).then_inc(s_fillc, 1)
                gp.memset(fd[:, :].rearrange("p (r w) -> p r w", w=DW)[:, :, F:F + 1], -1.0).then_inc(s_fillc, 1)
                gp.iota(cst["iota"][:, :], pattern=[[1, P]], base=0, channel_multiplier=0,
                        allow_small_or_imprecise_dtypes=True)
                gp.iota(tno[:, :], pattern=[[GT, G]], base=0, channel_multiplier=1,
                        allow_small_or_imprecise_dtypes=True)
                gp.memset(ones[:, :], 1.0)
                gp.memset(cst["ident"][:, :], 0.0)
                gp.memset(before[:, :, :], 0.0).then_inc(s_const, 1)
                gp.wait_ge(s_const, 1)
                gp.affine_select(out=cst["ident"][:, :], in_=cst["ident"][:, :], compare_op=ALU.not_equal, fill=1.0,
                                 base=0, pattern=[[-1, P]], channel_multiplier=1)
                gp.affine_select(out=tri[:, :], in_=ones[:, :], compare_op=ALU.is_gt, fill=0.0,
                                 base=0, pattern=[[1, P]], channel_multiplier=-1).then_inc(s_const, 1)
                gp.wait_ge(s_filled, 32)
                start_at_one(gp, *s_free)
                with gp.Fori(0, n_it) as i:
                    for s in range(KS):
                        gp.wait_ge(s_put[s], i + 1)
                        gp.wait_ge(s_puta[s], i * 2 + 2 + ONE)
                        gp.sem_inc(s_begun, 1)
                        for k in range(KT):
                            gp.indirect_dma_start(
                                out=dr["S"], out_offset=bass.IndirectOffsetOnAxis(ap=idx[:, s, k:k + 1], axis=0),
                                in_=rows[:, s, k, :], in_offset=None).then_inc(s_sent[s], 16)
                        for done in ([s - 1] if s else []) + ([s] if s == KS - 1 else []):
                            gp.wait_ge(s_sent[done], (i + 1) * (16 * KT))
                            gp.sem_inc(s_free[done], 1)

            @block.tensor
            def _(pe):
                pe.wait_ge(s_const, 2)
                pe.wait_ge(s_cl, NE)
                pe.wait_ge(s_cla, 2 * NE)
                nc.tensor.matmul(ps_tot[:, 0:2 * NE], ones[:, :], cnt[:, :], start=True, stop=True)
                nc.tensor.matmul(ps_pre[:, 0:2 * NE], tri[:, :], cnt[:, :], start=True, stop=True).then_inc(s_sum, 1)

            @block.scalar
            def _(act):
                act.wait_ge(s_prep, 1)
                with act.Fori(0, NE) as b:
                    loop = counter(act, s_cla, b * 2)
                    loop(act.activation(slot[0], blk[1][:, :], ACT.Abs, bias=cst["iota"][:, bass.ds(b, 1)], scale=-1.0))
                    act.sem_inc(s_begun_a, 1)
                    loop(act.activation(slot[0], slot[0], ACT.Relu, bias=1.0, scale=-1.0,
                                        accum_out=cnt[:, bass.ds(b + NE, 1)]))
                for o in range(2):
                    with act.Fori(0, NE // 2) as i:
                        for k in range(2):
                            act.wait_ge(s_cp[o][k], i + ONE)
                            act.sem_inc(s_begun_a, 1)
                            act.activation(slot[k], blk[o][:, :], ACT.Abs, bias=cst["iota"][:, bass.ds(i * 2 + k, 1)],
                                           scale=-1.0).then_inc(s_abs[o], 1)
                            act.wait_ge(s_abs[o], i * 2 + (k + 1))
                            act.activation(slot[k], slot[k], ACT.Relu, bias=1.0, scale=-1.0).then_inc(s_mask[o][k], 1)
                start_at_one(act, *s_puta)
                with act.Fori(0, n_it) as i:
                    for s in range(KS):
                        act.wait_ge(s_attr[s], i * 32 + 32)
                        act.wait_ge(s_free[s], i + ONE)
                        act.activation(rows[:, s, :, W_A2:W_A2 + 2],
                                       a2[:, s, :].rearrange("p (k c) -> p k c", c=2), ACT.Copy).then_inc(s_puta[s], 1)
                        act.activation(rows[:, s, :, W_A8:W_A8 + 8],
                                       a8[:, s, :].rearrange("p (k c) -> p k c", c=8), ACT.Copy).then_inc(s_puta[s], 1)

            @block.vector
            def _(dve):
                step = counter(dve, s_dve)
                step(nc.vector.memset(base[:, :], 0.0))
                tmp = mask[:, :].bitcast(I32)
                for o in range(2):
                    dve.wait_ge(s_key[o], 16)
                    step(nc.vector.tensor_scalar(tmp, key[o][:, :], 7, None, ALU.arith_shift_right))
                    step(nc.vector.tensor_copy(blk[o][:, :], tmp))
                    step(nc.vector.tensor_scalar(tmp, key[o][:, :], P - 1, None, ALU.bitwise_and))
                    step(nc.vector.tensor_copy(low[o][:, :], tmp))
                dve.wait_ge(s_const, 2)
                dve.sem_inc(s_prep, 1)
                with dve.Fori(0, NE) as b:
                    loop = counter(dve, s_cl, b)
                    loop(nc.vector.tensor_scalar(scan[:, :], blk[0][:, :], cst["iota"][:, bass.ds(b, 1)], 0.0,
                                                 ALU.is_equal, ALU.add, accum_out=cnt[:, bass.ds(b, 1)]))
                dve.wait_ge(s_sum, 1)
                step(nc.vector.tensor_scalar(tiles[:, :], ps_tot[:, 0:2 * NE], (P - 1) / 2, 1.0 / P, ALU.add, ALU.mult))
                step(nc.vector.tensor_scalar(tiles[:, :], tiles[:, :], MAGIC, -MAGIC, ALU.add, ALU.add))
                for o in range(2):
                    part = tiles[:, o * NE:o * NE + NB]
                    step(nc.vector.tensor_tensor_scan(before[:, o, 1:NB + 1], part, part, 0.0, ALU.add, ALU.max))
                    step(nc.vector.scalar_tensor_tensor(out=base[:, o * NE:o * NE + NB], in0=before[:, o, 0:NB],
                                                        scalar=float(P), in1=ps_pre[:, o * NE:o * NE + NB],
                                                        op0=ALU.mult, op1=ALU.add))
                for o in range(2):
                    step(nc.vector.memset(pos[o][:, :], 0.0))
                    start_at_one(dve, *s_cp[o])
                    with dve.Fori(0, NE // 2) as i:
                        for k in range(2):
                            dve.wait_ge(s_mask[o][k], i + 1)
                            nc.vector.tensor_tensor_scan(scan[:, :], slot[k], slot[k],
                                                         base[:, bass.ds(i * 2 + (k + o * NE), 1)], ALU.add, ALU.max
                                                         ).then_inc(s_scan[o], 1)
                            dve.wait_ge(s_scan[o], i * 2 + (k + 1))
                            dve.sem_inc(s_begun_d, 1)
                            nc.vector.copy_predicated(pos[o][:, :], slot[k].bitcast(I16), scan[:, :]).then_inc(s_cp[o][k], 1)
                            dve.wait_ge(s_cp[o][k], i + 1 + ONE)
                t = blk[0][:, :]
                for o in range(2):
                    step(nc.vector.tensor_scalar(t, pos[o][:, :], -(P + 1) / 2, 1.0 / P, ALU.add, ALU.mult))
                    step(nc.vector.tensor_scalar(t, t, MAGIC, -MAGIC, ALU.add, ALU.add))
                    step(nc.vector.scalar_tensor_tensor(out=pos[o][:, :], in0=t, scalar=-float(P), in1=pos[o][:, :],
                                                        op0=ALU.mult, op1=ALU.add))
                    step(nc.vector.scalar_tensor_tensor(out=pos[o][:, :], in0=pos[o][:, :], scalar=float(GT), in1=t,
                                                        op0=ALU.mult, op1=ALU.add))
                    step(nc.vector.tensor_scalar(t, t, -(GT - 1) / 2, 1.0 / GT, ALU.add, ALU.mult))
                    step(nc.vector.tensor_scalar(t, t, MAGIC, -MAGIC, ALU.add, ALU.add))
                    step(nc.vector.scalar_tensor_tensor(out=pos[o][:, :], in0=t, scalar=float((P - 1) * GT),
                                                        in1=pos[o][:, :], op0=ALU.mult, op1=ALU.add))
                    step(nc.vector.tensor_scalar(row[o], pos[o][:, :], -float(GT), None, ALU.add))
                for o, name in enumerate(("own_src", "own_dst")):
                    own = cst[name][0:GT, :].rearrange("p (g b) -> p g b", b=NB)
                    tn = tno[0:GT, :].unsqueeze(2).to_broadcast([GT, G, NB])
                    sh3 = [GT, G, NB]
                    past = pos[0][0:GT, 0:G * NB].rearrange("p (g b) -> p g b", b=NB)
                    step(nc.vector.tensor_tensor(own, tn, bc(before[0:GT, o, 0:NB], 1, sh3), ALU.is_ge))
                    step(nc.vector.tensor_tensor(past, tn, bc(before[0:GT, o, 1:NB + 1], 1, sh3), ALU.is_ge))
                    step(nc.vector.tensor_tensor(own, own, past, ALU.subtract))
                    if o == 0:
                        step(nc.vector.tensor_reduce(nblk[0:GT, :], past, AX.X, ALU.add))
                        nc.vector.tensor_scalar(tcol[0:GT, :], nblk[0:GT, :], float(NB - 1), float(C1),
                                                ALU.min, ALU.mult).then_inc(s_tcol, 1)
                with dve.Fori(0, n_it) as i:
                    for s in range(KS):
                        dve.wait_ge(s_free[s], i + ONE)
                        at = i * (KS * KT) + s * KT
                        r = rows[:, s, :, :]
                        ri = r.bitcast(I32)

                        def col(x):
                            return x[:, bass.ds(at, KT)].unsqueeze(2)
                        nc.vector.tensor_copy(r[:, :, W_SLO:W_SLO + 1], col(low[0][:, :]))
                        nc.vector.tensor_copy(r[:, :, W_DLO:W_DLO + 1], col(low[1][:, :]))
                        nc.vector.tensor_copy(ri[:, :, W_DST:W_DST + 1], col(key[1][:, :]))
                        nc.vector.tensor_copy(ri[:, :, W_DROW:W_DROW + 1], col(row[1]))
                        nc.vector.tensor_copy(ri[:, :, W_SRC:W_SRC + 1], col(key[0][:, :]))
                        nc.vector.tensor_copy(r[:, :, W_DHI:W_DHI + 1], col(blk[1][:, :]))
                        nc.vector.tensor_copy(idx[:, s, :], row[0][:, bass.ds(at, KT)]).then_inc(s_put[s], 1)


def norm_phase(nc, sh, tag, x, h, io=None, tail=None):
    NB = sh.nb
    with nc.cleanup_on_exit(), ExitStack() as ctx:
        xc = ctx.enter_context(nc.sbuf_tensor("xc" + tag, [P, P * F], FP))
        sq = ctx.enter_context(nc.sbuf_tensor("sq" + tag, [P, P * F], FP))
        st = ctx.enter_context(nc.sbuf_tensor("st" + tag, [P, 4, P], FP))
        s_x = nc.alloc_semaphore("nx" + tag)
        s_c = nc.alloc_semaphore("nc" + tag)
        s_v = nc.alloc_semaphore("nv" + tag)
        s_r = nc.alloc_semaphore("nr" + tag)
        s_z = nc.alloc_semaphore("nz" + tag)
        x3, c3, q3, h3 = (v[0:NB, :].rearrange("p (l f) -> p l f", f=F) for v in (x, xc, sq, h))
        with nc.Block() as block:
            if io is not None:
                @block.gpsimd
                def _(gp):
                    gp.memset(x[:, :], 0.0).then_inc(s_z, 1)

                @block.sync
                def _(sp):
                    sp.wait_ge(s_z, 1)
                    full = sh.nb - 1
                    sp.dma_start(x[0:full, :], io["x"][0:full * P, :].rearrange("(b l) f -> b (l f)", l=P)).then_inc(s_x, 16)
                    sp.dma_start(x[full:NB, 0:sh.last * F],
                                 io["x"][full * P:sh.n, :].rearrange("(b l) f -> b (l f)", b=1)).then_inc(s_x, 16)

            @block.vector
            def _(dve):
                if io is not None:
                    dve.wait_ge(s_x, 32)
                step = counter(dve, s_c)
                full = [NB, P, F]
                step(nc.vector.tensor_reduce(st[0:NB, 0, :], x3, AX.X, ALU.add))
                step(nc.vector.tensor_scalar(st[0:NB, 0, :], st[0:NB, 0, :], 1.0 / F, None, ALU.mult))
                step(nc.vector.tensor_tensor(c3, x3, bc(st[0:NB, 0, :], 2, full), ALU.subtract))
                step(nc.vector.tensor_tensor(q3, c3, c3, ALU.mult))
                step(nc.vector.tensor_reduce(st[0:NB, 1, :], q3, AX.X, ALU.add))
                nc.vector.tensor_scalar(st[0:NB, 1, :], st[0:NB, 1, :], 1.0 / F, 1e-5, ALU.mult, ALU.add).then_inc(s_v, 1)
                dve.wait_ge(s_r, 1)
                step(nc.vector.reciprocal(st[0:NB, 3, :], st[0:NB, 2, :]))
                step(nc.vector.tensor_tensor(c3, c3, bc(st[0:NB, 3, :], 2, full), ALU.mult))
                step(nc.vector.tensor_scalar(h3, c3, 0.0, None, ALU.max))

            @block.scalar
            def _(act):
                act.wait_ge(s_v, 1)
                act.activation(st[0:NB, 2, :], st[0:NB, 1, :], ACT.Sqrt).then_inc(s_r, 1)


def node_matmul(nc, sh, tag, src, weights, C, cst, mode, out, extra=None):
    NB = sh.nb
    L = 8
    n_pc = 1 if C * L <= 512 else 4
    lp = L // n_pc
    wid = lp * C
    CW = out.shape[1] if mode == "table" else C
    with nc.cleanup_on_exit(), ExitStack() as ctx:
        def sb(name, shape, dt=FP):
            return ctx.enter_context(nc.sbuf_tensor(name + tag, shape, dt))

        def sem(name):
            return nc.alloc_semaphore(f"nm_{name}{tag}")
        wbd = sb("wbd", [P, L * C])
        hs = sb("hs", [P, 2, P])
        hT = sb("hT", [P, 2, P])
        stage = sb("stage", [P, 2, L, CW])
        tp = [ctx.enter_context(nc.psum_tensor(f"tp{q}{tag}", [P, 512], FP)) for q in range(2)]
        pp = [ctx.enter_context(nc.psum_tensor(f"pp{k}{tag}", [P, 512], FP)) for k in range(n_pc)]
        s_z, s_w = sem("zero"), sem("weights")
        s_hs, s_tp, s_hT = ([sem(f"{n}{q}") for q in range(2)] for n in ("slice", "transposed", "features_first"))
        s_pp, s_begun = sem("product"), sem("begun")
        s_out = [sem(f"out{k}") for k in range(n_pc)]
        s_st = [sem(f"stored{q}") for q in range(2)]
        s_ch, s_pad, s_ex = sem("chain"), sem("pad"), sem("extra_cols")
        on_act = mode == "table" and extra is None

        with nc.Block() as block:
            @block.gpsimd
            def _(gp):
                gp.memset(wbd[:, :], 0.0).then_inc(s_z, 1)
                gp.memset(stage[:, :, :, :], 0.0).then_inc(s_pad, 1)

            @block.sync
            def _(sp):
                sp.wait_ge(s_z, 1)
                for k in range(L):
                    at = 0
                    for w in weights:
                        c = w.shape[1]
                        sp.dma_start(wbd[F * k:F * k + F, k * C + at:k * C + at + c], w).then_inc(s_w, 16)
                        at += c
                if mode == "table":
                    start_at_one(sp, *s_st)
                    y = out.rearrange("(b l) c -> b (l c)", l=P)
                    with sp.Fori(0, P // L // 2) as i:
                        for q in range(2):
                            for k in range(n_pc):
                                sp.wait_ge(s_out[k], i * 2 + (q + 1) + ONE)
                            sp.sem_inc(s_begun, 1)
                            if extra is not None:
                                sp.wait_ge(s_ex, i * 4 + (2 * q + 2))
                            sp.dma_start(y[:, bass.ds((i * 2 + q) * (L * CW), L * CW)],
                                         stage[0:NB, q, :, :].rearrange("p l c -> p (l c)")).then_inc(s_st[q], 16)
                    for q in range(2):
                        sp.wait_ge(s_st[q], 16 * (P // L // 2) + ONE)

            @block.tensor
            def _(pe):
                pe.wait_ge(s_w, 16 * L * len(weights))
                start_at_one(pe, *s_tp)
                with pe.Fori(0, P // L // 2) as i:
                    for q in range(2):
                        pe.wait_ge(s_hs[q], i + 1)
                        nc.tensor.transpose(tp[q][:, 0:NB], hs[0:NB, q, :], cst["ident"][0:NB, 0:NB]).then_inc(s_tp[q], 1)
                        pe.wait_ge(s_hT[q], i + 1)
                        for k in range(n_pc):
                            pe.wait_ge(s_out[k], i * 2 + q + ONE)
                            nc.tensor.matmul(pp[k][0:NB, 0:wid], hT[:, q, 0:NB], wbd[:, k * wid:(k + 1) * wid],
                                             start=True, stop=True).then_inc(s_pp, 1)

            @block.scalar
            def _(act):
                if on_act:
                    act.wait_ge(s_pad, 1)
                    start_at_one(act, *s_out[0::2])
                with act.Fori(0, P // L // 2) as i:
                    for q in range(2):
                        act.wait_ge(s_tp[q], i + ONE)
                        act.activation(hs[0:NB, q, :], src[0:NB, bass.ds((i * 2 + q) * (L * F), L * F)],
                                       ACT.Copy).then_inc(s_hs[q], 1)
                        act.wait_ge(s_tp[q], i + 1 + ONE)
                        act.activation(hT[:, q, 0:NB], tp[q][:, 0:NB], ACT.Copy).then_inc(s_hT[q], 1)
                        if on_act:
                            act.wait_ge(s_st[q], i * 16 + ONE)
                            for k in range(0, n_pc, 2):
                                act.wait_ge(s_pp, (i * 2 + q) * n_pc + (k + 1))
                                act.activation(stage[0:NB, q, k * lp:(k + 1) * lp, 0:C],
                                               pp[k][0:NB, 0:wid].rearrange("p (l c) -> p l c", c=C),
                                               ACT.Copy).then_inc(s_out[k], 1)

            @block.vector
            def _(dve):
                dve.wait_ge(s_pad, 1)
                start_at_one(dve, *s_out[1::2], *([] if on_act else s_out[0::2]))
                with dve.Fori(0, P // L // 2) as i:
                    for q in range(2):
                        n = i * 2 + q
                        if mode == "table":
                            dve.wait_ge(s_st[q], i * 16 + ONE)
                        for k in range(1 if on_act else 0, n_pc, 2 if on_act else 1):
                            dve.wait_ge(s_pp, n * n_pc + (k + 1))
                            prod = pp[k][0:NB, 0:wid].rearrange("p (l c) -> p l c", c=C)
                            lo = n * L + k * lp
                            part = (slice(0, NB), q, slice(k * lp, (k + 1) * lp))
                            if mode == "table" and extra is None:
                                nc.vector.tensor_copy(stage[0:NB, q, k * lp:(k + 1) * lp, 0:C], prod).then_inc(s_out[k], 1)
                            elif mode == "table":
                                nc.vector.tensor_tensor(stage[0:NB, q, k * lp:(k + 1) * lp, 0:C], prod,
                                                        bc(extra["bias"][0:NB, :], 1, [NB, lp, C]), ALU.add).then_inc(s_out[k], 1)
                            elif mode == "copy":
                                nc.vector.tensor_scalar(out[0:NB, bass.ds(lo * F, lp * F)], pp[k][0:NB, 0:wid], extra, None,
                                                        ALU.mult).then_inc(s_out[k], 1)
                            elif mode == "final":
                                nc.vector.scalar_tensor_tensor(out=out[0:NB, bass.ds(lo * F, lp * F)], in0=pp[k][0:NB, 0:wid],
                                                               scalar=extra, in1=out[0:NB, bass.ds(lo * F, lp * F)],
                                                               op0=ALU.mult, op1=ALU.add).then_inc(s_out[k], 1)
                            else:
                                ag = extra[0:NB, bass.ds(lo * F, lp * F)].rearrange("p (l c) -> p l c", c=F)
                                st4 = stage[0:NB, q, k * lp:(k + 1) * lp, :].rearrange("p l (c o) -> p l c o", o=F)
                                nc.vector.tensor_tensor(st4, pp[k][0:NB, 0:wid].rearrange("p (l c o) -> p l c o", c=F, o=F),
                                                        bc(ag, 3, [NB, lp, F, F]), ALU.mult).then_inc(s_ch, 1)
                                dve.wait_ge(s_ch, n * n_pc + (k + 1))
                                nc.vector.tensor_reduce(
                                    out[0:NB, bass.ds(lo * F, lp * F)].rearrange("p (l c) -> p l c", c=F),
                                    stage[0:NB, q, k * lp:(k + 1) * lp, :].rearrange("p l (c o) -> p l o c", o=F),
                                    AX.X, ALU.add).then_inc(s_out[k], 1)
                        if mode == "table" and extra is not None:
                            nc.vector.tensor_copy(stage[0:NB, q, :, C:C + F],
                                                  src[0:NB, bass.ds(n * (L * F), L * F)].rearrange("p (l f) -> p l f", f=F)
                                                  ).then_inc(s_ex, 1)
                            nc.vector.tensor_copy(stage[0:NB, q, :, C + F:C + F + 1],
                                                  extra["dinv"][0:NB, bass.ds(n * L, L)].unsqueeze(2)).then_inc(s_ex, 1)


def edge_phase(nc, sh, layer, io, dr, cst, table, hist=None):
    G, NB = sh.g, sh.nb
    C = table.shape[1]
    M = F + 1 if layer == 0 else F
    tag = f"_L{layer}"
    with nc.cleanup_on_exit(), ExitStack() as ctx:
        def sb(name, shape, dt=FP):
            return ctx.enter_context(nc.sbuf_tensor(name + tag, shape, dt))

        def pb(name):
            return ctx.enter_context(nc.psum_tensor(name + tag, [P, 512], FP))

        def sem(name):
            return nc.alloc_semaphore(f"{name}{tag}")

        def two(name):
            return [sem(f"{name}{s}") for s in range(2)]
        pay = sb("pay", [P, 2, HT, PW])
        payi = pay[:, :, :, :].bitcast(I32)
        rows = sb("rows", [P, 2, CT, C])
        msg = sb("msg", [P, 2, CT, M])
        hot = sb("hot", [P, 2, CT, P])
        stg = sb("stg", [F + 1, 2, CT * P])
        ps = [pb(f"ps{s}") for s in range(2)]
        s_pay, s_gat, s_hot, s_msg, s_taken, s_sc, s_ev, s_st = (
            two(n) for n in ("payload", "gathered", "onehot", "message", "rows_used", "scattered", "evacuated", "stored"))
        s_ch = sem("chain")
        s_one = sem("ones")
        s_basis_ch = sem("basis_chain")
        if layer == 0:
            hat = sb("hat", [P, HT, 2, 4])
            basis = sb("basis", [P, 2, HT, F])
            cen = sb("centers", [P, 4])
            prod = sb("prod", [P, CT, 256])
            hlo = sb("hlo", [P, 2, CT, P], BF)
            hhi = sb("hhi", [P, 2, CT, NB], BF)
            zb = sb("zeros_bf", [P, P], BF)
            ps_h = pb("ps_hist")
            s_hh = two("hist_onehot")
            s_hd = two("hist_done")
            s_hf = sem("hist_final")
        if layer in (2, 3):
            prod = sb("prod", [P, CT, 128])
            pre = sb("pre", [P, 2, CT, F])
            s_pre = two("presilu")
        s_taken = {0: s_taken, 2: s_msg, 3: s_pre if layer == 3 else None}[layer]
        s_begun = sem("begun")

        def half(i, hf):
            return dr["S"][bass.ds(i * (GT * P), GT * P), :].rearrange("(p t) w -> p t w", t=GT)[:, hf * HT:(hf + 1) * HT, :]

        with nc.Block() as block:
            @block.scalar
            def _(act):
                for hf in range(2):
                    act.dma_start(pay[:, hf, :, :], half(0, hf)).then_inc(s_pay[hf], 16)
                start_at_one(act, *s_ev)
                if layer == 3:
                    start_at_one(act, *s_msg)
                with act.Fori(0, G) as i:
                    for q in range(QN):
                        s, m = q % 2, q // 2
                        if layer == 3:
                            act.wait_ge(s_pre[s], i * HQ + (m + 1) + ONE)
                            act.wait_ge(s_sc[s], i * HQ + m + ONE)
                            act.activation(msg[:, s, :, :], pre[:, s, :, :], ACT.Silu,
                                           scale=float(1.0 / (F * 8) ** 0.5)).then_inc(s_msg[s], 1)
                        act.wait_ge(s_sc[s], i * HQ + (m + 1) + ONE)
                        act.wait_ge(s_st[s], (i * HQ + m) * 16 + ONE)
                        act.activation(stg[0:M, s, :], ps[s][0:M, :], ACT.Copy).then_inc(s_ev[s], 1)
                        if q in (HQ, QN - 1):
                            hf = 0 if q == HQ else 1
                            lq = (HQ if hf == 0 else QN) - 1
                            if layer == 0:
                                act.wait_ge(s_hh[lq % 2], (i * HQ + (lq // 2 + 1)) * 2)
                            act.dma_start(pay[:, hf, :, :], half(i + 1, hf)).then_inc(s_pay[hf], 16)
                for hf in range(2):
                    act.wait_ge(s_pay[hf], 16 * (G + 1))

            @block.gpsimd
            def _(gp):
                def gather(i, q):
                    s, m = q % 2, q // 2
                    if q == 0 or q == HQ:
                        gp.wait_ge(s_pay[q // HQ], i * 16 + 16)
                    gp.wait_ge(s_taken[s], i * HQ + m + ONE)
                    gp.sem_inc(s_begun, 1)
                    hf, t0 = q // HQ, (q % HQ) * CT
                    for k in range(CT):
                        gp.indirect_dma_start(
                            out=rows[:, s, k, :], out_offset=None, in_=table,
                            in_offset=bass.IndirectOffsetOnAxis(ap=payi[:, hf, t0 + k, W_DST:W_DST + 1], axis=0)
                        ).then_inc(s_gat[s], 16)

                if layer == 0:
                    gp.memset(msg[:, :, :, F:F + 1], 1.0).then_inc(s_one, 1)
                    for c in range(4):
                        gp.memset(cen[:, c:c + 1], -1.0 + c * 2.0 / 3.0)
                    gp.memset(zb[:, :], 0.0).then_inc(s_one, 1)
                with gp.Fori(0, G) as i:
                    for q in range(QN):
                        gather(i, q)
                for s in range(2):
                    gp.wait_ge(s_gat[s], 16 * CT * HQ * G)

            @block.sync
            def _(sp):
                start_at_one(sp, *s_st)
                with sp.Fori(0, G) as i:
                    for q in range(QN):
                        s, m = q % 2, q // 2
                        sp.wait_ge(s_ev[s], i * HQ + (m + 1) + ONE)
                        sums = dr["P"][bass.ds(i * GT + q * CT, CT), 0:M * P].rearrange("t (f l) -> f t l", l=P)
                        sp.dma_start(sums, stg[0:M, s, :].rearrange("f (t l) -> f t l", l=P)).then_inc(s_st[s], 16)
                for s in range(2):
                    sp.wait_ge(s_st[s], 16 * HQ * G + ONE)

            @block.tensor
            def _(pe):
                start_at_one(pe, *s_sc, *(s_hd if layer == 0 else []))
                if layer == 0:
                    pe.wait_ge(s_one, 2)
                    nc.tensor.matmul(ps_h[0:NB, 0:P], zb[:, 0:NB], zb[:, :], start=True, stop=False)
                with pe.Fori(0, G) as i:
                    for q in range(QN):
                        s, m = q % 2, q // 2
                        pe.wait_ge(s_hot[s], i * HQ + (m + 1))
                        pe.wait_ge(s_msg[s], i * HQ + (m + 1) + ONE)
                        pe.wait_ge(s_ev[s], i * HQ + m + ONE)
                        for k in range(CT):
                            last = nc.tensor.matmul(ps[s][0:M, k * P:(k + 1) * P], msg[:, s, k, :], hot[:, s, k, :],
                                                    start=True, stop=True)
                        last.then_inc(s_sc[s], 1)
                        if layer == 0:
                            pe.wait_ge(s_hh[s], (i * HQ + m) * 2 + 2)
                            for k in range(CT):
                                last = nc.tensor.matmul(ps_h[0:NB, 0:P], hhi[:, s, k, :], hlo[:, s, k, :],
                                                        start=False, stop=False)
                            last.then_inc(s_hd[s], 1)
                if layer == 0:
                    nc.tensor.matmul(ps_h[0:NB, 0:P], zb[:, 0:NB], zb[:, :], start=False, stop=True).then_inc(s_hf, 1)

            @block.vector
            def _(dve):
                start_at_one(dve, *{0: s_taken + s_msg, 2: s_msg, 3: s_taken}[layer])
                if layer == 0:
                    dve.wait_ge(s_one, 2)
                per_chunk = {0: 1, 2: 2, 3: 1}[layer]
                iota = cst["iota"]
                with dve.Fori(0, G) as i:
                    step = counter(dve, s_ch, i * (QN * per_chunk))
                    bstep = counter(dve, s_basis_ch, i * 10)
                    for q in range(QN):
                        s, m = q % 2, q // 2
                        hf, t0 = q // HQ, (q % HQ) * CT
                        turn = i * HQ + m
                        if q % HQ == 0:
                            dve.wait_ge(s_pay[hf], i * 16 + 16)
                            if layer == 0:
                                ph = pay[:, hf, :, W_A2:W_A2 + 2]
                                sh4 = [P, HT, 2, 4]
                                bstep(nc.vector.tensor_tensor(hat[:, :, :, :], bc(ph, 3, sh4),
                                                              cen[:, :].unsqueeze(1).unsqueeze(1).to_broadcast(sh4), ALU.subtract))
                                flat = hat[:, :, :, :].rearrange("p t a u -> p (t a u)")
                                bstep(nc.vector.scalar_tensor_tensor(out=flat, in0=flat, scalar=-1.0, in1=flat,
                                                                     op0=ALU.mult, op1=ALU.max))
                                bstep(nc.vector.tensor_scalar(flat, flat, -1.5, 1.0, ALU.mult, ALU.add))
                                bstep(nc.vector.tensor_scalar(hat[:, :, :, :], hat[:, :, :, :], 0.0, None, ALU.max))
                                bstep(nc.vector.tensor_tensor(
                                    basis[:, hf, :, :].rearrange("p t (u v) -> p t u v", v=4),
                                    bc(hat[:, :, 0, :], 3, [P, HT, 4, 4]), bc(hat[:, :, 1, :], 2, [P, HT, 4, 4]), ALU.mult))
                        dve.wait_ge(s_sc[s], turn + ONE)
                        here = pay[:, hf, t0:t0 + CT, :]
                        nc.vector.tensor_tensor(hot[:, s, :, :], bc(iota[:, :], 1, [P, CT, P]),
                                                here[:, :, W_SLO:W_SLO + 1].to_broadcast([P, CT, P]),
                                                ALU.is_equal).then_inc(s_hot[s], 1)
                        if layer == 0:
                            dve.wait_ge(s_hd[s], turn + ONE)
                            nc.vector.tensor_tensor(hlo[:, s, :, :], bc(iota[:, :], 1, [P, CT, P]),
                                                    here[:, :, W_DLO:W_DLO + 1].to_broadcast([P, CT, P]),
                                                    ALU.is_equal).then_inc(s_hh[s], 1)
                            nc.vector.tensor_tensor(hhi[:, s, :, :], bc(iota[:, 0:NB], 1, [P, CT, NB]),
                                                    here[:, :, W_DHI:W_DHI + 1].to_broadcast([P, CT, NB]),
                                                    ALU.is_equal).then_inc(s_hh[s], 1)
                        dve.wait_ge(s_gat[s], (turn + 1) * (16 * CT))
                        got = rows[:, s, :, :]
                        if layer == 0:
                            ba = basis[:, hf, t0:t0 + CT, :]
                            ins = nc.vector.tensor_tensor(
                                prod[:, :, :].rearrange("p t (k o) -> p t k o", o=F),
                                got.rearrange("p t (k o) -> p t k o", o=F), bc(ba, 3, [P, CT, F, F]), ALU.mult)
                            ins.then_inc(s_taken[s], 1)
                            dve.wait_ge(s_taken[s], turn + 1 + ONE)
                            nc.vector.tensor_reduce(msg[:, s, :, 0:F], prod[:, :, :].rearrange("p t (k o) -> p t o k", o=F),
                                                    AX.X, ALU.add).then_inc(s_msg[s], 1)
                            dve.wait_ge(s_msg[s], turn + 1 + ONE)
                        else:
                            a8 = here[:, :, W_A8:W_A8 + 8]
                            step(nc.vector.tensor_tensor(
                                prod[:, :, :].rearrange("p t (k o) -> p t k o", o=F),
                                got[:, :, 0:128].rearrange("p t (k o) -> p t k o", o=F), bc(a8, 3, [P, CT, 8, F]), ALU.mult))
                            red = prod[:, :, :].rearrange("p t (k o) -> p t o k", o=F)
                            if layer == 2:
                                step(nc.vector.tensor_reduce(pre[:, s, :, :], red, AX.X, ALU.add))
                                nc.vector.tensor_tensor(msg[:, s, :, :], pre[:, s, :, :], got[:, :, 128:144],
                                                        ALU.add).then_inc(s_msg[s], 1)
                                dve.wait_ge(s_msg[s], turn + 1 + ONE)
                            else:
                                dve.wait_ge(s_msg[s], turn + ONE)
                                nc.vector.tensor_reduce(pre[:, s, :, :], red, AX.X, ALU.add).then_inc(s_pre[s], 1)
                                dve.wait_ge(s_pre[s], turn + 1 + ONE)
                    if layer != 0:
                        assert step.count[0] == QN * per_chunk, step.count
                if layer == 0:
                    dve.wait_ge(s_hf, 1)
                    nc.vector.tensor_copy(hist[0:NB, :], ps_h[0:NB, 0:P])


def sheaf_phase(nc, sh, io, dr, cst, table):
    G, NB = sh.g, sh.nb
    C = table.shape[1]
    CU = 9 * F + 1
    with nc.cleanup_on_exit(), ExitStack() as ctx:
        def sb(name, shape, dt=FP):
            return ctx.enter_context(nc.sbuf_tensor(name + "_L1", shape, dt))

        def pb(name, banks=1):
            return ctx.enter_context(nc.psum_tensor(name + "_L1", [P, 512 * banks], FP))

        def sem(name):
            return nc.alloc_semaphore(f"{name}_L1")

        def two(name):
            return [sem(f"{name}{s}") for s in range(2)]
        tbl = sb("table", [P, NB * C])
        cols = sb("tile_cols", [1, sh.t + 2 * CT], I32)
        pay = sb("pay", [P, 2, HT, PW])
        payi = pay[:, :, :, :].bitcast(I32)
        rows = sb("rows", [P, 2, CT, C])
        hot = sb("hot", [P, HQ, CT, P])
        hotT = sb("hotT", [P, CT * P])
        hid = sb("hid", [P, CT, P])
        hidT = sb("hidT", [P, CT * P])
        w2 = sb("w2", [P, 2 * F])
        b2 = sb("b2", [P, 2, F])
        v = sb("v", [P, CT, 2, F])
        tv = sb("tv", [P, CT, 2, F])
        cur = sb("cur", [P, 2, CT, 2, F])
        sc = sb("sc", [P, 4, CT * 2])
        msg = sb("msg", [P, 2, CT, F])
        dst = sb("dmsg", [P, 2, CT, DW])
        stg = sb("stg", [F, 2, CT * P])
        ps = [pb(f"ps{s}") for s in range(2)]
        ps_o, ps_t, ps_v = pb("ps_o"), pb("ps_t"), pb("ps_v")
        ps_g = pb("ps_g", 2)
        s_pay, s_gat, s_hot, s_msg, s_taken, s_sc, s_ev, s_st, s_dm, s_dsent, s_dfree = (
            two(n) for n in ("payload", "gathered", "onehot", "message", "rows_used", "scattered", "evacuated",
                             "stored", "dst_message", "dst_sent", "dst_free"))
        s_w2, s_w2z, s_dz, s_tbl, s_colz = sem("w2"), sem("w2_zero"), sem("dmsg_zero"), sem("table"), sem("cols_zero")
        s_hotT, s_hotTc, s_src, s_srcread, s_hid, s_hidT, s_hidTc, s_v, s_vread = (
            sem(n) for n in ("hotT", "hotT_copied", "src_rows", "src_rows_read", "hidden", "hiddenT",
                             "hiddenT_copied", "vectors", "vectors_read"))
        s_ch, s_own, s_cur = sem("chain"), sem("own_features"), sem("sent_features")
        s_begun = sem("begun")
        per_chunk = 13

        def half(i, hf):
            return dr["S"][bass.ds(i * (GT * P), GT * P), :].rearrange("(p t) w -> p t w", t=GT)[:, hf * HT:(hf + 1) * HT, :]

        def ahead(i, q, by):
            return (i, q + by) if q + by < QN else (i + 1, q + by - QN)

        with nc.Block() as block:
            @block.scalar
            def _(act):
                act.dma_start(pay[:, 0, :, :], half(0, 0)).then_inc(s_pay[0], 16)
                start_at_one(act, *s_ev, s_hotTc, s_hidTc)

                def copy_hot(n):
                    act.wait_ge(s_src, n + ONE)
                    act.wait_ge(s_hotT, n + 1)
                    act.activation(hotT[:, :], ps_o[:, :], ACT.Copy).then_inc(s_hotTc, 1)

                def relu_hidden(n):
                    act.wait_ge(s_hidT, n + 1)
                    act.activation(hidT[:, :], ps_t[:, :], ACT.Relu).then_inc(s_hidTc, 1)

                copy_hot(0)
                relu_hidden(0)
                copy_hot(1)
                with act.Fori(0, G) as i:
                    for q in range(QN):
                        s, m = q % 2, q // 2
                        n = i * QN + q
                        relu_hidden(n + 1)
                        copy_hot(n + 2)
                        act.wait_ge(s_sc[s], i * HQ + (m + 1) + ONE)
                        act.wait_ge(s_st[s], (i * HQ + m) * 16 + ONE)
                        act.activation(stg[:, s, :], ps[s][0:F, :], ACT.Copy).then_inc(s_ev[s], 1)
                        if q == 1:
                            act.wait_ge(s_dfree[1], i * HQ + ONE)
                            act.dma_start(pay[:, 1, :, :], half(i, 1)).then_inc(s_pay[1], 16)
                        if q == HQ + 1:
                            act.wait_ge(s_dfree[0], i * HQ + (HQ // 2 + 1) + ONE)
                            act.dma_start(pay[:, 0, :, :], half(i + 1, 0)).then_inc(s_pay[0], 16)
                act.wait_ge(s_pay[0], 16 * (G + 1))
                act.wait_ge(s_pay[1], 16 * G)

            @block.gpsimd
            def _(gp):
                def gather(i, q):
                    s, m = q % 2, q // 2
                    if q == 0 or q == HQ:
                        gp.wait_ge(s_pay[q // HQ], i * 16 + 16)
                    gp.wait_ge(s_taken[s], i * HQ + m + ONE)
                    gp.sem_inc(s_begun, 1)
                    hf, t0 = q // HQ, (q % HQ) * CT
                    for k in range(CT):
                        gp.indirect_dma_start(
                            out=rows[:, s, k, :], out_offset=None, in_=table,
                            in_offset=bass.IndirectOffsetOnAxis(ap=payi[:, hf, t0 + k, W_DST:W_DST + 1], axis=0)
                        ).then_inc(s_gat[s], 16)

                gp.memset(cols[:, :], 0).then_inc(s_colz, 1)
                start_at_one(gp, *s_dfree)
                gp.memset(dst[:, :, :, :], 0.0).then_inc(s_dz, 1)
                gather(0, 0)
                gather(0, 1)
                with gp.Fori(0, G) as i:
                    for q in range(QN):
                        gather(*ahead(i, q, 2))
                        s, m = q % 2, q // 2
                        hf, t0 = q // HQ, (q % HQ) * CT
                        gp.wait_ge(s_dm[s], i * HQ + (m + 1))
                        gp.sem_inc(s_begun, 1)
                        for k in range(CT):
                            gp.indirect_dma_start(
                                out=dr["D"], out_offset=bass.IndirectOffsetOnAxis(
                                    ap=payi[:, hf, t0 + k, W_DROW:W_DROW + 1], axis=0),
                                in_=dst[:, s, k, :], in_offset=None, bounds_check=sh.t * P - 1,
                                oob_is_err=False).then_inc(s_dsent[s], 16)
                        for d in ([q - 1] if q else []) + ([q] if q == QN - 1 else []):
                            gp.wait_ge(s_dsent[d % 2], (i * HQ + (d // 2 + 1)) * (16 * CT))
                            gp.sem_inc(s_dfree[d % 2], 1)
                for s in range(2):
                    gp.wait_ge(s_gat[s], 16 * CT * (HQ * G + 1))

            @block.sync
            def _(sp):
                sp.dma_start(tbl[:, :].rearrange("p (b c) -> p b c", c=C),
                             table.rearrange("(b l) c -> l b c", l=P)).then_inc(s_tbl, 16)
                sp.wait_ge(s_colz, 1)
                sp.dma_start(cols[:, 0:sh.t], dr["cols"]).then_inc(s_tbl, 16)
                sp.wait_ge(s_w2z, 1)
                for k in range(2):
                    sp.dma_start(w2[64 * k:64 * k + 64, F * k:F * k + F], io["w2t"]).then_inc(s_w2, 16)
                    sp.dma_start(b2[:, k, :], io["b2"].partition_broadcast(P)).then_inc(s_w2, 16)
                start_at_one(sp, *s_st)
                with sp.Fori(0, G) as i:
                    for q in range(QN):
                        s, m = q % 2, q // 2
                        sp.wait_ge(s_ev[s], i * HQ + (m + 1) + ONE)
                        sums = dr["P"][bass.ds(i * GT + q * CT, CT), 0:F * P].rearrange("t (f l) -> f t l", l=P)
                        sp.dma_start(sums, stg[:, s, :].rearrange("f (t l) -> f t l", l=P)).then_inc(s_st[s], 16)
                for s in range(2):
                    sp.wait_ge(s_st[s], 16 * HQ * G + ONE)

            @block.tensor
            def _(pe):
                start_at_one(pe, *s_sc, s_src)
                pe.wait_ge(s_w2, 64)
                pe.wait_ge(s_tbl, 32)
                regs = [pe.alloc_register(f"tile_col{k}") for k in range(CT)]

                def turn_one_hots(i, q):
                    s, m = q % 2, q // 2
                    n = i * QN + q
                    pe.load(regs, cols[0:1, bass.ds(n * CT, CT)])
                    at = [pe.snap(r, min_val=0, max_val=(NB - 1) * C) for r in regs]
                    pe.wait_ge(s_hot[s], i * HQ + (m + 1))
                    pe.wait_ge(s_hotTc, n + ONE)
                    for k in range(CT):
                        last = nc.tensor.transpose(ps_o[:, k * P:(k + 1) * P], hot[:, q % HQ, k, :], cst["ident"][:, :])
                    last.then_inc(s_hotT, 1)
                    return at

                def src_rows(i, q, at):
                    n = i * QN + q
                    pe.wait_ge(s_hotTc, n + 1 + ONE)
                    pe.wait_ge(s_srcread, n + ONE)
                    for k in range(CT):
                        to = (k // 2) * 512 + (k % 2) * CU
                        last = nc.tensor.matmul(ps_g[:, to:to + CU], hotT[:, k * P:(k + 1) * P],
                                                tbl[:, bass.ds(at[k], CU)], start=True, stop=True)
                    last.then_inc(s_src, 1)

                def vectors(i, q):
                    n = i * QN + q
                    pe.wait_ge(s_hid, n + 1)
                    pe.wait_ge(s_hidTc, n + ONE)
                    for k in range(CT):
                        last = nc.tensor.transpose(ps_t[:, k * P:(k + 1) * P], hid[:, k, :], cst["ident"][:, :])
                    last.then_inc(s_hidT, 1)
                    at = turn_one_hots(*ahead(i, q, 1))
                    pe.wait_ge(s_hidTc, n + 1 + ONE)
                    pe.wait_ge(s_vread, n + ONE)
                    for k in range(CT):
                        last = nc.tensor.matmul(ps_v[:, k * 2 * F:(k + 1) * 2 * F], hidT[:, k * P:(k + 1) * P],
                                                w2[:, :], start=True, stop=True)
                    last.then_inc(s_v, 1)
                    src_rows(*ahead(i, q, 1), at)

                src_rows(0, 0, turn_one_hots(0, 0))
                vectors(0, 0)
                with pe.Fori(0, G) as i:
                    for q in range(QN):
                        s, m = q % 2, q // 2
                        vectors(*ahead(i, q, 1))
                        pe.wait_ge(s_msg[s], i * HQ + (m + 1) + ONE)
                        pe.wait_ge(s_ev[s], i * HQ + m + ONE)
                        for k in range(CT):
                            last = nc.tensor.matmul(ps[s][0:F, k * P:(k + 1) * P], msg[:, s, k, :], hot[:, q % HQ, k, :],
                                                    start=True, stop=True)
                        last.then_inc(s_sc[s], 1)

            @block.vector
            def _(dve):
                start_at_one(dve, *s_taken, *s_msg, s_vread, s_srcread)
                nc.vector.memset(w2[:, :], 0.0).then_inc(s_w2z, 1)
                dve.wait_ge(s_dz, 1)
                dve.wait_ge(s_w2, 64)
                iota = cst["iota"]
                sh4 = [P, CT, 2, F]

                def one_hots(i, q):
                    s, m = q % 2, q // 2
                    hf, t0 = q // HQ, (q % HQ) * CT
                    if q % HQ == 0:
                        dve.wait_ge(s_pay[hf], i * 16 + 16)
                    nc.vector.tensor_tensor(hot[:, q % HQ, :, :], bc(iota[:, :], 1, [P, CT, P]),
                                            pay[:, hf, t0:t0 + CT, W_SLO:W_SLO + 1].to_broadcast([P, CT, P]),
                                            ALU.is_equal).then_inc(s_hot[s], 1)

                def hidden(i, q):
                    s, m = q % 2, q // 2
                    n = i * QN + q
                    dve.wait_ge(s_gat[s], (i * HQ + (m + 1)) * (16 * CT))
                    dve.wait_ge(s_src, n + 1 + ONE)
                    D = rows[:, s, :, :].rearrange("p (a b) c -> p a b c", b=2)
                    S = ps_g[:, :].rearrange("p (a r) -> p a r", a=2)[:, :, 0:2 * CU].rearrange("p a (b c) -> p a b c", c=CU)
                    h4 = hid[:, :, :].rearrange("p (a b) c -> p a b c", b=2)
                    nc.vector.tensor_tensor(h4[:, :, :, 0:64], S[:, :, :, 0:64], D[:, :, :, 64:128], ALU.add)
                    nc.vector.tensor_tensor(h4[:, :, :, 64:128], D[:, :, :, 0:64], S[:, :, :, 64:128],
                                            ALU.add).then_inc(s_hid, 1)
                    c5 = cur[:, s, :, :, :].rearrange("p (a b) e f -> p a b e f", b=2)
                    nc.vector.tensor_tensor(c5[:, :, :, 0, :], D[:, :, :, 128:144],
                                            D[:, :, :, 144:145].to_broadcast([P, 2, 2, F]),
                                            ALU.mult).then_inc(s_taken[s], 1)
                    nc.vector.tensor_copy(c5[:, :, :, 1, :], S[:, :, :, 128:144]).then_inc(s_own, 1)
                    nc.vector.tensor_copy(sc[:, 3, 0:CT].rearrange("p (a b) -> p a b", b=2).unsqueeze(3),
                                          S[:, :, :, 144:145]).then_inc(s_srcread, 1)
                    one_hots(*ahead(i, q, 1))
                    dve.wait_ge(s_own, n + 1)
                    dve.wait_ge(s_srcread, n + 1 + ONE)
                    nc.vector.tensor_tensor(cur[:, s, :, 1, :], cur[:, s, :, 1, :],
                                            bc(sc[:, 3, 0:CT], 2, [P, CT, F]), ALU.mult).then_inc(s_cur, 1)

                one_hots(0, 0)
                hidden(0, 0)
                dve.wait_ge(s_cur, 1)
                with dve.Fori(0, G) as i:
                    step = counter(dve, s_ch, i * (QN * per_chunk))
                    for q in range(QN):
                        s, m = q % 2, q // 2
                        n = i * QN + q
                        turn = i * HQ + m
                        hf, t0 = q // HQ, (q % HQ) * CT
                        hidden(*ahead(i, q, 1))
                        now = cur[:, s, :, :, :]
                        dve.wait_ge(s_v, n + 1)
                        dve.wait_ge(s_cur, n + 2)
                        nc.vector.tensor_tensor(v[:, :, :, :], ps_v[:, 0:CT * 2 * F].rearrange("p (t a f) -> p t a f", a=2, f=F),
                                                bc(b2[:, :, :], 1, sh4), ALU.add).then_inc(s_vread, 1)
                        dve.wait_ge(s_vread, n + 1 + ONE)
                        step(nc.vector.tensor_tensor(tv[:, :, :, :], v[:, :, :, :], v[:, :, :, :], ALU.mult))
                        w = [sc[:, k, :].rearrange("p (t a) -> p t a", a=2) for k in range(3)]
                        step(nc.vector.tensor_reduce(w[0], tv[:, :, :, :], AX.X, ALU.add))
                        step(nc.vector.tensor_scalar(sc[:, 0, :], sc[:, 0, :], 1e-24, 0.5, ALU.max, ALU.mult))
                        step(nc.vector.reciprocal(sc[:, 1, :], sc[:, 0, :]))
                        dve.wait_ge(s_sc[s], turn + ONE)
                        dve.wait_ge(s_dfree[s], turn + ONE)
                        vv = [v[:, :, a, :] for a in range(2)]
                        cc = [w[1][:, :, a] for a in range(2)]
                        for near in range(2):
                            order = (0, 1) if near else (1, 0)
                            for a in range(2):
                                ins = nc.vector.tensor_tensor(tv[:, :, a, :], vv[order[a]], now[:, :, a, :], ALU.mult)
                            step(ins)
                            step(nc.vector.tensor_reduce(w[2], tv[:, :, :, :], AX.X, ALU.add))
                            for a in range(2):
                                ins = nc.vector.tensor_tensor(w[0][:, :, a], w[2][:, :, a], cc[order[a]], ALU.mult)
                            step(ins)
                            for a in range(2):
                                ins = nc.vector.tensor_tensor(tv[:, :, a, :], vv[order[a]], bc(w[0][:, :, a], 2, [P, CT, F]), ALU.mult)
                            step(ins)
                            if not near:
                                step(nc.vector.tensor_tensor(now, now, tv[:, :, :, :], ALU.subtract))
                        nc.vector.tensor_tensor(msg[:, s, :, :], now[:, :, 0, :], tv[:, :, 0, :], ALU.subtract).then_inc(s_msg[s], 1)
                        nc.vector.tensor_copy(dst[:, s, :, F:F + 1], pay[:, hf, t0:t0 + CT, W_DLO:W_DLO + 1])
                        nc.vector.tensor_tensor(dst[:, s, :, 0:F], now[:, :, 1, :], tv[:, :, 1, :], ALU.subtract).then_inc(s_dm[s], 1)
                        dve.wait_ge(s_dm[s], turn + 1)
                    assert step.count[0] == QN * per_chunk, step.count


def dst_phase(nc, sh, dr, cst):
    G = sh.g
    tag = "_D"
    with nc.cleanup_on_exit(), ExitStack() as ctx:
        def sb(name, shape, dt=FP):
            return ctx.enter_context(nc.sbuf_tensor(name + tag, shape, dt))

        def two(name):
            return [nc.alloc_semaphore(f"{name}{s}{tag}") for s in range(2)]
        pay = sb("pay", [P, 2, HT, DW])
        hot = sb("hot", [P, 2, CT, P])
        stg = sb("stg", [F, HQ, CT * P])
        ps = [ctx.enter_context(nc.psum_tensor(f"ps{s}{tag}", [P, 512], FP)) for s in range(2)]
        s_pay, s_hot, s_sc, s_ev = (two(n) for n in ("payload", "onehot", "scattered", "evacuated"))
        s_st = [nc.alloc_semaphore(f"stored{k}{tag}") for k in range(HQ)]

        def half(i, hf):
            return dr["D"][bass.ds(i * (GT * P), GT * P), :].rearrange("(p t) w -> p t w", t=GT)[:, hf * HT:(hf + 1) * HT, :]

        with nc.Block() as block:
            @block.scalar
            def _(act):
                for hf in range(2):
                    act.dma_start(pay[:, hf, :, :], half(0, hf)).then_inc(s_pay[hf], 16)
                start_at_one(act, *s_ev)
                with act.Fori(0, G) as i:
                    for q in range(QN):
                        s, m = q % 2, q // 2
                        act.wait_ge(s_sc[s], i * HQ + (m + 1) + ONE)
                        act.wait_ge(s_st[q % HQ], (i * 2 + q // HQ) * 16 + ONE)
                        act.activation(stg[:, q % HQ, :], ps[s][0:F, :], ACT.Copy).then_inc(s_ev[s], 1)
                        if q in (HQ - 1, QN - 1):
                            act.dma_start(pay[:, q // HQ, :, :], half(i + 1, q // HQ)).then_inc(s_pay[q // HQ], 16)
                for hf in range(2):
                    act.wait_ge(s_pay[hf], 16 * (G + 1))

            @block.sync
            def _(sp):
                start_at_one(sp, *s_st)
                with sp.Fori(0, G) as i:
                    for q in range(QN):
                        s, m = q % 2, q // 2
                        sp.wait_ge(s_ev[s], i * HQ + (m + 1) + ONE)
                        sums = dr["P"][bass.ds(i * GT + q * CT, CT), 0:F * P].rearrange("t (f l) -> f t l", l=P)
                        sp.dma_start(sums, stg[:, q % HQ, :].rearrange("f (t l) -> f t l", l=P)).then_inc(s_st[q % HQ], 16)
                for k in range(HQ):
                    sp.wait_ge(s_st[k], 16 * 2 * G + ONE)

            @block.tensor
            def _(pe):
                start_at_one(pe, *s_sc)
                with pe.Fori(0, G) as i:
                    for q in range(QN):
                        s, m = q % 2, q // 2
                        hf, t0 = q // HQ, (q % HQ) * CT
                        pe.wait_ge(s_hot[s], i * HQ + (m + 1))
                        pe.wait_ge(s_ev[s], i * HQ + m + ONE)
                        for k in range(CT):
                            last = nc.tensor.matmul(ps[s][0:F, k * P:(k + 1) * P], pay[:, hf, t0 + k, 0:F], hot[:, s, k, :],
                                                    start=True, stop=True)
                        last.then_inc(s_sc[s], 1)

            @block.vector
            def _(dve):
                with dve.Fori(0, G) as i:
                    for q in range(QN):
                        s, m = q % 2, q // 2
                        hf, t0 = q // HQ, (q % HQ) * CT
                        if q % HQ == 0:
                            dve.wait_ge(s_pay[hf], i * 16 + 16)
                        dve.wait_ge(s_sc[s], i * HQ + m + ONE)
                        nc.vector.tensor_tensor(hot[:, s, :, :], bc(cst["iota"][:, :], 1, [P, CT, P]),
                                                pay[:, hf, t0:t0 + CT, F:F + 1].to_broadcast([P, CT, P]),
                                                ALU.is_equal).then_inc(s_hot[s], 1)


def combine_phase(nc, sh, tag, own, dr, cst, M, finish):
    G, NB = sh.g, sh.nb
    n_bank = -(-M * P // 512)
    with nc.cleanup_on_exit(), ExitStack() as ctx:
        part = ctx.enter_context(nc.sbuf_tensor("part" + tag, [P, 2, M * P], FP))
        who = ctx.enter_context(nc.sbuf_tensor("who" + tag, [P, NB], FP))
        zero = ctx.enter_context(nc.sbuf_tensor("zero" + tag, [P, 512], FP))
        bank = [ctx.enter_context(nc.psum_tensor(f"bank{k}{tag}", [P, 512], FP)) for k in range(n_bank)]
        s_ld = [nc.alloc_semaphore(f"cb_load{s}{tag}") for s in range(2)]
        s_z, s_who, s_mm, s_fin, s_ch, s_cp = (nc.alloc_semaphore(f"cb_{n}{tag}")
                                         for n in ("zero", "who", "product", "final", "chain", "aux"))
        MH = 8 * P

        def halves(s):
            return (0, MH) if s == 0 else (MH, M * P)
        with nc.Block() as block:
            @block.sync
            def _(sp):
                with sp.Fori(0, G) as i:
                    for s in range(2):
                        lo, hi = halves(s)
                        sp.wait_ge(s_mm, i * 2 + ONE)
                        sp.dma_start(part[0:GT, s, lo:hi], dr["P"][bass.ds(i * GT, GT), lo:hi]).then_inc(s_ld[s], 16)

            @block.gpsimd
            def _(gp):
                gp.memset(zero[:, :], 0.0).then_inc(s_z, 1)

            @block.tensor
            def _(pe):
                pe.wait_ge(s_z, 1)
                start_at_one(pe, s_mm)
                for k in range(n_bank):
                    nc.tensor.matmul(bank[k][0:NB, :], zero[0:GT, 0:NB], zero[0:GT, :], start=True, stop=False)
                with pe.Fori(0, G) as i:
                    pe.wait_ge(s_who, i + 1)
                    for s in range(2):
                        pe.wait_ge(s_ld[s], i * 16 + 16)
                        lo, hi = halves(s)
                        for c in range(lo, hi, 512):
                            n = min(512, hi - c)
                            last = nc.tensor.matmul(bank[c // 512][0:NB, 0:n], who[0:GT, :], part[0:GT, s, c:c + n],
                                                    start=False, stop=False)
                        last.then_inc(s_mm, 1)
                for k in range(n_bank):
                    last = nc.tensor.matmul(bank[k][0:NB, :], zero[0:GT, 0:NB], zero[0:GT, :], start=False, stop=True)
                last.then_inc(s_fin, 1)

            @block.vector
            def _(dve):
                with dve.Fori(0, G) as i:
                    dve.wait_ge(s_mm, i * 2 + ONE)
                    nc.vector.tensor_copy(who[0:GT, :], own[0:GT, bass.ds(i * NB, NB)]).then_inc(s_who, 1)
                dve.wait_ge(s_fin, 1)
                step = counter(dve, s_ch)
                finish(dve, bank, step, s_cp)

            @block.scalar
            def _(act):
                if finish.root is not None:
                    finish.root(act, s_cp)


def bank_view(bank, NB, k):
    return bank[k][0:NB, :].rearrange("p (f l) -> p l f", l=P)


def four(buf, NB, k):
    return buf[0:NB, :].rearrange("p (l f) -> p l f", f=F)[:, :, 4 * k:4 * k + 4]


def gnn(nc, sh, io, out):
    NB, G = sh.nb, sh.g

    def dram(name, shape):
        return nc.dram_tensor(name, shape, FP, kind="Internal").ap()
    dr = {
        "S": dram("edges_src_order", [(sh.t + GT) * P, PW]),
        "D": dram("messages_dst_order", [(sh.t + GT) * P, DW]),
        "P": dram("tile_sums", [sh.t, (F + 1) * P]),
        "cols": nc.dram_tensor("tile_cols", [1, sh.t], I32, kind="Internal").ap(),
    }
    table = [dram(f"table{l}", [sh.npad, c]) for l, c in enumerate((256, C1, 144, 128))]
    with ExitStack() as ctx:
        def sb(name, shape, dt=FP):
            return ctx.enter_context(nc.sbuf_tensor(name, shape, dt))
        cst = {
            "iota": sb("iota", [P, P]), "ident": sb("ident", [P, P]),
            "own_src": sb("own_src", [P, G * NB]), "own_dst": sb("own_dst", [P, G * NB]),
        }
        setup_phase(nc, sh, io, dr, cst)

        x, h, agg = (sb(n, [P, P * F]) for n in ("x", "h", "agg"))
        hist, deg, dinv = (sb(n, [P, P]) for n in ("hist", "deg", "dinv"))
        bias = sb("bias1", [P, P])

        norm_phase(nc, sh, "0", x, h, io=io)
        node_matmul(nc, sh, "_t0", h, [io["w0"]], 256, cst, "table", table[0])
        edge_phase(nc, sh, 0, io, dr, cst, table[0], hist=hist)

        def finish0(dve, bank, step, s_cp):
            for k in range(4):
                step(nc.vector.tensor_tensor(four(x, NB, k), four(x, NB, k), bank_view(bank, NB, k), ALU.add))
            step(nc.vector.tensor_tensor(deg[0:NB, :], hist[0:NB, :], bank[4][0:NB, 0:P], ALU.add))
            nc.vector.tensor_scalar(deg[0:NB, :], deg[0:NB, :], 1e-5, None, ALU.max).then_inc(s_cp, 1)
            dve.wait_ge(s_cp, 2)
            step(nc.vector.reciprocal(dinv[0:NB, :], deg[0:NB, :]))

        def root0(act, s_cp):
            act.wait_ge(s_cp, 1)
            act.activation(deg[0:NB, :], deg[0:NB, :], ACT.Sqrt).then_inc(s_cp, 1)
        finish0.root = root0
        combine_phase(nc, sh, "_c0", cst["own_src"], dr, cst, F + 1, finish0)

        norm_phase(nc, sh, "1", x, h)
        s_bz, s_bl = nc.alloc_semaphore("bias_zero"), nc.alloc_semaphore("bias_load")
        with nc.Block() as block:
            @block.vector
            def _(dve):
                nc.vector.memset(bias[:, :], 0.0).then_inc(s_bz, 1)

            @block.sync
            def _(sp):
                sp.wait_ge(s_bz, 1)
                sp.dma_start(bias[:, 0:64], io["b1"].partition_broadcast(P)).then_inc(s_bl, 16)
                sp.wait_ge(s_bl, 16)
        node_matmul(nc, sh, "_t1", h, [io["w1a"], io["w1b"]], 128, cst, "table", table[1],
                    extra={"bias": bias, "dinv": dinv})
        sheaf_phase(nc, sh, io, dr, cst, table[1])

        def finish1s(dve, bank, step, s_cp):
            for k in range(4):
                step(nc.vector.tensor_copy(four(agg, NB, k), bank_view(bank, NB, k)))
        finish1s.root = None
        combine_phase(nc, sh, "_c1s", cst["own_src"], dr, cst, F, finish1s)
        dst_phase(nc, sh, dr, cst)

        def finish1d(dve, bank, step, s_cp):
            for k in range(4):
                step(nc.vector.tensor_tensor(four(agg, NB, k), four(agg, NB, k), bank_view(bank, NB, k), ALU.add))
            a3 = agg[0:NB, :].rearrange("p (l f) -> p l f", f=F)
            step(nc.vector.tensor_tensor(a3, a3, bc(dinv[0:NB, :], 2, [NB, P, F]), ALU.mult))
            step(nc.vector.tensor_tensor(agg[0:NB, :], agg[0:NB, :], h[0:NB, :], ALU.add))
            step(nc.vector.scalar_tensor_tensor(out=x[0:NB, :], in0=agg[0:NB, :], scalar=0.0, in1=x[0:NB, :],
                                                op0=ALU.max, op1=ALU.add))
        finish1d.root = None
        combine_phase(nc, sh, "_c1d", cst["own_dst"], dr, cst, F, finish1d)

        norm_phase(nc, sh, "2", x, h)
        node_matmul(nc, sh, "_t2", h, [io["w2k"], io["w2b"]], 144, cst, "table", table[2])
        edge_phase(nc, sh, 2, io, dr, cst, table[2])

        def finish2(dve, bank, step, s_cp):
            for k in range(4):
                step(nc.vector.tensor_tensor(four(x, NB, k), four(x, NB, k), bank_view(bank, NB, k), ALU.add))
        finish2.root = None
        combine_phase(nc, sh, "_c2", cst["own_src"], dr, cst, F, finish2)

        norm_phase(nc, sh, "3", x, h)
        node_matmul(nc, sh, "_t3", h, [io["w3"]], 128, cst, "table", table[3])
        edge_phase(nc, sh, 3, io, dr, cst, table[3])
        combine_phase(nc, sh, "_c3", cst["own_src"], dr, cst, F, finish1s)
        u = sb("u", [P, P * F])
        su = sb("silu_u", [P, P * F])
        agg2 = sb("agg2", [P, P * F])
        node_matmul(nc, sh, "_lin", agg, [io["wml"]], F, cst, "copy", agg2, extra=0.25)
        node_matmul(nc, sh, "_upd", h, [io["wupd"]], 256, cst, "upd", u, extra=agg2)
        with nc.Block() as block:
            @block.scalar
            def _(act):
                act.activation(su[0:NB, :], u[0:NB, :], ACT.Silu, scale=1.0 / 16)

            @block.vector
            def _(dve):
                nc.vector.tensor_tensor(x[0:NB, :], x[0:NB, :], h[0:NB, :], ALU.add)
        node_matmul(nc, sh, "_fin", su, [io["wul"]], F, cst, "final", x, extra=0.25)
        s_o = nc.alloc_semaphore("stored_out")
        with nc.Block() as block:
            @block.sync
            def _(sp):
                full = NB - 1
                sp.dma_start(out[0:full * P, :].rearrange("(b l) f -> b (l f)", l=P), x[0:full, :]).then_inc(s_o, 16)
                sp.dma_start(out[full * P:sh.n, :].rearrange("(b l) f -> b (l f)", b=1), x[full:NB, 0:sh.last * F]).then_inc(s_o, 16)
                sp.wait_ge(s_o, 32)


def laid_out(inputs):
    import numpy as np
    c = np.ascontiguousarray
    a = {k: np.asarray(v) for k, v in inputs.items()}
    w1 = a["L1_gnn_W1"]
    return {
        "x": c(a["x"]), "src": c(a["src"]), "dst": c(a["dst"]),
        "edge_attr_2": c(a["edge_attr_2"]), "edge_attr_8": c(a["edge_attr_8"]),
        "w0": c(a["L0_gnn_weight"].reshape(16, 16, 16).transpose(1, 0, 2).reshape(16, 256)),
        "w1a": c(w1[:, 0:16].T), "w1b": c(w1[:, 16:32].T), "b1": c(a["L1_gnn_b1"]),
        "w2t": c(a["L1_gnn_W2"].T), "b2": c(a["L1_gnn_b2"]),
        "w2k": c(a["L2_gnn_kernel"].reshape(8, 16, 16).transpose(2, 0, 1).reshape(16, 128)),
        "w2b": c(a["L2_gnn_bias"].reshape(16, 16).T),
        "w3": c(a["L3_gnn_W_msg_tp"].reshape(16, 128)), "wml": c(a["L3_gnn_W_msg_lin"]),
        "wupd": c(a["L3_gnn_W_upd_tp"].reshape(16, 256)), "wul": c(a["L3_gnn_W_upd_lin"]),
    }


def kernel(**inputs):
    import concourse.bacc as _bacc
    from concourse.bass_utils import run_bass_kernel_spmd as _run

    arrays = laid_out(inputs)
    nc = _bacc.Bacc("TRN2", target_bir_lowering=False, num_devices=1)
    io = {k: nc.dram_tensor(f"in_{k}", v.shape, mybir.dt.from_np(v.dtype), kind="ExternalInput").ap()
          for k, v in arrays.items()}
    n = arrays["x"].shape[0]
    out = nc.dram_tensor("out_nodes", [n, F], FP, kind="ExternalOutput").ap()
    gnn(nc, Shapes(n, arrays["src"].shape[0]), io, out)
    r = _run(nc, [{f"in_{k}": v for k, v in arrays.items()}], core_ids=[0])
    return r.results[0]["out_nodes"]
```

```python
import concourse.bass as bass
from concourse import mybir
from contextlib import ExitStack

FP = mybir.dt.float32
BF = mybir.dt.bfloat16
I32 = mybir.dt.int32
I16 = mybir.dt.int16
ALU = mybir.AluOpType
ACT = mybir.ActivationFunctionType
AX = mybir.AxisListType

P = 128
F = 16
GT = 104
CT = 4
HT = GT // 2
QN = GT // CT
HQ = QN // 2
PW = 16
DW = 20
KT = 25
KS = 5
C1 = 148
MAGIC = 12582912.0
ADD_AT = 3
ONE = 1
OUTSIDE = 1 << 20

W_SLO, W_DLO, W_DST, W_DROW, W_SRC, W_DHI, W_A2, W_A8 = 0, 1, 2, 3, 4, 5, 6, 8


class Shapes:
    def __init__(self, n_nodes, n_edges):
        self.n = n_nodes
        self.e = n_edges
        self.nb = -(-n_nodes // P)
        self.npad = self.nb * P
        self.last = n_nodes - (self.nb - 1) * P
        self.j = n_edges // P
        self.g = -(-(self.j + self.nb) // GT)
        self.t = self.g * GT
        assert n_edges % P == 0 and self.j % (KT * KS) == 0 and self.nb <= P
        turns = self.j // (KT * KS)
        self.parts = next(k for k in (5, 2, 1) if turns % k == 0)


def counter(eng, sem, base=0):
    n = [0]

    def step(ins):
        n[0] += 1
        ins.then_inc(sem, 1)
        eng.wait_ge(sem, base + n[0])
        return n[0]

    step.count = n
    return step


def start_at_one(eng, *sems):
    for s in sems:
        eng.sem_inc(s, ONE)


def bc(ap, axis, shape):
    return ap.unsqueeze(axis).to_broadcast(shape)


def setup_phase(nc, sh, io, dr, cst):
    J, NB, G = sh.j, sh.nb, sh.g
    n_it = J // (KT * KS)
    parts = sh.parts
    PJ = J // parts
    IT = n_it // parts
    src_v = io["src"].rearrange("(p j) -> p j", p=P)
    dst_v = io["dst"].rearrange("(p j) -> p j", p=P)
    a2_v = io["edge_attr_2"].rearrange("(p j) c -> p (j c)", p=P)
    a8_v = io["edge_attr_8"].rearrange("(p j) c -> p (j c)", p=P)
    with nc.cleanup_on_exit(), ExitStack() as ctx:
        def sb(name, shape, dt):
            return ctx.enter_context(nc.sbuf_tensor(name, shape, dt))

        def sem(name):
            return nc.alloc_semaphore("su_" + name)

        key = [sb("key_src", [P, J], I32), sb("key_dst", [P, J], I32)]
        blk = [sb("blk_src", [P, J], BF), sb("blk_dst", [P, J], BF)]
        low = [sb("low_src", [P, J], FP), sb("low_dst", [P, J], FP)]
        pos = sb("pos", [P, 2, PJ], FP)
        slot_t = sb("slot_tile", [P, PJ], FP)
        mask = sb("mask", [P, J], FP)
        scan = sb("scan", [P, J], FP)
        row = [sb("row_src", [P, J], I32), sb("row_dst", [P, J], I32)]
        slot = [mask[:, :].bitcast(BF)[:, k * J:(k + 1) * J] for k in range(2)]
        NE = -(-NB // (2 * IT)) * (2 * IT)
        pairs = NE // (2 * IT)
        assert NE <= P
        NA = NE // 3
        cnt = sb("cnt", [P, 2 * NE], FP)
        tiles = sb("tiles", [P, 2 * NE], FP)
        base = sb("base", [P, 2 * NE], FP)
        before = sb("before", [P, 2, P + 1], FP)
        tri = sb("tri", [P, P], FP)
        ones = sb("ones", [P, P], FP)
        tno = sb("tile_no", [P, G], FP)
        nblk = sb("blocks_before_tile", [P, G], FP)
        tcol = sb("tile_col", [P, G], I32)
        fs = sb("fill_src", [P, GT * PW], FP)
        fd = sb("fill_dst", [P, HT * DW], FP)
        a2 = sb("a2_in", [P, KS, KT * 2], FP)
        a8 = sb("a8_in", [P, KS, KT * 8], FP)
        rows = sb("rows", [P, KS, KT, PW], FP)
        idx = sb("row_idx", [P, KS, KT], I32)
        ps_tot = ctx.enter_context(nc.psum_tensor("ps_tot", [P, 512], FP))
        ps_pre = ctx.enter_context(nc.psum_tensor("ps_pre", [P, 512], FP))

        s_key = [sem("key_src"), sem("key_dst")]
        s_fillc = sem("fill_const")
        s_tcol, s_tcolst = sem("tile_col"), sem("tile_col_stored")
        s_filled = sem("filled")
        s_const = sem("const")
        s_sum = sem("sums")
        s_dve = sem("dve_chain")
        s_cl = sem("count_loop")
        s_cla = sem("count_loop_act")
        s_prep = sem("keys_split")
        s_cp, s_mask = ([sem(f"{n}{k}") for k in range(2)] for n in ("placed", "masked"))
        s_abs = sem("distance")
        s_scan, s_part = sem("scanned"), sem("part_chain")
        s_begun, s_begun_d, s_begun_a = sem("begun_pool"), sem("begun_dve"), sem("begun_act")
        s_attr = [sem(f"attr{s}") for s in range(KS)]
        s_put = [sem(f"words_dve{s}") for s in range(KS)]
        s_puta = [sem(f"words_act{s}") for s in range(KS)]
        s_sent = [sem(f"rows_sent{s}") for s in range(KS)]
        s_free = [sem(f"rows_free{s}") for s in range(KS)]

        with nc.Block() as block:
            @block.sync
            def _(sp):
                sp.dma_start(key[0][:, :], src_v).then_inc(s_key[0], 16)
                sp.dma_start(key[1][:, :], dst_v).then_inc(s_key[1], 16)
                sp.wait_ge(s_fillc, 4)
                sp.dma_start(dr["S"].rearrange("(p g r) w -> p g (r w)", p=P, r=GT),
                             fs[:, :].unsqueeze(1).to_broadcast([P, G + 1, GT * PW])).then_inc(s_filled, 16)
                sp.dma_start(dr["D"].rearrange("(p g r) w -> p g (r w)", p=P, r=HT),
                             fd[:, :].unsqueeze(1).to_broadcast([P, 2 * (G + 1), HT * DW])).then_inc(s_filled, 16)
                sp.wait_ge(s_const, 1)
                for c in range(0, (F + 1) * P, P):
                    sp.dma_start(dr["P"][0:GT, c:c + P], cst["zero"][0:GT, 0:P]).then_inc(s_filled, 16)
                with sp.Fori(0, n_it) as i:
                    for s in range(KS):
                        sp.wait_ge(s_puta[s], i * 2 + ONE)
                        at = i * (KS * KT) + s * KT
                        sp.dma_start(a2[:, s, :], a2_v[:, bass.ds(at * 2, KT * 2)]).then_inc(s_attr[s], 16)
                        sp.dma_start(a8[:, s, :], a8_v[:, bass.ds(at * 8, KT * 8)]).then_inc(s_attr[s], 16)
                sp.wait_ge(s_tcol, 1)
                sp.dma_start(dr["cols"].rearrange("a (g t) -> (a t) g", t=GT), tcol[0:GT, :],
                             allow_slow_non_contiguous=True).then_inc(s_tcolst, 16)
                sp.wait_ge(s_tcolst, 16)

            @block.gpsimd
            def _(gp):
                gp.memset(fs[:, :], 0.0).then_inc(s_fillc, 1)
                gp.memset(fd[:, :], 0.0).then_inc(s_fillc, 1)
                gp.wait_ge(s_fillc, 2)
                fs_w = fs[:, :].rearrange("p (r w) -> p r w", w=PW)
                gp.memset(fs_w[:, :, W_SLO:W_DLO + 1], -1.0)
                gp.memset(fs_w.bitcast(I32)[:, :, W_DROW:W_DROW + 1], OUTSIDE).then_inc(s_fillc, 1)
                gp.memset(fd[:, :].rearrange("p (r w) -> p r w", w=DW)[:, :, F:F + 1], -1.0).then_inc(s_fillc, 1)
                gp.iota(cst["iota"][:, :], pattern=[[1, P]], base=0, channel_multiplier=0,
                        allow_small_or_imprecise_dtypes=True)
                gp.iota(tno[:, :], pattern=[[GT, G]], base=0, channel_multiplier=1,
                        allow_small_or_imprecise_dtypes=True)
                gp.memset(cst["own_src"][:, 0:NB], 0.0)
                gp.memset(cst["own_dst"][:, 0:NB], 0.0)
                gp.memset(ones[:, :], 1.0)
                gp.memset(cst["zero"][:, :], 0.0)
                gp.memset(cst["ident"][:, :], 0.0)
                gp.memset(before[:, :, :], 0.0).then_inc(s_const, 1)
                gp.wait_ge(s_const, 1)
                gp.affine_select(out=cst["ident"][:, :], in_=cst["ident"][:, :], compare_op=ALU.not_equal, fill=1.0,
                                 base=0, pattern=[[-1, P]], channel_multiplier=1)
                gp.affine_select(out=tri[:, :], in_=ones[:, :], compare_op=ALU.is_gt, fill=0.0,
                                 base=0, pattern=[[1, P]], channel_multiplier=-1).then_inc(s_const, 1)
                gp.wait_ge(s_filled, 32 + 16 * (F + 1))
                start_at_one(gp, *s_free)
                with gp.Fori(0, n_it) as i:
                    for s in range(KS):
                        gp.wait_ge(s_put[s], i + 1)
                        gp.wait_ge(s_puta[s], i * 2 + 2 + ONE)
                        gp.sem_inc(s_begun, 1)
                        for k in range(KT):
                            gp.indirect_dma_start(
                                out=dr["S"], out_offset=bass.IndirectOffsetOnAxis(ap=idx[:, s, k:k + 1], axis=0),
                                in_=rows[:, s, k, :], in_offset=None).then_inc(s_sent[s], 16)
                        for done in ([s - 1] if s else []) + ([s] if s == KS - 1 else []):
                            gp.wait_ge(s_sent[done], (i + 1) * (16 * KT))
                            gp.sem_inc(s_free[done], 1)

            @block.tensor
            def _(pe):
                pe.wait_ge(s_const, 2)
                pe.wait_ge(s_cl, 2 * NE - NA)
                pe.wait_ge(s_cla, 2 * NA)
                nc.tensor.matmul(ps_tot[:, 0:2 * NE], ones[:, :], cnt[:, :], start=True, stop=True)
                nc.tensor.matmul(ps_pre[:, 0:2 * NE], tri[:, :], cnt[:, :], start=True, stop=True).then_inc(s_sum, 1)

            @block.scalar
            def _(act):
                act.wait_ge(s_prep, 1)
                with act.Fori(0, NA) as b:
                    loop = counter(act, s_cla, b * 2)
                    loop(act.activation(slot[0], blk[1][:, :], ACT.Abs, bias=cst["iota"][:, bass.ds(b + (NE - NA), 1)], scale=-1.0))
                    act.sem_inc(s_begun_a, 1)
                    loop(act.activation(slot[0], slot[0], ACT.Relu, bias=1.0, scale=-1.0,
                                        accum_out=cnt[:, bass.ds(b + (2 * NE - NA), 1)]))
                start_at_one(act, *s_puta)

                def masks(part, turn):
                    for o in range(2):
                        with act.Fori(0, pairs) as j:
                            for k in range(2):
                                done = (part * IT + turn) * (2 * pairs) + o * pairs + j
                                act.wait_ge(s_cp[k], done + ONE)
                                act.sem_inc(s_begun_a, 1)
                                act.activation(slot[k][:, 0:PJ], blk[o][:, bass.ds(part * PJ, PJ)], ACT.Abs,
                                               bias=cst["iota"][:, bass.ds((turn * pairs + j) * 2 + k, 1)],
                                               scale=-1.0).then_inc(s_abs, 1)
                                act.wait_ge(s_abs, done * 2 + (k + 1))
                                act.activation(slot[k][:, 0:PJ], slot[k][:, 0:PJ], ACT.Relu, bias=1.0,
                                               scale=-1.0).then_inc(s_mask[k], 1)

                def attributes(part, turn):
                    i = part * IT + turn
                    for s in range(KS):
                        act.wait_ge(s_attr[s], i * 32 + 32)
                        act.wait_ge(s_free[s], i + ONE)
                        act.activation(rows[:, s, :, W_A2:W_A2 + 2],
                                       a2[:, s, :].rearrange("p (k c) -> p k c", c=2), ACT.Copy).then_inc(s_puta[s], 1)
                        act.activation(rows[:, s, :, W_A8:W_A8 + 8],
                                       a8[:, s, :].rearrange("p (k c) -> p k c", c=8), ACT.Copy).then_inc(s_puta[s], 1)

                with act.Fori(0, IT) as t:
                    masks(0, t)
                with act.Fori(0, parts - 1) as part:
                    with act.Fori(0, IT) as t:
                        masks(part + 1, t)
                        attributes(part, t)
                with act.Fori(0, IT) as t:
                    attributes(parts - 1, t)

            @block.vector
            def _(dve):
                step = counter(dve, s_dve)
                step(nc.vector.memset(base[:, :], 0.0))
                tmp = mask[:, :].bitcast(I32)
                for o in range(2):
                    dve.wait_ge(s_key[o], 16)
                    step(nc.vector.tensor_scalar(tmp, key[o][:, :], 7, None, ALU.arith_shift_right))
                    step(nc.vector.tensor_copy(blk[o][:, :], tmp))
                    step(nc.vector.tensor_scalar(tmp, key[o][:, :], P - 1, None, ALU.bitwise_and))
                    step(nc.vector.tensor_copy(low[o][:, :], tmp))
                dve.wait_ge(s_const, 2)
                dve.sem_inc(s_prep, 1)
                equal = scan[:, :].bitcast(BF)[:, 0:J]
                for o, n in enumerate((NE, NE - NA)):
                    with dve.Fori(0, n) as b:
                        loop = counter(dve, s_cl, b + o * NE)
                        loop(nc.vector.tensor_scalar(equal, blk[o][:, :], cst["iota"][:, bass.ds(b, 1)], 0.0,
                                                     ALU.is_equal, ALU.add, accum_out=cnt[:, bass.ds(b + o * NE, 1)]))
                dve.wait_ge(s_sum, 1)
                step(nc.vector.tensor_scalar(tiles[:, :], ps_tot[:, 0:2 * NE], (P - 1) / 2, 1.0 / P, ALU.add, ALU.mult))
                step(nc.vector.tensor_scalar(tiles[:, :], tiles[:, :], MAGIC, -MAGIC, ALU.add, ALU.add))
                for o in range(2):
                    part = tiles[:, o * NE:o * NE + NB]
                    step(nc.vector.tensor_tensor_scan(before[:, o, 1:NB + 1], part, part, 0.0, ALU.add, ALU.max))
                    step(nc.vector.scalar_tensor_tensor(out=base[:, o * NE:o * NE + NB], in0=before[:, o, 0:NB],
                                                        scalar=float(P), in1=ps_pre[:, o * NE:o * NE + NB],
                                                        op0=ALU.mult, op1=ALU.add))
                start_at_one(dve, *s_cp)

                def ranks(part, turn):
                    for o in range(2):
                        with dve.Fori(0, pairs) as j:
                            for k in range(2):
                                done = (part * IT + turn) * (2 * pairs) + o * pairs + j
                                first = base[:, bass.ds((turn * pairs + j) * 2 + (k + o * NE), 1)]
                                dve.wait_ge(s_mask[k], done + 1)
                                nc.vector.tensor_tensor_scan(scan[:, 0:PJ], slot[k][:, 0:PJ], slot[k][:, 0:PJ],
                                                             first, ALU.add, ALU.max).then_inc(s_scan, 1)
                                dve.wait_ge(s_scan, done * 4 + (2 * k + 1))
                                dve.sem_inc(s_begun_d, 1)
                                nc.vector.tensor_copy(first, scan[:, PJ - 1:PJ]).then_inc(s_scan, 1)
                                nc.vector.copy_predicated(pos[:, o, :], slot[k][:, 0:PJ].bitcast(I16),
                                                          scan[:, 0:PJ]).then_inc(s_cp[k], 1)
                                dve.wait_ge(s_scan, done * 4 + (2 * k + 2))
                                dve.wait_ge(s_cp[k], done + 1 + ONE)

                def clear(part):
                    pstep = counter(dve, s_part, part * 17)
                    pstep(nc.vector.memset(pos[:, :, :], 0.0))
                    dve.sem_inc(s_begun_d, 1)

                def rows_of(part):
                    pstep = counter(dve, s_part, part * 17 + 1)
                    t = slot_t[:, :]
                    for o in range(2):
                        at = pos[:, o, :]
                        pstep(nc.vector.tensor_scalar(t, at, -(P + 1) / 2, 1.0 / P, ALU.add, ALU.mult))
                        pstep(nc.vector.tensor_scalar(t, t, MAGIC, -MAGIC, ALU.add, ALU.add))
                        pstep(nc.vector.scalar_tensor_tensor(out=at, in0=t, scalar=-float(P), in1=at,
                                                             op0=ALU.mult, op1=ALU.add))
                        pstep(nc.vector.scalar_tensor_tensor(out=at, in0=at, scalar=float(GT), in1=t,
                                                             op0=ALU.mult, op1=ALU.add))
                        pstep(nc.vector.tensor_scalar(t, t, -(GT - 1) / 2, 1.0 / GT, ALU.add, ALU.mult))
                        pstep(nc.vector.tensor_scalar(t, t, MAGIC, -MAGIC, ALU.add, ALU.add))
                        pstep(nc.vector.scalar_tensor_tensor(out=at, in0=t, scalar=float((P - 1) * GT), in1=at,
                                                             op0=ALU.mult, op1=ALU.add))
                        pstep(nc.vector.tensor_scalar(row[o][:, bass.ds(part * PJ, PJ)], at, -float(GT), None, ALU.add))
                    dve.sem_inc(s_begun_d, 1)

                def words(part, turn):
                    i = part * IT + turn
                    for s in range(KS):
                        dve.wait_ge(s_free[s], i + ONE)
                        at = i * (KS * KT) + s * KT
                        r = rows[:, s, :, :]
                        ri = r.bitcast(I32)

                        def col(x):
                            return x[:, bass.ds(at, KT)].unsqueeze(2)
                        nc.vector.tensor_copy(r[:, :, W_SLO:W_SLO + 1], col(low[0][:, :]))
                        nc.vector.tensor_copy(r[:, :, W_DLO:W_DLO + 1], col(low[1][:, :]))
                        nc.vector.tensor_copy(ri[:, :, W_DST:W_DST + 1], col(key[1][:, :]))
                        nc.vector.tensor_copy(ri[:, :, W_DROW:W_DROW + 1], col(row[1][:, :]))
                        nc.vector.tensor_copy(ri[:, :, W_SRC:W_SRC + 1], col(key[0][:, :]))
                        nc.vector.tensor_copy(r[:, :, W_DHI:W_DHI + 1], col(blk[1][:, :]))
                        nc.vector.tensor_copy(idx[:, s, :], row[0][:, bass.ds(at, KT)]).then_inc(s_put[s], 1)

                clear(0)
                with dve.Fori(0, IT) as t:
                    ranks(0, t)
                rows_of(0)
                with dve.Fori(0, parts - 1) as part:
                    clear(part + 1)
                    with dve.Fori(0, IT) as t:
                        ranks(part + 1, t)
                        words(part, t)
                    rows_of(part + 1)
                with dve.Fori(0, IT) as t:
                    words(parts - 1, t)
                dve.wait_ge(s_put[KS - 1], n_it)
                for o, name in enumerate(("own_src", "own_dst")):
                    own = cst[name][0:GT, NB:].rearrange("p (g b) -> p g b", b=NB)
                    tn = tno[0:GT, :].unsqueeze(2).to_broadcast([GT, G, NB])
                    sh3 = [GT, G, NB]
                    past = low[0][0:GT, 0:G * NB].rearrange("p (g b) -> p g b", b=NB)
                    step(nc.vector.tensor_tensor(own, tn, bc(before[0:GT, o, 0:NB], 1, sh3), ALU.is_ge))
                    step(nc.vector.tensor_tensor(past, tn, bc(before[0:GT, o, 1:NB + 1], 1, sh3), ALU.is_ge))
                    step(nc.vector.tensor_tensor(own, own, past, ALU.subtract))
                    if o == 0:
                        step(nc.vector.tensor_reduce(nblk[0:GT, :], past, AX.X, ALU.add))
                        nc.vector.tensor_scalar(tcol[0:GT, :], nblk[0:GT, :], float(NB - 1), float(C1),
                                                ALU.min, ALU.mult).then_inc(s_tcol, 1)


def norm_phase(nc, sh, tag, x, h, io=None):
    NB = sh.nb
    with nc.cleanup_on_exit(), ExitStack() as ctx:
        xc = ctx.enter_context(nc.sbuf_tensor("xc" + tag, [P, P * F], FP))
        sq = ctx.enter_context(nc.sbuf_tensor("sq" + tag, [P, P * F], FP))
        st = ctx.enter_context(nc.sbuf_tensor("st" + tag, [P, 4, P], FP))
        s_x = nc.alloc_semaphore("nx" + tag)
        s_c = nc.alloc_semaphore("nc" + tag)
        s_v = nc.alloc_semaphore("nv" + tag)
        s_r = nc.alloc_semaphore("nr" + tag)
        s_z = nc.alloc_semaphore("nz" + tag)
        x3, c3, q3, h3 = (v[0:NB, :].rearrange("p (l f) -> p l f", f=F) for v in (x, xc, sq, h))
        with nc.Block() as block:
            if io is not None:
                @block.gpsimd
                def _(gp):
                    gp.memset(x[:, :], 0.0).then_inc(s_z, 1)

                @block.sync
                def _(sp):
                    sp.wait_ge(s_z, 1)
                    full = sh.nb - 1
                    sp.dma_start(x[0:full, :], io["x"][0:full * P, :].rearrange("(b l) f -> b (l f)", l=P)).then_inc(s_x, 16)
                    sp.dma_start(x[full:NB, 0:sh.last * F],
                                 io["x"][full * P:sh.n, :].rearrange("(b l) f -> b (l f)", b=1)).then_inc(s_x, 16)

            @block.vector
            def _(dve):
                if io is not None:
                    dve.wait_ge(s_x, 32)
                step = counter(dve, s_c)
                full = [NB, P, F]
                step(nc.vector.tensor_reduce(st[0:NB, 0, :], x3, AX.X, ALU.add))
                step(nc.vector.tensor_scalar(st[0:NB, 0, :], st[0:NB, 0, :], 1.0 / F, None, ALU.mult))
                step(nc.vector.tensor_tensor(c3, x3, bc(st[0:NB, 0, :], 2, full), ALU.subtract))
                step(nc.vector.tensor_tensor(q3, c3, c3, ALU.mult))
                step(nc.vector.tensor_reduce(st[0:NB, 1, :], q3, AX.X, ALU.add))
                nc.vector.tensor_scalar(st[0:NB, 1, :], st[0:NB, 1, :], 1.0 / F, 1e-5, ALU.mult, ALU.add).then_inc(s_v, 1)
                dve.wait_ge(s_r, 1)
                step(nc.vector.reciprocal(st[0:NB, 3, :], st[0:NB, 2, :]))
                step(nc.vector.tensor_tensor(c3, c3, bc(st[0:NB, 3, :], 2, full), ALU.mult))
                step(nc.vector.tensor_scalar(h3, c3, 0.0, None, ALU.max))

            @block.scalar
            def _(act):
                act.wait_ge(s_v, 1)
                act.activation(st[0:NB, 2, :], st[0:NB, 1, :], ACT.Sqrt).then_inc(s_r, 1)


def node_matmul(nc, sh, tag, src, weights, C, cst, mode, out, extra=None):
    NB = sh.nb
    L = 8
    n_pc = 1 if C * L <= 512 else 4
    lp = L // n_pc
    wid = lp * C
    CW = out.shape[1] if mode == "table" else C
    with nc.cleanup_on_exit(), ExitStack() as ctx:
        def sb(name, shape, dt=FP):
            return ctx.enter_context(nc.sbuf_tensor(name + tag, shape, dt))

        def sem(name):
            return nc.alloc_semaphore(f"nm_{name}{tag}")
        wbd = sb("wbd", [P, L * C])
        hs = sb("hs", [P, 2, P])
        hT = sb("hT", [P, 2, P])
        stage = sb("stage", [P, 2, L, CW])
        tp = [ctx.enter_context(nc.psum_tensor(f"tp{q}{tag}", [P, 512], FP)) for q in range(2)]
        pp = [ctx.enter_context(nc.psum_tensor(f"pp{k}{tag}", [P, 512], FP)) for k in range(n_pc)]
        s_z, s_w = sem("zero"), sem("weights")
        s_hs, s_tp, s_hT = ([sem(f"{n}{q}") for q in range(2)] for n in ("slice", "transposed", "features_first"))
        s_pp, s_begun = sem("product"), sem("begun")
        s_out = [sem(f"out{k}") for k in range(n_pc)]
        s_st = [sem(f"stored{q}") for q in range(2)]
        s_ch, s_pad, s_ex = sem("chain"), sem("pad"), sem("extra_cols")
        on_act = mode == "table" and extra is None

        with nc.Block() as block:
            @block.gpsimd
            def _(gp):
                gp.memset(wbd[:, :], 0.0).then_inc(s_z, 1)
                gp.memset(stage[:, :, :, :], 0.0).then_inc(s_pad, 1)

            @block.sync
            def _(sp):
                sp.wait_ge(s_z, 1)
                for k in range(L):
                    at = 0
                    for w in weights:
                        c = w.shape[1]
                        sp.dma_start(wbd[F * k:F * k + F, k * C + at:k * C + at + c], w).then_inc(s_w, 16)
                        at += c
                if mode == "table":
                    start_at_one(sp, *s_st)
                    y = out.rearrange("(b l) c -> b (l c)", l=P)
                    with sp.Fori(0, P // L // 2) as i:
                        for q in range(2):
                            for k in range(n_pc):
                                sp.wait_ge(s_out[k], i * 2 + (q + 1) + ONE)
                            sp.sem_inc(s_begun, 1)
                            if extra is not None:
                                sp.wait_ge(s_ex, i * 4 + (2 * q + 2))
                            sp.dma_start(y[:, bass.ds((i * 2 + q) * (L * CW), L * CW)],
                                         stage[0:NB, q, :, :].rearrange("p l c -> p (l c)")).then_inc(s_st[q], 16)
                    for q in range(2):
                        sp.wait_ge(s_st[q], 16 * (P // L // 2) + ONE)

            @block.tensor
            def _(pe):
                pe.wait_ge(s_w, 16 * L * len(weights))
                start_at_one(pe, *s_tp)
                with pe.Fori(0, P // L // 2) as i:
                    for q in range(2):
                        pe.wait_ge(s_hs[q], i + 1)
                        nc.tensor.transpose(tp[q][:, 0:NB], hs[0:NB, q, :], cst["ident"][0:NB, 0:NB]).then_inc(s_tp[q], 1)
                        pe.wait_ge(s_hT[q], i + 1)
                        for k in range(n_pc):
                            pe.wait_ge(s_out[k], i * 2 + q + ONE)
                            nc.tensor.matmul(pp[k][0:NB, 0:wid], hT[:, q, 0:NB], wbd[:, k * wid:(k + 1) * wid],
                                             start=True, stop=True).then_inc(s_pp, 1)

            @block.scalar
            def _(act):
                if on_act:
                    act.wait_ge(s_pad, 1)
                    start_at_one(act, *s_out[0::2])
                with act.Fori(0, P // L // 2) as i:
                    for q in range(2):
                        act.wait_ge(s_tp[q], i + ONE)
                        act.activation(hs[0:NB, q, :], src[0:NB, bass.ds((i * 2 + q) * (L * F), L * F)],
                                       ACT.Copy).then_inc(s_hs[q], 1)
                        act.wait_ge(s_tp[q], i + 1 + ONE)
                        act.activation(hT[:, q, 0:NB], tp[q][:, 0:NB], ACT.Copy).then_inc(s_hT[q], 1)
                        if on_act:
                            act.wait_ge(s_st[q], i * 16 + ONE)
                            for k in range(0, n_pc, 2):
                                act.wait_ge(s_pp, (i * 2 + q) * n_pc + (k + 1))
                                act.activation(stage[0:NB, q, k * lp:(k + 1) * lp, 0:C],
                                               pp[k][0:NB, 0:wid].rearrange("p (l c) -> p l c", c=C),
                                               ACT.Copy).then_inc(s_out[k], 1)

            @block.vector
            def _(dve):
                dve.wait_ge(s_pad, 1)
                start_at_one(dve, *s_out[1::2], *([] if on_act else s_out[0::2]))
                with dve.Fori(0, P // L // 2) as i:
                    for q in range(2):
                        n = i * 2 + q
                        if mode == "table":
                            dve.wait_ge(s_st[q], i * 16 + ONE)
                        for k in range(1 if on_act else 0, n_pc, 2 if on_act else 1):
                            dve.wait_ge(s_pp, n * n_pc + (k + 1))
                            prod = pp[k][0:NB, 0:wid].rearrange("p (l c) -> p l c", c=C)
                            lo = n * L + k * lp
                            if mode == "table" and extra is None:
                                nc.vector.tensor_copy(stage[0:NB, q, k * lp:(k + 1) * lp, 0:C], prod).then_inc(s_out[k], 1)
                            elif mode == "table":
                                nc.vector.tensor_tensor(stage[0:NB, q, k * lp:(k + 1) * lp, 0:C], prod,
                                                        bc(extra["bias"][0:NB, :], 1, [NB, lp, C]), ALU.add).then_inc(s_out[k], 1)
                            elif mode == "copy":
                                nc.vector.tensor_scalar(out[0:NB, bass.ds(lo * F, lp * F)], pp[k][0:NB, 0:wid], extra, None,
                                                        ALU.mult).then_inc(s_out[k], 1)
                            elif mode == "final":
                                nc.vector.scalar_tensor_tensor(out=out[0:NB, bass.ds(lo * F, lp * F)], in0=pp[k][0:NB, 0:wid],
                                                               scalar=extra, in1=out[0:NB, bass.ds(lo * F, lp * F)],
                                                               op0=ALU.mult, op1=ALU.add).then_inc(s_out[k], 1)
                            else:
                                ag = extra[0:NB, bass.ds(lo * F, lp * F)].rearrange("p (l c) -> p l c", c=F)
                                st4 = stage[0:NB, q, k * lp:(k + 1) * lp, :].rearrange("p l (c o) -> p l c o", o=F)
                                nc.vector.tensor_tensor(st4, pp[k][0:NB, 0:wid].rearrange("p (l c o) -> p l c o", c=F, o=F),
                                                        bc(ag, 3, [NB, lp, F, F]), ALU.mult).then_inc(s_ch, 1)
                                dve.wait_ge(s_ch, n * n_pc + (k + 1))
                                nc.vector.tensor_reduce(
                                    out[0:NB, bass.ds(lo * F, lp * F)].rearrange("p (l c) -> p l c", c=F),
                                    stage[0:NB, q, k * lp:(k + 1) * lp, :].rearrange("p l (c o) -> p l o c", o=F),
                                    AX.X, ALU.add).then_inc(s_out[k], 1)
                        if mode == "table" and extra is not None:
                            nc.vector.tensor_copy(stage[0:NB, q, :, C:C + F],
                                                  src[0:NB, bass.ds(n * (L * F), L * F)].rearrange("p (l f) -> p l f", f=F)
                                                  ).then_inc(s_ex, 1)
                            nc.vector.tensor_copy(stage[0:NB, q, :, C + F:C + F + 1],
                                                  extra["dinv"][0:NB, bass.ds(n * L, L)].unsqueeze(2)).then_inc(s_ex, 1)


def edge_phase(nc, sh, layer, io, dr, cst, table, finish, hist=None):
    G, NB = sh.g, sh.nb
    C = table.shape[1]
    M = F + 1 if layer == 0 else F
    tag = f"_L{layer}"
    with nc.cleanup_on_exit(), ExitStack() as ctx:
        def sb(name, shape, dt=FP):
            return ctx.enter_context(nc.sbuf_tensor(name + tag, shape, dt))

        def pb(name):
            return ctx.enter_context(nc.psum_tensor(name + tag, [P, 512], FP))

        def sem(name):
            return nc.alloc_semaphore(f"{name}{tag}")

        def two(name):
            return [sem(f"{name}{s}") for s in range(2)]
        pay = sb("pay", [P, 2, HT, PW])
        payi = pay[:, :, :, :].bitcast(I32)
        rows = sb("rows", [P, HQ, CT, C])
        msg = sb("msg", [P, 2, CT, M])
        hot = sb("hot", [P, 2, CT, P])
        stg = sb("stg", [F + 1, 2, CT * P])
        part = sb("tile_sums", [P, M * P])
        who = sb("owner", [P, NB])
        own = cst["own_src"]
        ps = [pb(f"ps{s}") for s in range(2)]
        bank = [pb(f"bank{k}") for k in range(-(-M * P // 512))]
        s_pl, s_who, s_added, s_fin, s_fch, s_aux = (
            sem(n) for n in ("sums_loaded", "owners", "sums_added", "final", "final_chain", "final_aux"))
        s_pay, s_hot, s_msg, s_taken, s_sc, s_ev, s_st = (
            two(n) for n in ("payload", "onehot", "message", "rows_used", "scattered", "evacuated", "stored"))
        s_gat = [sem(f"gathered{k}") for k in range(HQ)]
        s_rfree = sem("rows_free")
        s_ch = sem("chain")
        s_one = sem("ones")
        s_basis_ch = sem("basis_chain")
        if layer == 0:
            hat = sb("hat", [P, HT, 2, 4])
            basis = sb("basis", [P, 2, HT, F])
            cen = sb("centers", [P, 4])
            prod = sb("prod", [P, CT, 256])
            hlo = sb("hlo", [P, 2, CT, P], BF)
            hhi = sb("hhi", [P, 2, CT, NB], BF)
            zb = sb("zeros_bf", [P, P], BF)
            ps_h = pb("ps_hist")
            s_hlo, s_hhi = two("hist_onehot_low"), two("hist_onehot_block")
            s_away = sem("block_distance")
            s_hd = two("hist_done")
            s_hf = sem("hist_final")
        if layer in (2, 3):
            prod = sb("prod", [P, CT, 128])
            pre = sb("pre", [P, 2, CT, F])
            s_pre = two("presilu")
        s_begun, s_turns, s_asked = sem("begun"), sem("owners_begun"), sem("sums_asked")

        def half(i, hf):
            return dr["S"][bass.ds(i * (GT * P), GT * P), :].rearrange("(p t) w -> p t w", t=GT)[:, hf * HT:(hf + 1) * HT, :]

        with nc.Block() as block:
            @block.scalar
            def _(act):
                for hf in range(2):
                    act.dma_start(pay[:, hf, :, :], half(0, hf)).then_inc(s_pay[hf], 16)
                start_at_one(act, *s_ev)
                if layer == 3:
                    start_at_one(act, *s_msg)
                with act.Fori(0, G) as i:
                    for q in range(QN):
                        s, m = q % 2, q // 2
                        if layer == 0:
                            hf, t0 = q // HQ, (q % HQ) * CT
                            if q % HQ == 0:
                                act.wait_ge(s_pay[hf], i * 16 + 16)
                            act.wait_ge(s_hd[s], i * HQ + m + ONE)
                            for k in range(CT):
                                last = act.activation(hhi[:, s, k, :], cst["iota"][:, 0:NB], ACT.Abs,
                                                      bias=pay[:, hf, t0 + k, W_DHI:W_DHI + 1], scale=-1.0)
                            last.then_inc(s_away, 1)
                            act.wait_ge(s_away, i * QN + (q + 1))
                            act.activation(hhi[:, s, :, :], hhi[:, s, :, :], ACT.Relu, bias=1.0,
                                           scale=-1.0).then_inc(s_hhi[s], 1)
                        if layer == 3:
                            act.wait_ge(s_pre[s], i * HQ + (m + 1) + ONE)
                            act.wait_ge(s_sc[s], i * HQ + m + ONE)
                            act.activation(msg[:, s, :, :], pre[:, s, :, :], ACT.Silu,
                                           scale=float(1.0 / (F * 8) ** 0.5)).then_inc(s_msg[s], 1)
                        act.wait_ge(s_sc[s], i * HQ + (m + 1) + ONE)
                        act.wait_ge(s_st[s], (i * HQ + m) * 16 + ONE)
                        act.activation(stg[0:M, s, :], ps[s][0:M, :], ACT.Copy).then_inc(s_ev[s], 1)
                        if q in (HQ, QN - 1):
                            hf = 0 if q == HQ else 1
                            lq = (HQ if hf == 0 else QN) - 1
                            if layer == 0:
                                act.wait_ge(s_hlo[lq % 2], i * HQ + (lq // 2 + 1))
                                act.wait_ge(s_hhi[lq % 2], i * HQ + (lq // 2 + 1))
                            act.dma_start(pay[:, hf, :, :], half(i + 1, hf)).then_inc(s_pay[hf], 16)
                for hf in range(2):
                    act.wait_ge(s_pay[hf], 16 * (G + 1))
                if finish.root is not None:
                    finish.root(act, s_aux)

            @block.gpsimd
            def _(gp):
                def gather(i, q):
                    if q == 0 or q == HQ:
                        gp.wait_ge(s_pay[q // HQ], i * 16 + 16)
                    gp.wait_ge(s_rfree, i * QN + (q + 1))
                    gp.sem_inc(s_begun, 1)
                    hf, t0 = q // HQ, (q % HQ) * CT
                    for k in range(CT):
                        gp.indirect_dma_start(
                            out=rows[:, q % HQ, k, :], out_offset=None, in_=table,
                            in_offset=bass.IndirectOffsetOnAxis(ap=payi[:, hf, t0 + k, W_DST:W_DST + 1], axis=0)
                        ).then_inc(s_gat[q % HQ], 16)

                if layer == 0:
                    gp.memset(msg[:, :, :, F:F + 1], 1.0).then_inc(s_one, 1)
                    for c in range(4):
                        gp.memset(cen[:, c:c + 1], -1.0 + c * 2.0 / 3.0)
                    gp.memset(zb[:, :], 0.0).then_inc(s_one, 1)
                with gp.Fori(0, G) as i:
                    for q in range(QN):
                        gather(i, q)
                for k in range(HQ):
                    gp.wait_ge(s_gat[k], 16 * CT * 2 * G)

            @block.sync
            def _(sp):
                start_at_one(sp, *s_st)
                with sp.Fori(0, G) as i:
                    for s in range(2):
                        sp.wait_ge(s_st[s], i * (16 * HQ) + ONE)
                    sp.sem_inc(s_asked, 1)
                    sp.wait_ge(s_added, i + ONE)
                    sp.sem_inc(s_asked, 1)
                    sp.dma_start(part[0:GT, :], dr["P"][bass.ds(i * GT, GT), 0:M * P]).then_inc(s_pl, 16)
                    for q in range(QN):
                        s, m = q % 2, q // 2
                        sp.wait_ge(s_ev[s], i * HQ + (m + 1) + ONE)
                        sums = dr["P"][bass.ds(i * GT + (GT + q * CT), CT), 0:M * P].rearrange("t (f l) -> f t l", l=P)
                        sp.dma_start(sums, stg[0:M, s, :].rearrange("f (t l) -> f t l", l=P)).then_inc(s_st[s], 16)
                for s in range(2):
                    sp.wait_ge(s_st[s], 16 * HQ * G + ONE)
                sp.wait_ge(s_added, G + ONE)
                sp.dma_start(part[0:GT, :], dr["P"][G * GT:(G + 1) * GT, 0:M * P]).then_inc(s_pl, 16)

            @block.tensor
            def _(pe):
                start_at_one(pe, s_added, *s_sc, *(s_hd if layer == 0 else []))
                zero = cst["zero"]
                for k in range(len(bank)):
                    nc.tensor.matmul(bank[k][0:NB, :], zero[0:GT, 0:NB], zero[0:GT, :], start=True, stop=False)

                def add_sums(k):
                    n = min(512, M * P - 512 * k)
                    return nc.tensor.matmul(bank[k][0:NB, 0:n], who[0:GT, :], part[0:GT, 512 * k:512 * k + n],
                                            start=False, stop=False)

                if layer == 0:
                    pe.wait_ge(s_one, 2)
                    nc.tensor.matmul(ps_h[0:NB, 0:P], zb[:, 0:NB], zb[:, :], start=True, stop=False)
                with pe.Fori(0, G) as i:
                    for q in range(QN):
                        s, m = q % 2, q // 2
                        pe.wait_ge(s_hot[s], i * HQ + (m + 1))
                        pe.wait_ge(s_msg[s], i * HQ + (m + 1) + ONE)
                        pe.wait_ge(s_ev[s], i * HQ + m + ONE)
                        for k in range(CT):
                            last = nc.tensor.matmul(ps[s][0:M, k * P:(k + 1) * P], msg[:, s, k, :], hot[:, s, k, :],
                                                    start=True, stop=True)
                        last.then_inc(s_sc[s], 1)
                        if q == ADD_AT:
                            pe.wait_ge(s_pl, i * 16 + 16)
                            pe.wait_ge(s_who, i + 1)
                        if ADD_AT <= q < ADD_AT + len(bank):
                            added = add_sums(q - ADD_AT)
                            if q == ADD_AT + len(bank) - 1:
                                added.then_inc(s_added, 1)
                        if layer == 0:
                            pe.wait_ge(s_hlo[s], i * HQ + (m + 1))
                            pe.wait_ge(s_hhi[s], i * HQ + (m + 1))
                            for k in range(CT):
                                last = nc.tensor.matmul(ps_h[0:NB, 0:P], hhi[:, s, k, :], hlo[:, s, k, :],
                                                        start=False, stop=False)
                            last.then_inc(s_hd[s], 1)
                if layer == 0:
                    nc.tensor.matmul(ps_h[0:NB, 0:P], zb[:, 0:NB], zb[:, :], start=False, stop=True).then_inc(s_hf, 1)
                pe.wait_ge(s_pl, (G + 1) * 16)
                pe.wait_ge(s_who, G + 1)
                for k in range(len(bank)):
                    add_sums(k)
                for k in range(len(bank)):
                    last = nc.tensor.matmul(bank[k][0:NB, :], zero[0:GT, 0:NB], zero[0:GT, :], start=False, stop=True)
                last.then_inc(s_fin, 1)

            @block.vector
            def _(dve):
                dve.sem_inc(s_rfree, HQ)
                start_at_one(dve, *(s_taken + s_msg if layer == 0 else s_msg if layer == 2 else s_pre))
                if layer == 0:
                    dve.wait_ge(s_one, 2)
                per_chunk = {0: 1, 2: 2, 3: 1}[layer]
                iota = cst["iota"]
                with dve.Fori(0, G) as i:
                    step = counter(dve, s_ch, i * (QN * per_chunk))
                    bstep = counter(dve, s_basis_ch, i * 10)
                    dve.wait_ge(s_added, i + ONE)
                    dve.sem_inc(s_turns, 1)
                    nc.vector.tensor_copy(who[0:GT, :], own[0:GT, bass.ds(i * NB, NB)]).then_inc(s_who, 1)
                    for q in range(QN):
                        s, m = q % 2, q // 2
                        hf, t0 = q // HQ, (q % HQ) * CT
                        turn = i * HQ + m
                        if q % HQ == 0:
                            dve.wait_ge(s_pay[hf], i * 16 + 16)
                            if layer == 0:
                                ph = pay[:, hf, :, W_A2:W_A2 + 2]
                                sh4 = [P, HT, 2, 4]
                                bstep(nc.vector.tensor_tensor(hat[:, :, :, :], bc(ph, 3, sh4),
                                                              cen[:, :].unsqueeze(1).unsqueeze(1).to_broadcast(sh4), ALU.subtract))
                                flat = hat[:, :, :, :].rearrange("p t a u -> p (t a u)")
                                bstep(nc.vector.scalar_tensor_tensor(out=flat, in0=flat, scalar=-1.0, in1=flat,
                                                                     op0=ALU.mult, op1=ALU.max))
                                bstep(nc.vector.tensor_scalar(flat, flat, -1.5, 1.0, ALU.mult, ALU.add))
                                bstep(nc.vector.tensor_scalar(hat[:, :, :, :], hat[:, :, :, :], 0.0, None, ALU.max))
                                bstep(nc.vector.tensor_tensor(
                                    basis[:, hf, :, :].rearrange("p t (u v) -> p t u v", v=4),
                                    bc(hat[:, :, 0, :], 3, [P, HT, 4, 4]), bc(hat[:, :, 1, :], 2, [P, HT, 4, 4]), ALU.mult))
                        dve.wait_ge(s_sc[s], turn + ONE)
                        here = pay[:, hf, t0:t0 + CT, :]
                        nc.vector.tensor_tensor(hot[:, s, :, :], bc(iota[:, :], 1, [P, CT, P]),
                                                here[:, :, W_SLO:W_SLO + 1].to_broadcast([P, CT, P]),
                                                ALU.is_equal).then_inc(s_hot[s], 1)
                        if layer == 0:
                            dve.wait_ge(s_hd[s], turn + ONE)
                            nc.vector.tensor_tensor(hlo[:, s, :, :], bc(iota[:, :], 1, [P, CT, P]),
                                                    here[:, :, W_DLO:W_DLO + 1].to_broadcast([P, CT, P]),
                                                    ALU.is_equal).then_inc(s_hlo[s], 1)
                        dve.wait_ge(s_gat[q % HQ], (i * 2 + (q // HQ + 1)) * (16 * CT))
                        got = rows[:, q % HQ, :, :]
                        if layer == 0:
                            ba = basis[:, hf, t0:t0 + CT, :]
                            ins = nc.vector.tensor_tensor(
                                prod[:, :, :].rearrange("p t (k o) -> p t k o", o=F),
                                got.rearrange("p t (k o) -> p t k o", o=F), bc(ba, 3, [P, CT, F, F]), ALU.mult)
                            ins.then_inc(s_taken[s], 1)
                            dve.wait_ge(s_taken[s], turn + 1 + ONE)
                            dve.sem_inc(s_rfree, 1)
                            nc.vector.tensor_reduce(msg[:, s, :, 0:F], prod[:, :, :].rearrange("p t (k o) -> p t o k", o=F),
                                                    AX.X, ALU.add).then_inc(s_msg[s], 1)
                            dve.wait_ge(s_msg[s], turn + 1 + ONE)
                        else:
                            a8 = here[:, :, W_A8:W_A8 + 8]
                            step(nc.vector.tensor_tensor(
                                prod[:, :, :].rearrange("p t (k o) -> p t k o", o=F),
                                got[:, :, 0:128].rearrange("p t (k o) -> p t k o", o=F), bc(a8, 3, [P, CT, 8, F]), ALU.mult))
                            red = prod[:, :, :].rearrange("p t (k o) -> p t o k", o=F)
                            if layer == 2:
                                step(nc.vector.tensor_reduce(pre[:, s, :, :], red, AX.X, ALU.add))
                                nc.vector.tensor_tensor(msg[:, s, :, :], pre[:, s, :, :], got[:, :, 128:144],
                                                        ALU.add).then_inc(s_msg[s], 1)
                                dve.wait_ge(s_msg[s], turn + 1 + ONE)
                                dve.sem_inc(s_rfree, 1)
                            else:
                                dve.sem_inc(s_rfree, 1)
                                dve.wait_ge(s_msg[s], turn + ONE)
                                nc.vector.tensor_reduce(pre[:, s, :, :], red, AX.X, ALU.add).then_inc(s_pre[s], 1)
                                dve.wait_ge(s_pre[s], turn + 1 + ONE)
                    if layer != 0:
                        assert step.count[0] == QN * per_chunk, step.count
                fstep = counter(dve, s_fch)
                dve.wait_ge(s_added, G + ONE)
                nc.vector.tensor_copy(who[0:GT, :], own[0:GT, G * NB:(G + 1) * NB]).then_inc(s_who, 1)
                if layer == 0:
                    dve.wait_ge(s_hf, 1)
                    fstep(nc.vector.tensor_copy(hist[0:NB, :], ps_h[0:NB, 0:P]))
                dve.wait_ge(s_fin, 1)
                finish(dve, bank, fstep, s_aux)


def sheaf_phase(nc, sh, io, dr, cst, table, agg):
    G, NB = sh.g, sh.nb
    C = table.shape[1]
    CU = 9 * F + 1
    with nc.cleanup_on_exit(), ExitStack() as ctx:
        def sb(name, shape, dt=FP):
            return ctx.enter_context(nc.sbuf_tensor(name + "_L1", shape, dt))

        def pb(name, banks=1):
            return ctx.enter_context(nc.psum_tensor(name + "_L1", [P, 512 * banks], FP))

        def sem(name):
            return nc.alloc_semaphore(f"{name}_L1")

        def two(name):
            return [sem(f"{name}{s}") for s in range(2)]
        tbl = sb("table", [P, NB * C])
        cols = sb("tile_cols", [1, sh.t + 2 * CT], I32)
        pay = sb("pay", [P, 2, HT, PW])
        payi = pay[:, :, :, :].bitcast(I32)
        rows = sb("rows", [P, 2, CT, C])
        hot = sb("hot", [P, HQ, CT, P])
        hotT = sb("hotT", [P, CT * P])
        hid = sb("hid", [P, CT, P])
        hidT = sb("hidT", [P, CT * P])
        w2 = sb("w2", [P, 2 * F])
        b2 = sb("b2", [P, 2, F])
        v = sb("v", [P, CT, 2, F])
        tv = sb("tv", [P, CT, 2, F])
        cur = sb("cur", [P, 2, CT, 2, F])
        sc = sb("sc", [P, 4, CT * 2])
        msg = sb("msg", [P, 2, CT, F])
        dst = sb("dmsg", [P, 2, CT, DW])
        stg = sb("stg", [F, 2, CT * P])
        part = sb("tile_sums", [P, F * P])
        who = sb("owner", [P, NB])
        own = cst["own_src"]
        ps_q = pb("ps_quarter")
        s_pl, s_who, s_quarter, s_added = (sem(n) for n in ("sums_loaded", "owners", "quarter", "quarter_added"))
        s_turns, s_asked, s_agg = sem("owners_begun"), sem("sums_asked"), sem("agg_zero")
        ps = [pb(f"ps{s}") for s in range(2)]
        ps_o, ps_t, ps_v = pb("ps_o"), pb("ps_t"), pb("ps_v")
        ps_g = pb("ps_g", 2)
        s_pay, s_gat, s_hot, s_msg, s_taken, s_sc, s_ev, s_st, s_dm, s_dsent, s_dfree = (
            two(n) for n in ("payload", "gathered", "onehot", "message", "rows_used", "scattered", "evacuated",
                             "stored", "dst_message", "dst_sent", "dst_free"))
        s_w2, s_w2z, s_dz, s_tbl, s_colz = sem("w2"), sem("w2_zero"), sem("dmsg_zero"), sem("table"), sem("cols_zero")
        s_hotT, s_hotTc, s_src, s_srcread, s_hid, s_hidT, s_hidTc, s_v, s_vread = (
            sem(n) for n in ("hotT", "hotT_copied", "src_rows", "src_rows_read", "hidden", "hiddenT",
                             "hiddenT_copied", "vectors", "vectors_read"))
        s_ch, s_own, s_cur = sem("chain"), sem("own_features"), sem("sent_features")
        s_begun = sem("begun")
        per_chunk = 13

        def half(i, hf):
            return dr["S"][bass.ds(i * (GT * P), GT * P), :].rearrange("(p t) w -> p t w", t=GT)[:, hf * HT:(hf + 1) * HT, :]

        def ahead(i, q, by):
            return (i, q + by) if q + by < QN else (i + 1, q + by - QN)

        with nc.Block() as block:
            @block.scalar
            def _(act):
                act.dma_start(pay[:, 0, :, :], half(0, 0)).then_inc(s_pay[0], 16)
                start_at_one(act, *s_ev, s_hotTc, s_hidTc)

                def copy_hot(n):
                    act.wait_ge(s_src, n + ONE)
                    act.wait_ge(s_hotT, n + 1)
                    act.activation(hotT[:, :], ps_o[:, :], ACT.Copy).then_inc(s_hotTc, 1)

                def relu_hidden(n):
                    act.wait_ge(s_hidT, n + 1)
                    act.activation(hidT[:, :], ps_t[:, :], ACT.Relu).then_inc(s_hidTc, 1)

                copy_hot(0)
                relu_hidden(0)
                copy_hot(1)
                with act.Fori(0, G) as i:
                    for q in range(QN):
                        s, m = q % 2, q // 2
                        n = i * QN + q
                        relu_hidden(n + 1)
                        copy_hot(n + 2)
                        act.wait_ge(s_sc[s], i * HQ + (m + 1) + ONE)
                        act.wait_ge(s_st[s], (i * HQ + m) * 16 + ONE)
                        act.activation(stg[:, s, :], ps[s][0:F, :], ACT.Copy).then_inc(s_ev[s], 1)
                        if q == 1:
                            act.wait_ge(s_dfree[1], i * HQ + ONE)
                            act.dma_start(pay[:, 1, :, :], half(i, 1)).then_inc(s_pay[1], 16)
                        if q == HQ + 1:
                            act.wait_ge(s_dfree[0], i * HQ + (HQ // 2 + 1) + ONE)
                            act.dma_start(pay[:, 0, :, :], half(i + 1, 0)).then_inc(s_pay[0], 16)
                act.wait_ge(s_pay[0], 16 * (G + 1))
                act.wait_ge(s_pay[1], 16 * G)

            @block.gpsimd
            def _(gp):
                def gather(i, q):
                    s, m = q % 2, q // 2
                    if q == 0 or q == HQ:
                        gp.wait_ge(s_pay[q // HQ], i * 16 + 16)
                    gp.wait_ge(s_taken[s], i * HQ + m + ONE)
                    gp.sem_inc(s_begun, 1)
                    hf, t0 = q // HQ, (q % HQ) * CT
                    for k in range(CT):
                        gp.indirect_dma_start(
                            out=rows[:, s, k, :], out_offset=None, in_=table,
                            in_offset=bass.IndirectOffsetOnAxis(ap=payi[:, hf, t0 + k, W_DST:W_DST + 1], axis=0)
                        ).then_inc(s_gat[s], 16)

                gp.memset(cols[:, :], 0).then_inc(s_colz, 1)
                start_at_one(gp, *s_dfree)
                gp.memset(dst[:, :, :, :], 0.0).then_inc(s_dz, 1)
                gather(0, 0)
                gather(0, 1)
                gather(0, 2)
                with gp.Fori(0, G) as i:
                    for q in range(QN):
                        gather(*ahead(i, q, 3))
                        s, m = q % 2, q // 2
                        hf, t0 = q // HQ, (q % HQ) * CT
                        gp.wait_ge(s_dm[s], i * HQ + (m + 1))
                        gp.sem_inc(s_begun, 1)
                        for k in range(CT):
                            gp.indirect_dma_start(
                                out=dr["D"], out_offset=bass.IndirectOffsetOnAxis(
                                    ap=payi[:, hf, t0 + k, W_DROW:W_DROW + 1], axis=0),
                                in_=dst[:, s, k, :], in_offset=None, bounds_check=sh.t * P - 1,
                                oob_is_err=False).then_inc(s_dsent[s], 16)
                        for d in ([q - 1] if q else []) + ([q] if q == QN - 1 else []):
                            gp.wait_ge(s_dsent[d % 2], (i * HQ + (d // 2 + 1)) * (16 * CT))
                            gp.sem_inc(s_dfree[d % 2], 1)
                for s in range(2):
                    gp.wait_ge(s_gat[s], 16 * CT * (HQ * G + 2 - s))

            @block.sync
            def _(sp):
                sp.dma_start(tbl[:, :].rearrange("p (b c) -> p b c", c=C),
                             table.rearrange("(b l) c -> l b c", l=P)).then_inc(s_tbl, 16)
                sp.wait_ge(s_colz, 1)
                sp.dma_start(cols[:, 0:sh.t], dr["cols"]).then_inc(s_tbl, 16)
                sp.wait_ge(s_w2z, 1)
                for k in range(2):
                    sp.dma_start(w2[64 * k:64 * k + 64, F * k:F * k + F], io["w2t"]).then_inc(s_w2, 16)
                    sp.dma_start(b2[:, k, :], io["b2"].partition_broadcast(P)).then_inc(s_w2, 16)
                start_at_one(sp, *s_st)
                with sp.Fori(0, G) as i:
                    for s in range(2):
                        sp.wait_ge(s_st[s], i * (16 * HQ) + ONE)
                    sp.sem_inc(s_asked, 1)
                    sp.wait_ge(s_added, i * 4 + ONE)
                    sp.sem_inc(s_asked, 1)
                    sp.dma_start(part[0:GT, :], dr["P"][bass.ds(i * GT, GT), 0:F * P]).then_inc(s_pl, 16)
                    for q in range(QN):
                        s, m = q % 2, q // 2
                        sp.wait_ge(s_ev[s], i * HQ + (m + 1) + ONE)
                        sums = dr["P"][bass.ds(i * GT + (GT + q * CT), CT), 0:F * P].rearrange("t (f l) -> f t l", l=P)
                        sp.dma_start(sums, stg[:, s, :].rearrange("f (t l) -> f t l", l=P)).then_inc(s_st[s], 16)
                for s in range(2):
                    sp.wait_ge(s_st[s], 16 * HQ * G + ONE)
                sp.wait_ge(s_added, G * 4 + ONE)
                sp.dma_start(part[0:GT, :], dr["P"][G * GT:(G + 1) * GT, 0:F * P]).then_inc(s_pl, 16)

            @block.tensor
            def _(pe):
                start_at_one(pe, *s_sc, s_src)
                pe.wait_ge(s_w2, 64)
                pe.wait_ge(s_tbl, 32)
                regs = [pe.alloc_register(f"tile_col{k}") for k in range(CT)]

                def turn_one_hots(i, q):
                    s, m = q % 2, q // 2
                    n = i * QN + q
                    pe.load(regs, cols[0:1, bass.ds(n * CT, CT)])
                    at = [pe.snap(r, min_val=0, max_val=(NB - 1) * C) for r in regs]
                    pe.wait_ge(s_hot[s], i * HQ + (m + 1))
                    pe.wait_ge(s_hotTc, n + ONE)
                    for k in range(CT):
                        last = nc.tensor.transpose(ps_o[:, k * P:(k + 1) * P], hot[:, q % HQ, k, :], cst["ident"][:, :])
                    last.then_inc(s_hotT, 1)
                    return at

                def src_rows(i, q, at):
                    n = i * QN + q
                    pe.wait_ge(s_hotTc, n + 1 + ONE)
                    pe.wait_ge(s_srcread, n + ONE)
                    for k in range(CT):
                        to = (k // 2) * 512 + (k % 2) * CU
                        last = nc.tensor.matmul(ps_g[:, to:to + CU], hotT[:, k * P:(k + 1) * P],
                                                tbl[:, bass.ds(at[k], CU)], start=True, stop=True)
                    last.then_inc(s_src, 1)

                def vectors(i, q):
                    n = i * QN + q
                    pe.wait_ge(s_hid, n + 1)
                    pe.wait_ge(s_hidTc, n + ONE)
                    for k in range(CT):
                        last = nc.tensor.transpose(ps_t[:, k * P:(k + 1) * P], hid[:, k, :], cst["ident"][:, :])
                    last.then_inc(s_hidT, 1)
                    at = turn_one_hots(*ahead(i, q, 1))
                    pe.wait_ge(s_hidTc, n + 1 + ONE)
                    pe.wait_ge(s_vread, n + ONE)
                    for k in range(CT):
                        last = nc.tensor.matmul(ps_v[:, k * 2 * F:(k + 1) * 2 * F], hidT[:, k * P:(k + 1) * P],
                                                w2[:, :], start=True, stop=True)
                    last.then_inc(s_v, 1)
                    src_rows(*ahead(i, q, 1), at)

                def quarter(k):
                    return nc.tensor.matmul(ps_q[0:NB, :], who[0:GT, :], part[0:GT, 512 * k:512 * k + 512],
                                            start=True, stop=True)

                src_rows(0, 0, turn_one_hots(0, 0))
                vectors(0, 0)
                with pe.Fori(0, G) as i:
                    for q in range(QN):
                        s, m = q % 2, q // 2
                        vectors(*ahead(i, q, 1))
                        pe.wait_ge(s_msg[s], i * HQ + (m + 1) + ONE)
                        pe.wait_ge(s_ev[s], i * HQ + m + ONE)
                        for k in range(CT):
                            last = nc.tensor.matmul(ps[s][0:F, k * P:(k + 1) * P], msg[:, s, k, :], hot[:, q % HQ, k, :],
                                                    start=True, stop=True)
                        last.then_inc(s_sc[s], 1)
                        if q == ADD_AT:
                            pe.wait_ge(s_pl, i * 16 + 16)
                            pe.wait_ge(s_who, i + 1)
                        k = (q - ADD_AT) // 2
                        if (q - ADD_AT) % 2 == 0 and 0 <= k < 4:
                            pe.wait_ge(s_added, i * 4 + k + ONE)
                            quarter(k).then_inc(s_quarter, 1)
                pe.wait_ge(s_pl, (G + 1) * 16)
                pe.wait_ge(s_who, G + 1)
                for k in range(4):
                    pe.wait_ge(s_added, G * 4 + k + ONE)
                    quarter(k).then_inc(s_quarter, 1)

            @block.vector
            def _(dve):
                start_at_one(dve, *s_taken, *s_msg, s_vread, s_srcread, s_added)
                nc.vector.memset(agg[:, :], 0.0).then_inc(s_agg, 1)
                dve.wait_ge(s_agg, 1)
                nc.vector.memset(w2[:, :], 0.0).then_inc(s_w2z, 1)
                dve.wait_ge(s_dz, 1)
                dve.wait_ge(s_w2, 64)
                iota = cst["iota"]
                sh4 = [P, CT, 2, F]

                def add_quarter(k):
                    nc.vector.tensor_tensor(four(agg, NB, k), four(agg, NB, k), bank_view([ps_q], NB, 0),
                                            ALU.add).then_inc(s_added, 1)

                def one_hots(i, q):
                    s, m = q % 2, q // 2
                    hf, t0 = q // HQ, (q % HQ) * CT
                    if q % HQ == 0:
                        dve.wait_ge(s_pay[hf], i * 16 + 16)
                    nc.vector.tensor_tensor(hot[:, q % HQ, :, :], bc(iota[:, :], 1, [P, CT, P]),
                                            pay[:, hf, t0:t0 + CT, W_SLO:W_SLO + 1].to_broadcast([P, CT, P]),
                                            ALU.is_equal).then_inc(s_hot[s], 1)

                def hidden(i, q):
                    s, m = q % 2, q // 2
                    n = i * QN + q
                    dve.wait_ge(s_gat[s], (i * HQ + (m + 1)) * (16 * CT))
                    dve.wait_ge(s_src, n + 1 + ONE)
                    D = rows[:, s, :, :].rearrange("p (a b) c -> p a b c", b=2)
                    S = ps_g[:, :].rearrange("p (a r) -> p a r", a=2)[:, :, 0:2 * CU].rearrange("p a (b c) -> p a b c", c=CU)
                    h4 = hid[:, :, :].rearrange("p (a b) c -> p a b c", b=2)
                    nc.vector.tensor_tensor(h4[:, :, :, 0:64], S[:, :, :, 0:64], D[:, :, :, 64:128], ALU.add)
                    nc.vector.tensor_tensor(h4[:, :, :, 64:128], D[:, :, :, 0:64], S[:, :, :, 64:128],
                                            ALU.add).then_inc(s_hid, 1)
                    c5 = cur[:, s, :, :, :].rearrange("p (a b) e f -> p a b e f", b=2)
                    nc.vector.tensor_tensor(c5[:, :, :, 0, :], D[:, :, :, 128:144],
                                            D[:, :, :, 144:145].to_broadcast([P, 2, 2, F]),
                                            ALU.mult).then_inc(s_taken[s], 1)
                    nc.vector.tensor_copy(c5[:, :, :, 1, :], S[:, :, :, 128:144]).then_inc(s_own, 1)
                    nc.vector.tensor_copy(sc[:, 3, 0:CT].rearrange("p (a b) -> p a b", b=2).unsqueeze(3),
                                          S[:, :, :, 144:145]).then_inc(s_srcread, 1)
                    one_hots(*ahead(i, q, 1))
                    dve.wait_ge(s_own, n + 1)
                    dve.wait_ge(s_srcread, n + 1 + ONE)
                    nc.vector.tensor_tensor(cur[:, s, :, 1, :], cur[:, s, :, 1, :],
                                            bc(sc[:, 3, 0:CT], 2, [P, CT, F]), ALU.mult).then_inc(s_cur, 1)

                one_hots(0, 0)
                hidden(0, 0)
                dve.wait_ge(s_cur, 1)
                with dve.Fori(0, G) as i:
                    step = counter(dve, s_ch, i * (QN * per_chunk))
                    dve.wait_ge(s_added, i * 4 + ONE)
                    dve.sem_inc(s_turns, 1)
                    nc.vector.tensor_copy(who[0:GT, :], own[0:GT, bass.ds(i * NB, NB)]).then_inc(s_who, 1)
                    for q in range(QN):
                        s, m = q % 2, q // 2
                        n = i * QN + q
                        turn = i * HQ + m
                        hf, t0 = q // HQ, (q % HQ) * CT
                        hidden(*ahead(i, q, 1))
                        now = cur[:, s, :, :, :]
                        dve.wait_ge(s_v, n + 1)
                        dve.wait_ge(s_cur, n + 2)
                        nc.vector.tensor_tensor(v[:, :, :, :], ps_v[:, 0:CT * 2 * F].rearrange("p (t a f) -> p t a f", a=2, f=F),
                                                bc(b2[:, :, :], 1, sh4), ALU.add).then_inc(s_vread, 1)
                        dve.wait_ge(s_vread, n + 1 + ONE)
                        step(nc.vector.tensor_tensor(tv[:, :, :, :], v[:, :, :, :], v[:, :, :, :], ALU.mult))
                        w = [sc[:, k, :].rearrange("p (t a) -> p t a", a=2) for k in range(3)]
                        step(nc.vector.tensor_reduce(w[0], tv[:, :, :, :], AX.X, ALU.add))
                        step(nc.vector.tensor_scalar(sc[:, 0, :], sc[:, 0, :], 1e-24, 0.5, ALU.max, ALU.mult))
                        step(nc.vector.reciprocal(sc[:, 1, :], sc[:, 0, :]))
                        dve.wait_ge(s_sc[s], turn + ONE)
                        dve.wait_ge(s_dfree[s], turn + ONE)
                        vv = [v[:, :, a, :] for a in range(2)]
                        cc = [w[1][:, :, a] for a in range(2)]
                        for near in range(2):
                            order = (0, 1) if near else (1, 0)
                            for a in range(2):
                                ins = nc.vector.tensor_tensor(tv[:, :, a, :], vv[order[a]], now[:, :, a, :], ALU.mult)
                            step(ins)
                            step(nc.vector.tensor_reduce(w[2], tv[:, :, :, :], AX.X, ALU.add))
                            for a in range(2):
                                ins = nc.vector.tensor_tensor(w[0][:, :, a], w[2][:, :, a], cc[order[a]], ALU.mult)
                            step(ins)
                            for a in range(2):
                                ins = nc.vector.tensor_tensor(tv[:, :, a, :], vv[order[a]], bc(w[0][:, :, a], 2, [P, CT, F]), ALU.mult)
                            step(ins)
                            if not near:
                                step(nc.vector.tensor_tensor(now, now, tv[:, :, :, :], ALU.subtract))
                        nc.vector.tensor_tensor(msg[:, s, :, :], now[:, :, 0, :], tv[:, :, 0, :], ALU.subtract).then_inc(s_msg[s], 1)
                        nc.vector.tensor_copy(dst[:, s, :, F:F + 1], pay[:, hf, t0:t0 + CT, W_DLO:W_DLO + 1])
                        nc.vector.tensor_tensor(dst[:, s, :, 0:F], now[:, :, 1, :], tv[:, :, 1, :], ALU.subtract).then_inc(s_dm[s], 1)
                        dve.wait_ge(s_dm[s], turn + 1)
                        k = (q - ADD_AT) // 2
                        if (q - ADD_AT) % 2 == 1 and 0 <= k < 4:
                            dve.wait_ge(s_quarter, i * 4 + k + 1)
                            add_quarter(k)
                    assert step.count[0] == QN * per_chunk, step.count
                dve.wait_ge(s_added, G * 4 + ONE)
                nc.vector.tensor_copy(who[0:GT, :], own[0:GT, G * NB:(G + 1) * NB]).then_inc(s_who, 1)
                for k in range(4):
                    dve.wait_ge(s_quarter, G * 4 + k + 1)
                    add_quarter(k)


def dst_phase(nc, sh, dr, cst, finish):
    G, NB = sh.g, sh.nb
    tag = "_D"
    with nc.cleanup_on_exit(), ExitStack() as ctx:
        def sb(name, shape, dt=FP):
            return ctx.enter_context(nc.sbuf_tensor(name + tag, shape, dt))

        def two(name):
            return [nc.alloc_semaphore(f"{name}{s}{tag}") for s in range(2)]
        pay = sb("pay", [P, 2, HT, DW])
        hot = sb("hot", [P, 2, CT, P])
        stg = sb("stg", [F, HQ, CT * P])
        ps = [ctx.enter_context(nc.psum_tensor(f"ps{s}{tag}", [P, 512], FP)) for s in range(2)]
        part = sb("tile_sums", [P, F * P])
        who = sb("owner", [P, NB])
        own, zero = cst["own_dst"], cst["zero"]
        bank = [ctx.enter_context(nc.psum_tensor(f"bank{k}{tag}", [P, 512], FP)) for k in range(4)]
        s_pl, s_who, s_added, s_fin, s_fch, s_turns, s_asked = (
            nc.alloc_semaphore(n + tag) for n in ("sums_loaded", "owners", "sums_added", "final", "final_chain",
                                                  "owners_begun", "sums_asked"))
        s_pay, s_hot, s_sc, s_ev = (two(n) for n in ("payload", "onehot", "scattered", "evacuated"))
        s_st = [nc.alloc_semaphore(f"stored{k}{tag}") for k in range(HQ)]

        def half(i, hf):
            return dr["D"][bass.ds(i * (GT * P), GT * P), :].rearrange("(p t) w -> p t w", t=GT)[:, hf * HT:(hf + 1) * HT, :]

        with nc.Block() as block:
            @block.scalar
            def _(act):
                for hf in range(2):
                    act.dma_start(pay[:, hf, :, :], half(0, hf)).then_inc(s_pay[hf], 16)
                start_at_one(act, *s_ev)
                with act.Fori(0, G) as i:
                    for q in range(QN):
                        s, m = q % 2, q // 2
                        act.wait_ge(s_sc[s], i * HQ + (m + 1) + ONE)
                        act.wait_ge(s_st[q % HQ], (i * 2 + q // HQ) * 16 + ONE)
                        act.activation(stg[:, q % HQ, :], ps[s][0:F, :], ACT.Copy).then_inc(s_ev[s], 1)
                        if q in (HQ - 1, QN - 1):
                            act.dma_start(pay[:, q // HQ, :, :], half(i + 1, q // HQ)).then_inc(s_pay[q // HQ], 16)
                for hf in range(2):
                    act.wait_ge(s_pay[hf], 16 * (G + 1))

            @block.sync
            def _(sp):
                start_at_one(sp, *s_st)
                with sp.Fori(0, G) as i:
                    for s in range(HQ):
                        sp.wait_ge(s_st[s], i * (16 * 2) + ONE)
                    sp.sem_inc(s_asked, 1)
                    sp.wait_ge(s_added, i + ONE)
                    sp.sem_inc(s_asked, 1)
                    sp.dma_start(part[0:GT, :], dr["P"][bass.ds(i * GT, GT), 0:F * P]).then_inc(s_pl, 16)
                    for q in range(QN):
                        s, m = q % 2, q // 2
                        sp.wait_ge(s_ev[s], i * HQ + (m + 1) + ONE)
                        sums = dr["P"][bass.ds(i * GT + (GT + q * CT), CT), 0:F * P].rearrange("t (f l) -> f t l", l=P)
                        sp.dma_start(sums, stg[:, q % HQ, :].rearrange("f (t l) -> f t l", l=P)).then_inc(s_st[q % HQ], 16)
                for k in range(HQ):
                    sp.wait_ge(s_st[k], 16 * 2 * G + ONE)
                sp.wait_ge(s_added, G + ONE)
                sp.dma_start(part[0:GT, :], dr["P"][G * GT:(G + 1) * GT, 0:F * P]).then_inc(s_pl, 16)

            @block.tensor
            def _(pe):
                start_at_one(pe, s_added, *s_sc)
                for k in range(4):
                    nc.tensor.matmul(bank[k][0:NB, :], zero[0:GT, 0:NB], zero[0:GT, :], start=True, stop=False)

                def add_sums(k):
                    return nc.tensor.matmul(bank[k][0:NB, :], who[0:GT, :], part[0:GT, 512 * k:512 * k + 512],
                                            start=False, stop=False)

                with pe.Fori(0, G) as i:
                    for q in range(QN):
                        s, m = q % 2, q // 2
                        hf, t0 = q // HQ, (q % HQ) * CT
                        pe.wait_ge(s_hot[s], i * HQ + (m + 1))
                        pe.wait_ge(s_ev[s], i * HQ + m + ONE)
                        for k in range(CT):
                            last = nc.tensor.matmul(ps[s][0:F, k * P:(k + 1) * P], pay[:, hf, t0 + k, 0:F], hot[:, s, k, :],
                                                    start=True, stop=True)
                        last.then_inc(s_sc[s], 1)
                        if q == HQ:
                            pe.wait_ge(s_pl, i * 16 + 16)
                            pe.wait_ge(s_who, i + 1)
                        if HQ <= q < HQ + 4:
                            added = add_sums(q - HQ)
                            if q == HQ + 3:
                                added.then_inc(s_added, 1)
                pe.wait_ge(s_pl, (G + 1) * 16)
                pe.wait_ge(s_who, G + 1)
                for k in range(4):
                    add_sums(k)
                for k in range(4):
                    last = nc.tensor.matmul(bank[k][0:NB, :], zero[0:GT, 0:NB], zero[0:GT, :], start=False, stop=True)
                last.then_inc(s_fin, 1)

            @block.vector
            def _(dve):
                with dve.Fori(0, G) as i:
                    dve.wait_ge(s_added, i + ONE)
                    dve.sem_inc(s_turns, 1)
                    nc.vector.tensor_copy(who[0:GT, :], own[0:GT, bass.ds(i * NB, NB)]).then_inc(s_who, 1)
                    for q in range(QN):
                        s, m = q % 2, q // 2
                        hf, t0 = q // HQ, (q % HQ) * CT
                        if q % HQ == 0:
                            dve.wait_ge(s_pay[hf], i * 16 + 16)
                        dve.wait_ge(s_sc[s], i * HQ + m + ONE)
                        nc.vector.tensor_tensor(hot[:, s, :, :], bc(cst["iota"][:, :], 1, [P, CT, P]),
                                                pay[:, hf, t0:t0 + CT, F:F + 1].to_broadcast([P, CT, P]),
                                                ALU.is_equal).then_inc(s_hot[s], 1)
                dve.wait_ge(s_added, G + ONE)
                nc.vector.tensor_copy(who[0:GT, :], own[0:GT, G * NB:(G + 1) * NB]).then_inc(s_who, 1)
                dve.wait_ge(s_fin, 1)
                finish(dve, bank, counter(dve, s_fch), None)


def bank_view(bank, NB, k):
    return bank[k][0:NB, :].rearrange("p (f l) -> p l f", l=P)


def four(buf, NB, k):
    return buf[0:NB, :].rearrange("p (l f) -> p l f", f=F)[:, :, 4 * k:4 * k + 4]


def gnn(nc, sh, io, out):
    NB, G = sh.nb, sh.g

    def dram(name, shape):
        return nc.dram_tensor(name, shape, FP, kind="Internal").ap()
    dr = {
        "S": dram("edges_src_order", [(sh.t + GT) * P, PW]),
        "D": dram("messages_dst_order", [(sh.t + GT) * P, DW]),
        "P": dram("tile_sums", [GT + sh.t, (F + 1) * P]),
        "cols": nc.dram_tensor("tile_cols", [1, sh.t], I32, kind="Internal").ap(),
    }
    table = [dram(f"table{l}", [sh.npad, c]) for l, c in enumerate((256, C1, 144, 128))]
    with ExitStack() as ctx:
        def sb(name, shape, dt=FP):
            return ctx.enter_context(nc.sbuf_tensor(name, shape, dt))
        cst = {
            "iota": sb("iota", [P, P]), "ident": sb("ident", [P, P]),
            "own_src": sb("own_src", [P, (G + 1) * NB]), "own_dst": sb("own_dst", [P, (G + 1) * NB]),
            "zero": sb("zero", [P, 512]),
        }
        setup_phase(nc, sh, io, dr, cst)

        x, h, agg = (sb(n, [P, P * F]) for n in ("x", "h", "agg"))
        hist, deg, dinv = (sb(n, [P, P]) for n in ("hist", "deg", "dinv"))
        bias = sb("bias1", [P, P])

        norm_phase(nc, sh, "0", x, h, io=io)
        node_matmul(nc, sh, "_t0", h, [io["w0"]], 256, cst, "table", table[0])
        def finish0(dve, bank, step, s_cp):
            for k in range(4):
                step(nc.vector.tensor_tensor(four(x, NB, k), four(x, NB, k), bank_view(bank, NB, k), ALU.add))
            step(nc.vector.tensor_tensor(deg[0:NB, :], hist[0:NB, :], bank[4][0:NB, 0:P], ALU.add))
            nc.vector.tensor_scalar(deg[0:NB, :], deg[0:NB, :], 1e-5, None, ALU.max).then_inc(s_cp, 1)
            dve.wait_ge(s_cp, 2)
            step(nc.vector.reciprocal(dinv[0:NB, :], deg[0:NB, :]))

        def root0(act, s_cp):
            act.wait_ge(s_cp, 1)
            act.activation(deg[0:NB, :], deg[0:NB, :], ACT.Sqrt).then_inc(s_cp, 1)
        finish0.root = root0
        edge_phase(nc, sh, 0, io, dr, cst, table[0], finish0, hist=hist)

        norm_phase(nc, sh, "1", x, h)
        s_bz, s_bl = nc.alloc_semaphore("bias_zero"), nc.alloc_semaphore("bias_load")
        with nc.Block() as block:
            @block.vector
            def _(dve):
                nc.vector.memset(bias[:, :], 0.0).then_inc(s_bz, 1)

            @block.sync
            def _(sp):
                sp.wait_ge(s_bz, 1)
                sp.dma_start(bias[:, 0:64], io["b1"].partition_broadcast(P)).then_inc(s_bl, 16)
                sp.wait_ge(s_bl, 16)
        node_matmul(nc, sh, "_t1", h, [io["w1a"], io["w1b"]], 128, cst, "table", table[1],
                    extra={"bias": bias, "dinv": dinv})
        sheaf_phase(nc, sh, io, dr, cst, table[1], agg)

        def finish1d(dve, bank, step, s_cp):
            for k in range(4):
                step(nc.vector.tensor_tensor(four(agg, NB, k), four(agg, NB, k), bank_view(bank, NB, k), ALU.add))
            a3 = agg[0:NB, :].rearrange("p (l f) -> p l f", f=F)
            step(nc.vector.tensor_tensor(a3, a3, bc(dinv[0:NB, :], 2, [NB, P, F]), ALU.mult))
            step(nc.vector.tensor_tensor(agg[0:NB, :], agg[0:NB, :], h[0:NB, :], ALU.add))
            step(nc.vector.scalar_tensor_tensor(out=x[0:NB, :], in0=agg[0:NB, :], scalar=0.0, in1=x[0:NB, :],
                                                op0=ALU.max, op1=ALU.add))
        finish1d.root = None
        dst_phase(nc, sh, dr, cst, finish1d)

        norm_phase(nc, sh, "2", x, h)
        node_matmul(nc, sh, "_t2", h, [io["w2k"], io["w2b"]], 144, cst, "table", table[2])

        def finish2(dve, bank, step, s_cp):
            for k in range(4):
                step(nc.vector.tensor_tensor(four(x, NB, k), four(x, NB, k), bank_view(bank, NB, k), ALU.add))
        finish2.root = None
        edge_phase(nc, sh, 2, io, dr, cst, table[2], finish2)

        norm_phase(nc, sh, "3", x, h)
        node_matmul(nc, sh, "_t3", h, [io["w3"]], 128, cst, "table", table[3])

        def finish3(dve, bank, step, s_cp):
            for k in range(4):
                step(nc.vector.tensor_copy(four(agg, NB, k), bank_view(bank, NB, k)))
        finish3.root = None
        edge_phase(nc, sh, 3, io, dr, cst, table[3], finish3)
        u = sb("u", [P, P * F])
        su = sb("silu_u", [P, P * F])
        agg2 = sb("agg2", [P, P * F])
        node_matmul(nc, sh, "_lin", agg, [io["wml"]], F, cst, "copy", agg2, extra=0.25)
        node_matmul(nc, sh, "_upd", h, [io["wupd"]], 256, cst, "upd", u, extra=agg2)
        with nc.Block() as block:
            @block.scalar
            def _(act):
                act.activation(su[0:NB, :], u[0:NB, :], ACT.Silu, scale=1.0 / 16)

            @block.vector
            def _(dve):
                nc.vector.tensor_tensor(x[0:NB, :], x[0:NB, :], h[0:NB, :], ALU.add)
        node_matmul(nc, sh, "_fin", su, [io["wul"]], F, cst, "final", x, extra=0.25)
        s_o = nc.alloc_semaphore("stored_out")
        with nc.Block() as block:
            @block.sync
            def _(sp):
                full = NB - 1
                sp.dma_start(out[0:full * P, :].rearrange("(b l) f -> b (l f)", l=P), x[0:full, :]).then_inc(s_o, 16)
                sp.dma_start(out[full * P:sh.n, :].rearrange("(b l) f -> b (l f)", b=1), x[full:NB, 0:sh.last * F]).then_inc(s_o, 16)
                sp.wait_ge(s_o, 32)


def laid_out(inputs):
    import numpy as np
    c = np.ascontiguousarray
    a = {k: np.asarray(v) for k, v in inputs.items()}
    w1 = a["L1_gnn_W1"]
    return {
        "x": c(a["x"]), "src": c(a["src"]), "dst": c(a["dst"]),
        "edge_attr_2": c(a["edge_attr_2"]), "edge_attr_8": c(a["edge_attr_8"]),
        "w0": c(a["L0_gnn_weight"].reshape(16, 16, 16).transpose(1, 0, 2).reshape(16, 256)),
        "w1a": c(w1[:, 0:16].T), "w1b": c(w1[:, 16:32].T), "b1": c(a["L1_gnn_b1"]),
        "w2t": c(a["L1_gnn_W2"].T), "b2": c(a["L1_gnn_b2"]),
        "w2k": c(a["L2_gnn_kernel"].reshape(8, 16, 16).transpose(2, 0, 1).reshape(16, 128)),
        "w2b": c(a["L2_gnn_bias"].reshape(16, 16).T),
        "w3": c(a["L3_gnn_W_msg_tp"].reshape(16, 128)), "wml": c(a["L3_gnn_W_msg_lin"]),
        "wupd": c(a["L3_gnn_W_upd_tp"].reshape(16, 256)), "wul": c(a["L3_gnn_W_upd_lin"]),
    }


def kernel(**inputs):
    import concourse.bacc as _bacc
    from concourse.bass_utils import run_bass_kernel_spmd as _run

    arrays = laid_out(inputs)
    nc = _bacc.Bacc("TRN2", target_bir_lowering=False, num_devices=1)
    io = {k: nc.dram_tensor(f"in_{k}", v.shape, mybir.dt.from_np(v.dtype), kind="ExternalInput").ap()
          for k, v in arrays.items()}
    n = arrays["x"].shape[0]
    out = nc.dram_tensor("out_nodes", [n, F], FP, kind="ExternalOutput").ap()
    gnn(nc, Shapes(n, arrays["src"].shape[0]), io, out)
    r = _run(nc, [{f"in_{k}": v for k, v in arrays.items()}], core_ids=[0])
    return r.results[0]["out_nodes"]
```
